# Optimizing a Trainium2 kernel written in Bass

```python
import numpy as np
import jax
import jax.numpy as jnp

def _softmax(x, axis=-1):
    return jax.nn.softmax(x, axis=axis)

def _gelu(x):
    return jax.nn.gelu(x, approximate=True)

def _silu(x):
    return jax.nn.silu(x)

def _sigmoid(x):
    return jax.nn.sigmoid(x)

def _layernorm(x, axis=-1, eps=1e-05):
    m = jnp.mean(x, axis=axis, keepdims=True)
    v = jnp.var(x, axis=axis, keepdims=True)
    return (x - m) / jnp.sqrt(v + eps)

def _scatter_add(tgt, idx, src, axis=0):
    return tgt.at[idx].add(src)

def _segment_sum(src, seg, n):
    return jax.ops.segment_sum(src, seg, n)
kernel_name = 'mk_decoder_postln_d2_seqx_r8_ad922f'

def setup_inputs(seed: int=0):
    np.random.seed(seed)
    _w = jnp.asarray

    def _rec_inputs():
        import jax
        import jax.numpy as jnp
        _rk = jax.random.key(seed)
        x = -0.0003929 + 0.9999 * jax.random.normal(jax.random.fold_in(_rk, 1), (32, 128, 128), jnp.float32)
        _lenS = 128 - jax.random.randint(jax.random.fold_in(_rk, 7), (32,), 0, max(1, 128 // 4) + 1, jnp.int32)
        _lenS2 = 128 - jax.random.randint(jax.random.fold_in(_rk, 8), (32,), 0, max(1, 128 // 4) + 1, jnp.int32)
        _ctx_1024P = jax.random.normal(jax.random.fold_in(_rk, 11), (32, 16, 128), jnp.float32)
        _ctx_1024c = jax.random.dirichlet(jax.random.fold_in(_rk, 511), 0.3 * jnp.ones((16,), jnp.float32), (32, 128))
        _ctx_1024t = jnp.einsum('bsk,bkd->bsd', _ctx_1024c, _ctx_1024P)
        _ctx_1024t = _ctx_1024t * jax.lax.rsqrt(jnp.mean(jnp.square(_ctx_1024t)) + 1e-12) * 0.953939
        ctx_1024 = 2.81802e-05 + 1.00001 * (_ctx_1024t + 0.3 * jax.random.normal(jax.random.fold_in(_rk, 611), (32, 128, 128), jnp.float32))
        _validS = jnp.arange(128)[None, :] < _lenS[:, None]
        _validS2 = jnp.arange(128)[None, :] < _lenS2[:, None]
        _causal = jnp.tril(jnp.ones((128, 128), dtype=bool))
        mask_BxS2_bf1 = jnp.ones((32, 128), dtype=bool)
        return (x, ctx_1024, mask_BxS2_bf1)
    x, ctx_1024, mask_BxS2_bf1 = _rec_inputs()

    def _L0_attn_setup():
        import jax, jax.numpy as jnp
        import numpy as np
        D = 128
        H = 16
        DH = D // H
        key = jax.random.key(seed)
        ks = jax.random.split(key, 7)
        s = 0.02
        return {'z': jax.random.normal(ks[0], (8, 128, D), dtype=jnp.float32), 'ln_w': jnp.ones((D,), dtype=jnp.float32), 'ln_b': jnp.zeros((D,), dtype=jnp.float32), 'W_qkv': jax.random.normal(ks[1], (D, 3 * D), dtype=jnp.float32) * s, 'b_qkv': jnp.zeros((3 * D,), dtype=jnp.float32), 'W_proj': jax.random.normal(ks[2], (D, D), dtype=jnp.float32) * s, 'b_proj': jnp.zeros((D,), dtype=jnp.float32)}
    _L0_attn_all = _L0_attn_setup()
    _L0_attn_in = {k: v for k, v in _L0_attn_all.items() if k in ('ln_w', 'ln_b', 'W_qkv', 'b_qkv', 'W_proj', 'b_proj')}
    del _L0_attn_all

    def _L0_xattn_setup():
        import jax, jax.numpy as jnp
        import numpy as np
        D1, D2, D3 = (128, 128, 128)
        key = jax.random.key(seed)
        k1, k2, kw, kb = jax.random.split(key, 4)
        x1 = jax.random.normal(k1, (8, 256, D1), dtype=jnp.float32)
        x2 = jax.random.normal(k2, (8, 256, D2), dtype=jnp.float32)
        bound = 1.0 / np.sqrt(D1 + D2)
        W = jax.random.uniform(kw, (D3, D1 + D2), minval=-bound, maxval=bound, dtype=jnp.float32)
        b = jax.random.uniform(kb, (D3,), minval=-bound, maxval=bound, dtype=jnp.float32)
        return {'x1': x1, 'x2': x2, 'W': W, 'b': b}
    _L0_xattn_all = _L0_xattn_setup()
    _L0_xattn_in = {k: v for k, v in _L0_xattn_all.items() if k in ('W', 'b')}
    del _L0_xattn_all

    def _L0_ffn_setup():
        import jax, jax.numpy as jnp
        import numpy as np
        B, S, D = (1, 256, 128)
        E, K, F = (8, 2, 176)
        NS = 2
        SCALE = 2.5

        def _swiglu_mlp(x, wg, wu, wd):
            return jax.nn.silu(x @ wg) * (x @ wu) @ wd
        key = jax.random.key(seed)
        ks = jax.random.split(key, 8)
        s = 0.02
        return {'hidden_states': jax.random.normal(ks[0], (B, S, D), jnp.float32), 'gate_w': jax.random.normal(ks[1], (E, D), jnp.float32) * s, 'w_gate': jax.random.normal(ks[2], (E, D, F), jnp.float32) * s, 'w_up': jax.random.normal(ks[3], (E, D, F), jnp.float32) * s, 'w_down': jax.random.normal(ks[4], (E, F, D), jnp.float32) * s, 'sw_gate': jax.random.normal(ks[5], (D, F * NS), jnp.float32) * s, 'sw_up': jax.random.normal(ks[6], (D, F * NS), jnp.float32) * s, 'sw_down': jax.random.normal(ks[7], (F * NS, D), jnp.float32) * s}
    _L0_ffn_all = _L0_ffn_setup()
    _L0_ffn_in = {k: v for k, v in _L0_ffn_all.items() if k in ('gate_w', 'w_gate', 'w_up', 'w_down', 'sw_gate', 'sw_up', 'sw_down')}
    del _L0_ffn_all

    def _L1_attn_setup():
        import jax, jax.numpy as jnp
        import numpy as np
        EPS = 1e-05

        def layernorm(x, g, b):
            mu = jnp.mean(x, axis=-1, keepdims=True)
            var = jnp.mean(jnp.square(x - mu), axis=-1, keepdims=True)
            return (x - mu) * jax.lax.rsqrt(var + EPS) * g + b

        def ssm_block(h, Wa, ba, Wb, bb, Wc, bc):
            a = jax.nn.sigmoid(jnp.einsum('bsd,de->bse', h, Wa) + ba)
            b = jnp.tanh(jnp.einsum('bsd,de->bse', h, Wb) + bb)
            c = jax.nn.sigmoid(jnp.einsum('bsd,de->bse', h, Wc) + bc)

            def step(state, abc):
                a_t, b_t, c_t = abc
                state = a_t * state + (1.0 - a_t) * b_t
                return (state, c_t * state)
            B, S, D = h.shape
            init = jnp.zeros((B, D), h.dtype)
            xs = (jnp.swapaxes(a, 0, 1), jnp.swapaxes(b, 0, 1), jnp.swapaxes(c, 0, 1))
            _, ys = jax.lax.scan(step, init, xs)
            return jnp.swapaxes(ys, 0, 1)
        key = jax.random.key(seed)
        ks = jax.random.split(key, 16)
        B, S, D = (4, 256, 128)
        H = 4 * D
        s = 1.0 / np.sqrt(D)
        inp = {'x': jax.random.normal(ks[0], (B, S, D), dtype=jnp.float32), 'g1': jnp.ones((D,), jnp.float32), 'b1': jnp.zeros((D,), jnp.float32), 'Wa': jax.random.uniform(ks[1], (D, D), jnp.float32, -s, s), 'ba': jnp.zeros((D,), jnp.float32), 'Wb': jax.random.uniform(ks[2], (D, D), jnp.float32, -s, s), 'bb': jnp.zeros((D,), jnp.float32), 'Wc': jax.random.uniform(ks[3], (D, D), jnp.float32, -s, s), 'bc': jnp.zeros((D,), jnp.float32), 'g2': jnp.ones((D,), jnp.float32), 'b2': jnp.zeros((D,), jnp.float32), 'W1': jax.random.uniform(ks[4], (D, H), jnp.float32, -s, s), 'bm1': jnp.zeros((H,), jnp.float32), 'W2': jax.random.uniform(ks[5], (H, D), jnp.float32, -1.0 / np.sqrt(H), 1.0 / np.sqrt(H)), 'bm2': jnp.zeros((D,), jnp.float32)}
        return inp
    _L1_attn_all = _L1_attn_setup()
    _L1_attn_in = {k: v for k, v in _L1_attn_all.items() if k in ('g1', 'b1', 'Wa', 'ba', 'Wb', 'bb', 'Wc', 'bc', 'g2', 'b2', 'W1', 'bm1', 'W2', 'bm2')}
    del _L1_attn_all

    def _L1_xattn_setup():
        import jax, jax.numpy as jnp
        import numpy as np
        DIM = 128
        DIM_LATENT = 128
        DIM_HEAD = 64
        HEADS = 16
        INNER = HEADS * DIM_HEAD

        def layernorm(x, g, b, eps=1e-05):
            m = jnp.mean(x, axis=-1, keepdims=True)
            v = jnp.mean((x - m) ** 2, axis=-1, keepdims=True)
            return (x - m) / jnp.sqrt(v + eps) * g + b

        def rmsnorm(x, gamma, eps=1e-08):
            n = jnp.linalg.norm(x, axis=-1, keepdims=True) * x.shape[-1] ** (-0.5)
            return x / jnp.maximum(n, eps) * gamma
        key = jax.random.key(seed)
        ks = jax.random.split(key, 8)
        b, n, m = (4, 512, 64)
        x = jax.random.normal(ks[0], (b, n, DIM), dtype=jnp.float32)
        latents = jax.random.normal(ks[1], (b, m, DIM_LATENT), dtype=jnp.float32)
        mask = jnp.ones((b, n), dtype=bool)
        s = 0.02
        return {'x': x, 'latents': latents, 'mask': mask, 'ln_x_g': jnp.ones((DIM,), jnp.float32), 'ln_x_b': jnp.zeros((DIM,), jnp.float32), 'ln_l_g': jnp.ones((DIM_LATENT,), jnp.float32), 'ln_l_b': jnp.zeros((DIM_LATENT,), jnp.float32), 'qn_g': jnp.ones((DIM_HEAD,), jnp.float32), 'kn_g': jnp.ones((DIM_HEAD,), jnp.float32), 'Wq': jax.random.normal(ks[2], (DIM_LATENT, INNER), jnp.float32) * s, 'Wkv': jax.random.normal(ks[3], (DIM, 2 * INNER), jnp.float32) * s, 'Wout': jax.random.normal(ks[4], (INNER, DIM_LATENT), jnp.float32) * s, 'bout': jnp.zeros((DIM_LATENT,), jnp.float32)}
    _L1_xattn_all = _L1_xattn_setup()
    _L1_xattn_in = {k: v for k, v in _L1_xattn_all.items() if k in ('ln_x_g', 'ln_x_b', 'ln_l_g', 'ln_l_b', 'qn_g', 'kn_g', 'Wq', 'Wkv', 'Wout', 'bout')}
    del _L1_xattn_all

    def _L1_ffn_setup():
        import jax, jax.numpy as jnp
        import numpy as np
        HIDDEN = 128
        INNER = 512

        def _weight_quant(w):
            scale = 1.0 / jnp.clip(jnp.mean(jnp.abs(w)), 1e-05)
            wq = jnp.clip(jnp.round(w * scale), -1.0, 1.0) / scale
            return w + jax.lax.stop_gradient(wq - w)

        def _act_quant(x):
            scale = 127.0 / jnp.clip(jnp.max(jnp.abs(x), axis=-1, keepdims=True), 1e-05)
            xq = jnp.clip(jnp.round(x * scale), -128.0, 127.0) / scale
            return x + jax.lax.stop_gradient(xq - x)

        def _bitlinear(x, w):
            return jnp.einsum('bsi,oi->bso', _act_quant(x), _weight_quant(w))
        key = jax.random.key(seed)
        k0, k1, k2, k3 = jax.random.split(key, 4)
        x = jax.random.normal(k0, (4, 256, HIDDEN), dtype=jnp.float32)
        w_gate = jax.random.normal(k1, (INNER, HIDDEN), dtype=jnp.float32) / np.sqrt(HIDDEN)
        w_up = jax.random.normal(k2, (INNER, HIDDEN), dtype=jnp.float32) / np.sqrt(HIDDEN)
        w_down = jax.random.normal(k3, (HIDDEN, INNER), dtype=jnp.float32) / np.sqrt(INNER)
        return {'x': x, 'w_gate': w_gate, 'w_up': w_up, 'w_down': w_down}
    _L1_ffn_all = _L1_ffn_setup()
    _L1_ffn_in = {k: v for k, v in _L1_ffn_all.items() if k in ('w_gate', 'w_up', 'w_down')}
    del _L1_ffn_all
    return {'x': x, 'ctx_1024': ctx_1024, 'mask_BxS2_bf1': mask_BxS2_bf1, 'L0_attn_ln_w': _L0_attn_in['ln_w'], 'L0_attn_ln_b': _L0_attn_in['ln_b'], 'L0_attn_W_qkv': _L0_attn_in['W_qkv'], 'L0_attn_b_qkv': _L0_attn_in['b_qkv'], 'L0_attn_W_proj': _L0_attn_in['W_proj'], 'L0_attn_b_proj': _L0_attn_in['b_proj'], 'L0_xattn_W': _L0_xattn_in['W'], 'L0_xattn_b': _L0_xattn_in['b'], 'L0_ffn_gate_w': _L0_ffn_in['gate_w'], 'L0_ffn_w_gate': _L0_ffn_in['w_gate'], 'L0_ffn_w_up': _L0_ffn_in['w_up'], 'L0_ffn_w_down': _L0_ffn_in['w_down'], 'L0_ffn_sw_gate': _L0_ffn_in['sw_gate'], 'L0_ffn_sw_up': _L0_ffn_in['sw_up'], 'L0_ffn_sw_down': _L0_ffn_in['sw_down'], 'L1_attn_g1': _L1_attn_in['g1'], 'L1_attn_b1': _L1_attn_in['b1'], 'L1_attn_Wa': _L1_attn_in['Wa'], 'L1_attn_ba': _L1_attn_in['ba'], 'L1_attn_Wb': _L1_attn_in['Wb'], 'L1_attn_bb': _L1_attn_in['bb'], 'L1_attn_Wc': _L1_attn_in['Wc'], 'L1_attn_bc': _L1_attn_in['bc'], 'L1_attn_g2': _L1_attn_in['g2'], 'L1_attn_b2': _L1_attn_in['b2'], 'L1_attn_W1': _L1_attn_in['W1'], 'L1_attn_bm1': _L1_attn_in['bm1'], 'L1_attn_W2': _L1_attn_in['W2'], 'L1_attn_bm2': _L1_attn_in['bm2'], 'L1_xattn_ln_x_g': _L1_xattn_in['ln_x_g'], 'L1_xattn_ln_x_b': _L1_xattn_in['ln_x_b'], 'L1_xattn_ln_l_g': _L1_xattn_in['ln_l_g'], 'L1_xattn_ln_l_b': _L1_xattn_in['ln_l_b'], 'L1_xattn_qn_g': _L1_xattn_in['qn_g'], 'L1_xattn_kn_g': _L1_xattn_in['kn_g'], 'L1_xattn_Wq': _L1_xattn_in['Wq'], 'L1_xattn_Wkv': _L1_xattn_in['Wkv'], 'L1_xattn_Wout': _L1_xattn_in['Wout'], 'L1_xattn_bout': _L1_xattn_in['bout'], 'L1_ffn_w_gate': _L1_ffn_in['w_gate'], 'L1_ffn_w_up': _L1_ffn_in['w_up'], 'L1_ffn_w_down': _L1_ffn_in['w_down']}

def reference(x, ctx_1024, mask_BxS2_bf1, L0_attn_ln_w, L0_attn_ln_b, L0_attn_W_qkv, L0_attn_b_qkv, L0_attn_W_proj, L0_attn_b_proj, L0_xattn_W, L0_xattn_b, L0_ffn_gate_w, L0_ffn_w_gate, L0_ffn_w_up, L0_ffn_w_down, L0_ffn_sw_gate, L0_ffn_sw_up, L0_ffn_sw_down, L1_attn_g1, L1_attn_b1, L1_attn_Wa, L1_attn_ba, L1_attn_Wb, L1_attn_bb, L1_attn_Wc, L1_attn_bc, L1_attn_g2, L1_attn_b2, L1_attn_W1, L1_attn_bm1, L1_attn_W2, L1_attn_bm2, L1_xattn_ln_x_g, L1_xattn_ln_x_b, L1_xattn_ln_l_g, L1_xattn_ln_l_b, L1_xattn_qn_g, L1_xattn_kn_g, L1_xattn_Wq, L1_xattn_Wkv, L1_xattn_Wout, L1_xattn_bout, L1_ffn_w_gate, L1_ffn_w_up, L1_ffn_w_down):
    import jax
    import jax.numpy as jnp

    def _L0_attn_ref(z, ln_w, ln_b, W_qkv, b_qkv, W_proj, b_proj):
        import jax, jax.numpy as jnp
        import numpy as np
        D = 128
        H = 16
        DH = D // H
        b, n, d = z.shape
        mu = jnp.mean(z, axis=-1, keepdims=True)
        var = jnp.var(z, axis=-1, keepdims=True)
        zn = (z - mu) / jnp.sqrt(var + 1e-05) * ln_w + ln_b
        qkv = (zn @ W_qkv + b_qkv).reshape(b, n, 3, H, DH)
        q = qkv[:, :, 0].transpose(0, 2, 1, 3)
        k = qkv[:, :, 1].transpose(0, 2, 1, 3)
        v = qkv[:, :, 2].transpose(0, 2, 1, 3)
        scale = 1.0 / jnp.sqrt(jnp.asarray(DH, dtype=z.dtype))
        scores = jnp.einsum('bhqd,bhkd->bhqk', q, k) * scale
        attn = jax.nn.softmax(scores, axis=-1)
        msa = jnp.einsum('bhqk,bhkd->bhqd', attn, v)
        msa_cat = msa.transpose(0, 2, 1, 3).reshape(b, n, d)
        out = msa_cat @ W_proj + b_proj
        return z + out

    def _L0_xattn_ref(x1, x2, W, b):
        import jax, jax.numpy as jnp
        import numpy as np
        D1, D2, D3 = (128, 128, 128)
        d1 = x1.shape[-1]
        W1 = W[:, :d1]
        W2 = W[:, d1:]
        part1 = jnp.einsum('bld,ed->ble', x1, W1)
        part2 = jnp.einsum('bld,ed->be', x2, W2) / x2.shape[1]
        return part1 + part2[:, None, :] + b

    def _L0_ffn_ref(hidden_states, gate_w, w_gate, w_up, w_down, sw_gate, sw_up, sw_down):
        import jax, jax.numpy as jnp
        import numpy as np
        B, S, D = (1, 256, 128)
        E, K, F = (8, 2, 176)
        NS = 2
        SCALE = 2.5

        def _swiglu_mlp(x, wg, wu, wd):
            return jax.nn.silu(x @ wg) * (x @ wu) @ wd
        identity = hidden_states
        x = hidden_states.reshape(-1, hidden_states.shape[-1])
        T = x.shape[0]
        logits = x.astype(jnp.float32) @ gate_w.astype(jnp.float32).T
        scores = jax.nn.softmax(logits, axis=-1)
        topk_w, topk_i = jax.lax.top_k(scores, K)
        topk_w = topk_w / (topk_w.sum(-1, keepdims=True) + 1e-20) * SCALE
        combine = jnp.zeros((T, E), jnp.float32).at[jnp.arange(T)[:, None], topk_i].set(topk_w)
        g = jax.nn.silu(jnp.einsum('td,edf->etf', x, w_gate)) * jnp.einsum('td,edf->etf', x, w_up)
        expert_out = jnp.einsum('etf,efd->etd', g, w_down)
        y = jnp.einsum('te,etd->td', combine, expert_out).astype(x.dtype)
        y = y.reshape(identity.shape)
        return y + _swiglu_mlp(identity, sw_gate, sw_up, sw_down)

    def _L1_attn_ref(x, g1, b1, Wa, ba, Wb, bb, Wc, bc, g2, b2, W1, bm1, W2, bm2):
        import jax, jax.numpy as jnp
        import numpy as np
        EPS = 1e-05

        def layernorm(x, g, b):
            mu = jnp.mean(x, axis=-1, keepdims=True)
            var = jnp.mean(jnp.square(x - mu), axis=-1, keepdims=True)
            return (x - mu) * jax.lax.rsqrt(var + EPS) * g + b

        def ssm_block(h, Wa, ba, Wb, bb, Wc, bc):
            a = jax.nn.sigmoid(jnp.einsum('bsd,de->bse', h, Wa) + ba)
            b = jnp.tanh(jnp.einsum('bsd,de->bse', h, Wb) + bb)
            c = jax.nn.sigmoid(jnp.einsum('bsd,de->bse', h, Wc) + bc)

            def step(state, abc):
                a_t, b_t, c_t = abc
                state = a_t * state + (1.0 - a_t) * b_t
                return (state, c_t * state)
            B, S, D = h.shape
            init = jnp.zeros((B, D), h.dtype)
            xs = (jnp.swapaxes(a, 0, 1), jnp.swapaxes(b, 0, 1), jnp.swapaxes(c, 0, 1))
            _, ys = jax.lax.scan(step, init, xs)
            return jnp.swapaxes(ys, 0, 1)
        h = layernorm(x, g1, b1)
        x = x + ssm_block(h, Wa, ba, Wb, bb, Wc, bc)
        h2 = layernorm(x, g2, b2)
        mlp = jax.nn.gelu(jnp.einsum('bsd,dh->bsh', h2, W1) + bm1, approximate=False)
        x = x + jnp.einsum('bsh,hd->bsd', mlp, W2) + bm2
        return x

    def _L1_xattn_ref(x, latents, mask, ln_x_g, ln_x_b, ln_l_g, ln_l_b, qn_g, kn_g, Wq, Wkv, Wout, bout):
        import jax, jax.numpy as jnp
        import numpy as np
        DIM = 128
        DIM_LATENT = 128
        DIM_HEAD = 64
        HEADS = 16
        INNER = HEADS * DIM_HEAD

        def layernorm(x, g, b, eps=1e-05):
            m = jnp.mean(x, axis=-1, keepdims=True)
            v = jnp.mean((x - m) ** 2, axis=-1, keepdims=True)
            return (x - m) / jnp.sqrt(v + eps) * g + b

        def rmsnorm(x, gamma, eps=1e-08):
            n = jnp.linalg.norm(x, axis=-1, keepdims=True) * x.shape[-1] ** (-0.5)
            return x / jnp.maximum(n, eps) * gamma
        b, n, _ = x.shape
        m = latents.shape[1]
        h, d = (HEADS, DIM_HEAD)
        scale = d ** (-0.5)
        xn = layernorm(x, ln_x_g, ln_x_b)
        ln = layernorm(latents, ln_l_g, ln_l_b)
        q = (ln @ Wq).reshape(b, m, h, d).transpose(0, 2, 1, 3)
        kv = jnp.concatenate([xn @ Wkv, ln @ Wkv], axis=1)
        kv = kv.reshape(b, n + m, 2, h, d)
        k = kv[:, :, 0].transpose(0, 2, 1, 3)
        v = kv[:, :, 1].transpose(0, 2, 1, 3)
        qn = rmsnorm(q, qn_g) * scale
        kn = rmsnorm(k, kn_g)
        sim = jnp.einsum('bhid,bhjd->bhij', qn, kn)
        max_neg = -jnp.finfo(sim.dtype).max
        padded_mask = jnp.concatenate([mask, jnp.ones((b, m), bool)], axis=1)
        sim = jnp.where(padded_mask[:, None, None, :], sim, max_neg)
        attn = jax.nn.softmax(sim.astype(jnp.float32), axis=-1).astype(sim.dtype)
        out = jnp.einsum('bhij,bhjd->bhid', attn, v)
        out = out.transpose(0, 2, 1, 3).reshape(b, m, h * d)
        return out @ Wout + bout

    def _L1_ffn_ref(x, w_gate, w_up, w_down):
        import jax, jax.numpy as jnp
        import numpy as np
        HIDDEN = 128
        INNER = 512

        def _weight_quant(w):
            scale = 1.0 / jnp.clip(jnp.mean(jnp.abs(w)), 1e-05)
            wq = jnp.clip(jnp.round(w * scale), -1.0, 1.0) / scale
            return w + jax.lax.stop_gradient(wq - w)

        def _act_quant(x):
            scale = 127.0 / jnp.clip(jnp.max(jnp.abs(x), axis=-1, keepdims=True), 1e-05)
            xq = jnp.clip(jnp.round(x * scale), -128.0, 127.0) / scale
            return x + jax.lax.stop_gradient(xq - x)

        def _bitlinear(x, w):
            return jnp.einsum('bsi,oi->bso', _act_quant(x), _weight_quant(w))
        gate = jax.nn.silu(_bitlinear(x, w_gate))
        up = _bitlinear(x, w_up)
        return _bitlinear(gate * up, w_down)
    x = _layernorm(x + _L0_attn_ref(x, L0_attn_ln_w, L0_attn_ln_b, L0_attn_W_qkv, L0_attn_b_qkv, L0_attn_W_proj, L0_attn_b_proj), axis=-1)
    x = _layernorm(x + _L0_xattn_ref(x, ctx_1024, L0_xattn_W, L0_xattn_b), axis=-1)
    x = _layernorm(x + _L0_ffn_ref(x, L0_ffn_gate_w, L0_ffn_w_gate, L0_ffn_w_up, L0_ffn_w_down, L0_ffn_sw_gate, L0_ffn_sw_up, L0_ffn_sw_down), axis=-1)
    x = _layernorm(x + _L1_attn_ref(x, L1_attn_g1, L1_attn_b1, L1_attn_Wa, L1_attn_ba, L1_attn_Wb, L1_attn_bb, L1_attn_Wc, L1_attn_bc, L1_attn_g2, L1_attn_b2, L1_attn_W1, L1_attn_bm1, L1_attn_W2, L1_attn_bm2), axis=-1)
    x = _layernorm(x + _L1_xattn_ref(ctx_1024, x, mask_BxS2_bf1, L1_xattn_ln_x_g, L1_xattn_ln_x_b, L1_xattn_ln_l_g, L1_xattn_ln_l_b, L1_xattn_qn_g, L1_xattn_kn_g, L1_xattn_Wq, L1_xattn_Wkv, L1_xattn_Wout, L1_xattn_bout), axis=-1)
    x = _layernorm(x + _L1_ffn_ref(x, L1_ffn_w_gate, L1_ffn_w_up, L1_ffn_w_down), axis=-1)
    return x

_drawn_inputs = setup_inputs


def setup_inputs(seed=0):
    import zlib

    import numpy as np

    out = dict(_drawn_inputs(seed))
    spreads = {'L0_attn_ln_w': (1.0, 0.6),
     'L0_attn_ln_b': (0.0, 0.8),
     'L0_attn_b_qkv': (0.0, 0.645),
     'L0_attn_b_proj': (0.0, 0.1),
     'L1_attn_g1': (1.0, 0.6),
     'L1_attn_b1': (0.0, 0.586),
     'L1_attn_ba': (0.0, 2.0),
     'L1_attn_bb': (0.0, 0.368),
     'L1_attn_bc': (0.0, 0.8),
     'L1_attn_g2': (1.0, 0.6),
     'L1_attn_b2': (0.0, 0.773),
     'L1_attn_bm1': (0.0, 0.408),
     'L1_attn_bm2': (0.0, 0.1),
     'L1_xattn_ln_x_g': (1.0, 0.6),
     'L1_xattn_ln_x_b': (0.0, 0.8),
     'L1_xattn_ln_l_g': (1.0, 0.6),
     'L1_xattn_ln_l_b': (0.0, 0.8),
     'L1_xattn_qn_g': (1.0, 0.6),
     'L1_xattn_kn_g': (1.0, 0.6),
     'L1_xattn_bout': (0.0, 0.1)}
    factors = {'L0_attn_W_qkv': 8.0,
     'L0_attn_W_proj': 3.856,
     'L0_ffn_gate_w': 5.118,
     'L0_ffn_w_gate': 4.517,
     'L0_ffn_w_up': 4.48,
     'L0_ffn_w_down': 4.471,
     'L0_ffn_sw_gate': 5.58,
     'L0_ffn_sw_up': 5.562,
     'L0_ffn_sw_down': 5.571}
    for name, (base, spread) in spreads.items():
        noise = np.random.default_rng([zlib.crc32(name.encode()), seed]).standard_normal(out[name].shape)
        drawn = base * np.exp(spread * noise) if base else spread * noise
        out[name] = jnp.asarray(drawn.astype(out[name].dtype))
    for name, factor in factors.items():
        out[name] = (out[name] * factor).astype(out[name].dtype)
    return out
```

```python
from contextlib import ExitStack, contextmanager

import numpy as np

import concourse.bass as bass
from concourse import mybir

F32 = mybir.dt.float32
BF16 = mybir.dt.bfloat16
ALU = mybir.AluOpType
ACT = mybir.ActivationFunctionType
AX = mybir.AxisListType.X

NB, S, D = 32, 128, 128
NH0, DH0 = 16, 8
NE, FE, FS = 8, 176, 352
FF = NE * FE + FS
FCH = [(c, min(128, FF - c)) for c in range(0, FF, 128)]
NEC = NE * FE // 128
HM = 4 * D
NH1, DH1 = 16, 64
INNER = NH1 * DH1
FB = 512
EPS = 1e-5
MAGIC = 1.5 * 2.0 ** 23


class Shared:
    pass


@contextmanager
def semaphores(nc, prefix):
    taken = []

    def sem(name):
        taken.append(nc.alloc_semaphore(name=prefix + name))
        return taken[-1]

    yield sem
    nc.clear_and_free_semaphores(taken)
    nc.all_engine_barrier()


def wait(eng, sem, count):
    if isinstance(count, int) and count <= 0:
        return
    eng.wait_ge(sem, count)


def wait_apart(eng, sem, count, passed):
    wait(eng, sem, count)
    if not isinstance(count, int):
        eng.sem_inc(passed, 1)


def live(i, n):
    return not isinstance(i, int) or 0 <= i < n


def steps(eng, n, lag, head, body):
    assert (n - head) % 2 == 0
    for t in range(head):
        body(t, t % 2)
    with eng.Fori(0, (n - head) // 2) as r:
        for u in range(2):
            body(r * 2 + (head + u), (head + u) % 2)
    for t in range(n, n + lag):
        body(t, t % 2)


def load_stage(nc, K, ctx, early):
    def sb(name, shape, dt=F32):
        return ctx.enter_context(nc.sbuf_tensor(name, shape, dt))

    def sb_early(name, shape, dt=F32):
        return early.enter_context(nc.sbuf_tensor(name, shape, dt))

    def sem(name):
        return ctx.enter_context(nc.semaphore(name))

    K.X = sb("x_tok", [S, NB, D])
    K.CTX = sb("ctx_tok", [S, NB, D])
    K.ident = sb("ident", [128, 128])
    K.identb = sb("identb", [128, 128], BF16)
    K.ones = sb("ones", [128, 128])
    K.onesb = sb("onesb", [1, 128])
    K.half = sb("minus_half", [128, 64])
    K.eps = sb("eps", [128, 64])
    K.colsx = sb("colsx", [128, 6])
    K.qg = sb("qg_scaled", [128, 1])
    K.wq1 = sb("wq1", [D, INNER])
    K.wkv1 = sb("wkv1", [D, 2 * INNER])
    K.wout = sb("wout", [128, INNER // 128, D])
    K.bout = sb("bout_row", [1, D])
    K.wbraw = sb("wb_raw", [128, 3, FB])
    K.head_mask = sb_early("head_mask", [128, 8])
    K.ones_mask = sb_early("ones_mask", [128, 4, 32])
    K.tie = sb_early("tie", [128, 64])
    K.expert_of = sb_early("expert_of", [24, NE * FE])
    K.expert_ofb = sb_early("expert_ofb", [24, NE * FE], BF16)
    K.w_qkv = sb_early("w_qkv", [D, 3 * D])
    K.w_proj = sb_early("w_proj", [D, D])
    K.cols0 = sb_early("cols0", [128, 4])
    K.bv = sb_early("bv_rows", [128, D])
    K.bproj = sb_early("bproj_rows", [128, D])
    K.wx = sb_early("wx_raw", [D, 2 * D])
    K.wxT = sb_early("wxT", [128, 2 * D])
    K.bx = sb_early("bx_row", [1, D])
    K.gate_raw = sb_early("gate_raw", [NE, D])
    K.gateT = sb_early("gateT", [D, NE])
    K.wg = sb_early("wg", [D, FF])
    K.wu = sb_early("wu", [D, FF])
    K.wd = sb_early("wd", [128, len(FCH), D])
    K.wabc = sb_early("wabc", [D, 3, D])
    K.cols1 = sb_early("cols1", [128, 7])
    K.habc = sb_early("half_ba_bc", [128, 3])
    K.w1 = sb_early("w1", [D, HM])
    K.bm1 = sb_early("bm1", [128, HM // 128])
    K.w2 = sb_early("w2", [128, HM // 128, D])
    K.bm2 = sb_early("bm2_row", [1, D])
    K.x_in, K.ctx_in = sem("x_in"), sem("ctx_in")
    K.consts_in, K.w0_in, K.wx_in = sem("consts_in"), sem("w0_in"), sem("wx_in")
    K.moe_in, K.w1_in, K.wx1_in, K.wb_in = sem("moe_in"), sem("w1_in"), sem("wx1_in"), sem("wb_in")
    K.n_in = {}
    K.small_ready = sem("small_ready")
    A = K.A

    with nc.Block() as block:
        @block.sync
        def _(sp):
            def load(s, dst, src):
                K.n_in[s.name] = K.n_in.get(s.name, 0) + 16
                sp.dma_start(dst, src).then_inc(s, 16)

            xs = A["x"].rearrange("b s d -> s b d")
            cs = A["ctx_1024"].rearrange("b s d -> s b d")
            load(K.x_in, K.X[:, 0:4, :], xs[:, 0:4, :])
            load(K.consts_in, K.ident[:], A["c_ident"])
            load(K.consts_in, K.head_mask[:], A["c_head_mask"])
            load(K.consts_in, K.ones_mask[:], A["c_ones_mask"])
            load(K.w0_in, K.w_qkv[:], A["L0_attn_W_qkv"])
            load(K.w0_in, K.cols0[:, 0:1], A["L0_attn_ln_w"].rearrange("(p o) -> p o", o=1))
            load(K.w0_in, K.cols0[:, 1:2], A["L0_attn_ln_b"].rearrange("(p o) -> p o", o=1))
            for n in range(2):
                load(K.w0_in, K.cols0[:, 2 + n:3 + n], A["L0_attn_b_qkv"][D * n:D * n + D].rearrange("(p o) -> p o", o=1))
            load(K.w0_in, K.bv[:], A["L0_attn_b_qkv"][2 * D:3 * D].partition_broadcast(128))
            load(K.w0_in, K.w_proj[:], A["L0_attn_W_proj"])
            load(K.w0_in, K.bproj[:], A["L0_attn_b_proj"].partition_broadcast(128))
            for b in range(4, NB, 7):
                load(K.x_in, K.X[:, b:b + 7, :], xs[:, b:b + 7, :])
            load(K.consts_in, K.tie[:], A["c_tie"].partition_broadcast(128))
            load(K.consts_in, K.expert_of[:], A["c_expert_of"])
            for b in range(0, NB, 8):
                load(K.ctx_in, K.CTX[:, b:b + 8, :], cs[:, b:b + 8, :])
            load(K.wx_in, K.wx[:], A["L0_xattn_W"])
            load(K.wx_in, K.bx[:], A["L0_xattn_b"].rearrange("(o d) -> o d", o=1))
            load(K.wx_in, K.gate_raw[:], A["L0_ffn_gate_w"])
            for dst, w, shared in ((K.wg, "w_gate", "sw_gate"), (K.wu, "w_up", "sw_up")):
                load(K.moe_in, dst[:, 0:NE * FE].rearrange("d (e f) -> d e f", e=NE),
                     A["L0_ffn_" + w].rearrange("e d f -> d e f"))
                load(K.moe_in, dst[:, NE * FE:FF], A["L0_ffn_" + shared])
            down = A["L0_ffn_w_down"].rearrange("e f d -> (e f) d")
            load(K.moe_in, K.wd[:, 0:NEC, :], down.rearrange("(c p) d -> p c d", p=128))
            for n, (c, w) in enumerate(FCH):
                if n >= NEC:
                    load(K.moe_in, K.wd[0:w, n, :], A["L0_ffn_sw_down"][c - NE * FE:c - NE * FE + w, :])
            for n, w in enumerate(("Wa", "Wb", "Wc")):
                load(K.w1_in, K.wabc[:, n, :], A["L1_attn_" + w])
            for n, w in enumerate(("g1", "b1", "ba", "bb", "bc", "g2", "b2")):
                load(K.w1_in, K.cols1[:, n:n + 1], A["L1_attn_" + w].rearrange("(p o) -> p o", o=1))
            load(K.w1_in, K.w1[:], A["L1_attn_W1"])
            for n in range(HM // 128):
                load(K.w1_in, K.bm1[:, n:n + 1], A["L1_attn_bm1"][128 * n:128 * n + 128].rearrange("(p o) -> p o", o=1))
            load(K.w1_in, K.w2[:], A["L1_attn_W2"].rearrange("(c p) d -> p c d", p=128))
            load(K.w1_in, K.bm2[:], A["L1_attn_bm2"].rearrange("(o d) -> o d", o=1))
            for n, w in enumerate(("ln_x_g", "ln_x_b", "ln_l_g", "ln_l_b")):
                load(K.wx1_in, K.colsx[:, n:n + 1], A["L1_xattn_" + w].rearrange("(p o) -> p o", o=1))
            for n, w in enumerate(("qn_g", "kn_g")):
                for half in range(2):
                    load(K.wx1_in, K.colsx[64 * half:64 * half + 64, 4 + n:5 + n],
                         A["L1_xattn_" + w].rearrange("(p o) -> p o", o=1))
            load(K.wx1_in, K.wq1[:], A["L1_xattn_Wq"])
            load(K.wx1_in, K.wkv1[:], A["L1_xattn_Wkv"])
            load(K.wx1_in, K.wout[:], A["L1_xattn_Wout"].rearrange("(c p) d -> p c d", p=128))
            load(K.wx1_in, K.bout[:], A["L1_xattn_bout"].rearrange("(o d) -> o d", o=1))
            for n, w in enumerate(("w_gate", "w_up")):
                load(K.wb_in, K.wbraw[:, n, :].rearrange("p (c i) -> p c i", c=4),
                     A["L1_ffn_" + w].rearrange("(c p) i -> p c i", p=128))
            load(K.wb_in, K.wbraw[:, 2, :], A["L1_ffn_w_down"])

        @block.gpsimd
        def _(pool):
            nc.gpsimd.memset(K.ones[:], 1.0)
            nc.gpsimd.memset(K.onesb[:], 1.0)
            nc.gpsimd.memset(K.half[:], -0.5)
            nc.gpsimd.memset(K.eps[:], EPS)
            nc.gpsimd.memset(K.magic[:], MAGIC)

        @block.vector
        def _(dve):
            dve.wait_ge(K.consts_in, 16 * 5)
            nc.vector.tensor_copy(K.identb[:], K.ident[:])
            nc.vector.tensor_copy(K.expert_ofb[:], K.expert_of[:])


def self_attention(nc, K):
    LAG, HEAD = 6, 8
    with ExitStack() as ctx:
        def sb(name, shape, dt=F32):
            return ctx.enter_context(nc.sbuf_tensor("a_" + name, shape, dt))

        sem = ctx.enter_context(semaphores(nc, "a_"))

        bn = sb("bn", [S, 6])
        mv = sb("mv", [S, 2, 2])
        rstd = sb("rstd", [S, 2, 1])
        veps = sb("veps", [S, 2, 1])
        bn2 = sb("bn2", [S, 6])
        mv2 = sb("mv2", [S, 2, 2])
        rstd2 = sb("rstd2", [S, 2, 1])
        veps2 = sb("veps2", [S, 2, 1])
        zn = sb("zn", [S, 2, D])
        znT = sb("znT", [D, 2, S])
        q = sb("q", [D, 2, S])
        kmask = sb("kmask", [D, 2, 8, S])
        vmask = sb("vmask", [S, 2, NH0, 32])
        neg_max = sb("neg_max", [S, 2, NH0])
        prob = sb("prob", [S, 2, NH0, S])
        probT = sb("probT", [S, NH0, S])
        recip = sb("recip", [D, S])
        att = sb("att", [D, 2, S])
        resid = sb("resid", [S, 2, D])
        r = sb("r", [S, 2, D])
        score, ring, tq, out = K.bank[0:4], K.bank[4:6], K.bank[6], K.bank[7]

        stat, agg, rst, veps_s, zn_s = sem("stat"), sem("agg"), sem("rst"), sem("veps"), sem("zn")
        znT_ps, znT_s, qkv_ps = sem("znT_ps"), sem("znT"), sem("qkv_ps")
        q_s, k_s, v_s, vzero = sem("q"), sem("k"), sem("v"), sem("vzero")
        s_ps, mx, ex = sem("s_ps"), sem("mx"), sem("ex")
        pT_ps, pT_dve, pT_act = sem("pT_ps"), sem("pT_dve"), sem("pT_act")
        pv_ps, rc, att_s, y_ps = sem("pv_ps"), sem("rc"), sem("att"), sem("y_ps")
        res0, res_s, r_s = sem("res0"), sem("res"), sem("r")
        stat2, agg2, veps2_s, rst2, x_s = sem("stat2"), sem("agg2"), sem("veps2"), sem("rst2"), sem("x_new")

        passed = sem("passed")
        block = ctx.enter_context(nc.Block())

        @block.gpsimd
        def _(pool):
            nc.gpsimd.memset(vmask[:], 0.0).then_inc(vzero, 1)
            pool.wait_ge(K.w0_in, K.n_in[K.w0_in.name])
            pool.wait_ge(K.x_in, K.n_in[K.x_in.name])

            def body(t, p):
                i, b = t, p
                if live(i, NB):
                    wait(pool, agg, i + 1)
                    nc.gpsimd.tensor_tensor(veps[:, b], mv[:, b, 1:2], K.eps[:, 0:1], ALU.add).then_inc(veps_s, 1)
                    wait(pool, veps_s, i + 1)
                    nc.gpsimd.tensor_tensor(rstd[:, b], veps[:, b], K.half[:, 0:1], ALU.pow).then_inc(rst, 1)
                i, b = t - 5, (p - 5) % 2
                if live(i, NB):
                    wait(pool, r_s, i - 1)
                    nc.gpsimd.tensor_tensor(resid[:, b], K.X[:, i, :], K.X[:, i, :], ALU.add).then_inc(res0, 1)
                    wait(pool, res0, i + 1)
                    nc.gpsimd.tensor_tensor(resid[:, b], resid[:, b], K.bproj[:], ALU.add).then_inc(res_s, 1)
                i, b = t - 6, (p - 6) % 2
                if live(i, NB):
                    wait(pool, agg2, i + 1)
                    nc.gpsimd.tensor_tensor(veps2[:, b], mv2[:, b, 1:2], K.eps[:, 0:1], ALU.add).then_inc(veps2_s, 1)
                    wait(pool, veps2_s, i + 1)
                    nc.gpsimd.tensor_tensor(rstd2[:, b], veps2[:, b], K.half[:, 0:1], ALU.pow).then_inc(rst2, 1)
            steps(pool, NB, LAG, HEAD, body)

        @block.vector
        def _(dve):
            dve.wait_ge(K.consts_in, K.n_in[K.consts_in.name])
            dve.wait_ge(K.w0_in, K.n_in[K.w0_in.name])
            dve.wait_ge(K.x_in, K.n_in[K.x_in.name])
            dve.wait_ge(vzero, 1)

            def row_max(i, b, j):
                wait(dve, s_ps, i * 4 + (j + 1))
                nc.vector.tensor_reduce(neg_max[:, b, 4 * j:4 * j + 4],
                                        score[j][:].rearrange("q (h k) -> q h k", h=4),
                                        AX, ALU.max, negate=True).then_inc(mx, 1)

            def turn(i, j):
                wait(dve, pT_ps, i * 4 + (j + 1))
                wait(dve, pv_ps, i)
                nc.vector.tensor_copy(probT[:, 4 * j:4 * j + 4, :],
                                      ring[j % 2][:].rearrange("k (h q) -> k h q", h=4)).then_inc(pT_dve, 1)

            def body(t, p):
                i, b = t, p
                if live(i, NB):
                    nc.vector.bn_stats(bn[:], K.X[:, i, :]).then_inc(stat, 1)
                    wait(dve, stat, i + 1)
                    wait_apart(dve, rst, i - 1, passed)
                    nc.vector.bn_aggr(mv[:, b], bn[:]).then_inc(agg, 1)
                i, b = t - 5, (p - 5) % 2
                if live(i, NB):
                    wait(dve, pv_ps, i + 1)
                    nc.vector.reciprocal(recip[:], out[:, 128:256]).then_inc(rc, 1)
                    wait(dve, rc, i + 1)
                    wait(dve, y_ps, i - 1)
                    nc.vector.tensor_tensor(att[:, b], out[:, 0:128], recip[:], ALU.mult).then_inc(att_s, 1)
                i3, b3 = t - 3, (p - 3) % 2
                i4 = t - 4
                if live(i3, NB):
                    row_max(i3, b3, 0)
                if live(i4, NB):
                    turn(i4, 0)
                i, b = t - 6, (p - 6) % 2
                if live(i, NB):
                    wait(dve, y_ps, i + 1)
                    wait(dve, res_s, i + 1)
                    nc.vector.tensor_tensor(r[:, b], out[:, 256:384], resid[:, b], ALU.add).then_inc(r_s, 1)
                    wait(dve, r_s, i + 1)
                    nc.vector.bn_stats(bn2[:], r[:, b]).then_inc(stat2, 1)
                    wait(dve, stat2, i + 1)
                    wait_apart(dve, rst2, i - 1, passed)
                    nc.vector.bn_aggr(mv2[:, b], bn2[:]).then_inc(agg2, 1)
                if live(i3, NB):
                    row_max(i3, b3, 1)
                if live(i4, NB):
                    turn(i4, 1)
                i, b = t, p
                if live(i, NB):
                    wait(dve, rst, i + 1)
                    wait(dve, znT_ps, i - 1)
                    nc.vector.tensor_scalar(zn[:, b], K.X[:, i, :], mv[:, b, 0:1], rstd[:, b],
                                            ALU.subtract, ALU.mult).then_inc(zn_s, 1)
                i, b = t - 1, (p - 1) % 2
                if live(i, NB):
                    wait(dve, znT_ps, i + 1)
                    wait(dve, qkv_ps, i)
                    nc.vector.tensor_scalar(znT[:, b], tq[:, 0:128], K.cols0[:, 0:1], K.cols0[:, 1:2],
                                            ALU.mult, ALU.add).then_inc(znT_s, 1)
                if live(i3, NB):
                    row_max(i3, b3, 2)
                i, b = t - 6, (p - 6) % 2
                if live(i, NB):
                    wait(dve, rst2, i + 1)
                    nc.vector.tensor_scalar(K.X[:, i, :], r[:, b], mv2[:, b, 0:1], rstd2[:, b],
                                            ALU.subtract, ALU.mult).then_inc(x_s, 1)
                if live(i3, NB):
                    row_max(i3, b3, 3)
                i, b = t - 2, (p - 2) % 2
                if live(i, NB):
                    wait(dve, qkv_ps, i + 1)
                    wait(dve, s_ps, (i - 1) * 4)
                    nc.vector.scalar_tensor_tensor(
                        out=kmask[:, b], in0=tq[:, 256:384].unsqueeze(1).to_broadcast([D, 8, S]),
                        scalar=K.cols0[:, 3:4], in1=K.head_mask[:].unsqueeze(2).to_broadcast([D, 8, S]),
                        op0=ALU.add, op1=ALU.mult).then_inc(k_s, 1)
                    nc.vector.tensor_scalar(q[:, b], tq[:, 128:256], K.cols0[:, 2:3], float(DH0) ** -0.5,
                                            ALU.add, ALU.mult).then_inc(q_s, 1)
                    wait(dve, pv_ps, i - 1)
                    nc.vector.tensor_tensor(
                        head_columns(vmask, b),
                        tq[:, 384:512].rearrange("k (j g c) -> k j g c", j=4, g=4),
                        K.bv[:].rearrange("k (j g c) -> k j g c", j=4, g=4), ALU.add).then_inc(v_s, 1)
            steps(dve, NB, LAG, HEAD, body)

        @block.scalar
        def _(act):
            def exps(i, b, j):
                wait(act, mx, i * 4 + (j + 1))
                wait(act, pT_ps, (i - 1) * 4)
                for h in range(4 * j, 4 * j + 4):
                    last = nc.scalar.activation(prob[:, b, h, :], score[j][:, 128 * (h % 4):128 * (h % 4) + 128],
                                                ACT.Exp, bias=neg_max[:, b, h:h + 1])
                last.then_inc(ex, 1)

            def turn(i, j):
                wait(act, pT_ps, i * 4 + (j + 1))
                wait(act, pv_ps, i)
                nc.scalar.copy(probT[:, 4 * j:4 * j + 4, :],
                               ring[j % 2][:].rearrange("k (h q) -> k h q", h=4)).then_inc(pT_act, 1)

            def body(t, p):
                i3, b3, i4 = t - 3, (p - 3) % 2, t - 4
                if live(i3, NB):
                    exps(i3, b3, 0)
                    exps(i3, b3, 1)
                if live(i4, NB):
                    turn(i4, 2)
                if live(i3, NB):
                    exps(i3, b3, 2)
                if live(i4, NB):
                    turn(i4, 3)
                if live(i3, NB):
                    exps(i3, b3, 3)
            steps(act, NB, LAG, HEAD, body)

        @block.tensor
        def _(pe):
            pe.wait_ge(K.consts_in, K.n_in[K.consts_in.name])
            pe.wait_ge(K.w0_in, K.n_in[K.w0_in.name])

            def scores(i, b, j):
                rows = slice(64 * (j // 2), 64 * (j // 2) + 64)
                wait(pe, q_s, i + 1)
                wait(pe, k_s, i + 1)
                wait(pe, ex, (i - 1) * 4 + (j + 1))
                nc.tensor.matmul(score[j][:], q[rows, b, :], kmask[rows, b, 4 * (j % 2):4 * (j % 2) + 4, :],
                                 start=True, stop=True).then_inc(s_ps, 1)

            def turn(i, b, j):
                wait(pe, ex, i * 4 + (j + 1))
                if j < 2:
                    wait(pe, pT_act, (i - 1) * 2 + (j + 1))
                else:
                    wait(pe, pT_dve, i * 2 + (j - 1))
                for h in range(4 * j, 4 * j + 4):
                    last = nc.tensor.transpose(ring[j % 2][:, 128 * (h % 4):128 * (h % 4) + 128],
                                               prob[:, b, h, :], K.ident[:])
                last.then_inc(pT_ps, 1)

            def body(t, p):
                i3, b3, i4, b4 = t - 3, (p - 3) % 2, t - 4, (p - 4) % 2
                for j in range(4):
                    if live(i3, NB):
                        scores(i3, b3, j)
                    if live(i4, NB):
                        turn(i4, b4, j)
                    if j == 1:
                        i, b = t - 1, (p - 1) % 2
                        if live(i, NB):
                            wait(pe, zn_s, i + 1)
                            wait(pe, znT_s, i)
                            wait(pe, v_s, i - 1)
                            nc.tensor.transpose(tq[:, 0:128], zn[:, b], K.ident[:]).then_inc(znT_ps, 1)
                        i, b = t - 2, (p - 2) % 2
                        if live(i, NB):
                            wait(pe, znT_s, i + 1)
                            wait(pe, v_s, i)
                            nc.tensor.matmul(tq[:, 128:256], K.w_qkv[:, 0:128], znT[:, b], start=True, stop=True)
                            nc.tensor.matmul(tq[:, 256:384], K.w_qkv[:, 128:256], znT[:, b], start=True, stop=True)
                            nc.tensor.matmul(tq[:, 384:512], znT[:, b], K.w_qkv[:, 256:384],
                                             start=True, stop=True).then_inc(qkv_ps, 1)
                i, b = t - 5, (p - 5) % 2
                if live(i, NB):
                    wait(pe, att_s, i + 1)
                    wait(pe, r_s, i)
                    nc.tensor.matmul(out[:, 256:384], att[:, b], K.w_proj[:], start=True, stop=True).then_inc(y_ps, 1)
                if live(i4, NB):
                    wait(pe, v_s, i4 + 1)
                    wait(pe, pT_dve, i4 * 2 + 2)
                    wait(pe, pT_act, i4 * 2 + 2)
                    wait(pe, att_s, i4)
                    for cols, weights in ((slice(0, 128), 0), (slice(128, 256), 1)):
                        for g in range(4):
                            for j in range(4):
                                h = 4 * j + g
                                lhsT = K.ones_mask[:, g, :] if weights else vmask[:, b4, h, :]
                                last = nc.tensor.matmul(out[32 * j:32 * j + 32, cols], lhsT, probT[:, h, :],
                                                        start=(g == 0), stop=(g == 3))
                    last.then_inc(pv_ps, 1)
            steps(pe, NB, LAG, HEAD, body)


def head_columns(vmask, b):
    v = vmask[:, b, :, :].rearrange("k (j g) (e c) -> k j g e c", j=4, e=4)
    return diagonal(v)


def diagonal(v):
    (ps, pn), (js, jn), (gs, gn), (es, en), (cs, cn) = [tuple(x) for x in v.ap]
    return bass.AP(tensor=v.tensor, offset=v.offset, ap=[[ps, pn], [js, jn], [gs + es, gn], [cs, cn]])


def context_mix(nc, K):
    NG = NB // 4
    LAG, HEAD = 3, 4
    with ExitStack() as ctx:
        def sb(name, shape, dt=F32):
            return ctx.enter_context(nc.sbuf_tensor("b_" + name, shape, dt))

        sem = ctx.enter_context(semaphores(nc, "b_"))

        mean_row = sb("mean_col", [D, NB])
        xT = sb("xT", [D, 2, 512])
        mT = sb("mT", [D, 2, 512])
        x2T = sb("x2T", [D, 2, 512])
        xs = sb("xs", [S, 2, 4, D])
        x2s = sb("x2s", [S, 2, 4, D])
        r = sb("r", [S, 2, 4, D])
        bn = sb("bn", [S, 4, 6])
        mv = sb("mv", [S, 2, 4, 2])
        veps = sb("veps", [S, 2, 4])
        rstd = sb("rstd", [S, 2, 4])
        turn_ps, y_ps, turn2_ps, logit_ps, prep = K.bank[0], K.bank[1], K.bank[2], K.bank[3], K.bank[4]
        mean_ps = K.bank[5]

        prep_ps, prep_s, mean_p, mean_s, inv_s = sem("prep_ps"), sem("prep"), sem("mean_ps"), sem("mean"), sem("inv")
        xs_s, X_s = sem("xs"), sem("X")
        xT_ps, xT_s, mT_s, y_s, r_s = sem("xT_ps"), sem("xT"), sem("mT"), sem("y_ps"), sem("r")
        stat, agg, veps_s, rst, x_s = sem("stat"), sem("agg"), sem("veps"), sem("rst"), sem("x_new")
        x2T_ps, x2T_s, XT_s, lg_ps, lg_s = sem("x2T_ps"), sem("x2T"), sem("XT"), sem("lg_ps"), sem("lg")
        inv = sb("inv", [S, 2])
        passed = sem("passed")
        block = ctx.enter_context(nc.Block())

        @block.gpsimd
        def _(pool):
            nc.gpsimd.memset(inv[:], 1.0 / S).then_inc(inv_s, 1)

            def body(t, p):
                i, b = t, p
                if live(i, NG):
                    wait_apart(pool, xT_ps, i - 1, passed)
                    nc.gpsimd.tensor_copy(xs[:, b], K.X[:, bass.ds(i * 4, 4), :]).then_inc(xs_s, 1)
                i, b = t - 2, p
                if live(i, NG):
                    wait(pool, agg, i * 4 + 4)
                    nc.gpsimd.tensor_tensor(veps[:, b], mv[:, b, :, 1], K.eps[:, 0:4], ALU.add).then_inc(veps_s, 1)
                    wait(pool, veps_s, i + 1)
                    nc.gpsimd.tensor_tensor(rstd[:, b], veps[:, b], K.half[:, 0:4], ALU.pow).then_inc(rst, 1)
                    wait_apart(pool, x_s, i * 4 + 4, passed)
                    nc.gpsimd.tensor_copy(K.X[:, bass.ds(i * 4, 4), :], x2s[:, b]).then_inc(X_s, 1)
            steps(pool, NG, LAG, HEAD, body)

        @block.vector
        def _(dve):
            dve.wait_ge(prep_ps, 1)
            nc.vector.tensor_copy(K.wxT[:], prep[:, 0:256]).then_inc(prep_s, 1)
            nc.vector.tensor_copy(K.gateT[:], prep[:, 256:264]).then_inc(prep_s, 1)
            dve.wait_ge(mean_p, 1)
            nc.vector.tensor_copy(mean_row[:], mean_ps[:, 0:NB]).then_inc(mean_s, 1)
            dve.wait_ge(mean_s, 1)

            def body(t, p):
                i, b = t - 1, (p - 1) % 2
                if live(i, NG):
                    wait(dve, y_s, i - 1)
                    nc.vector.tensor_copy(mT[:, b].rearrange("d (n s) -> d n s", n=4),
                                          mean_row[:, bass.ds(i * 4, 4)].unsqueeze(2).to_broadcast([D, 4, S])
                                          ).then_inc(mT_s, 1)
                i, b = t - 2, p
                if live(i, NG):
                    wait(dve, y_s, i + 1)
                    nc.vector.tensor_tensor(r[:, b], y_ps[:].rearrange("s (n d) -> s n d", n=4),
                                            K.X[:, bass.ds(i * 4, 4), :], ALU.add).then_inc(r_s, 1)
                    wait(dve, r_s, i + 1)
                    for n in range(4):
                        nc.vector.bn_stats(bn[:, n], r[:, b, n]).then_inc(stat, 1)
                    for n in range(4):
                        wait_apart(dve, stat, i * 4 + (n + 1), passed)
                        nc.vector.bn_aggr(mv[:, b, n], bn[:, n]).then_inc(agg, 1)
                    wait(dve, rst, i + 1)
                    wait(dve, x2T_ps, i - 1)
                    wait(dve, X_s, i - 1)
                    for n in range(4):
                        nc.vector.tensor_scalar(x2s[:, b, n], r[:, b, n], mv[:, b, n, 0:1],
                                                rstd[:, b, n:n + 1], ALU.subtract, ALU.mult).then_inc(x_s, 1)
                i = t - 3
                if live(i, NG):
                    wait(dve, lg_ps, i + 1)
                    nc.vector.tensor_copy(K.logits[:, bass.ds(i * 4, 4), :],
                                          logit_ps[:, 0:32].rearrange("s (n e) -> s n e", n=4)).then_inc(lg_s, 1)
            steps(dve, NG, LAG, HEAD, body)

        @block.scalar
        def _(act):
            def body(t, p):
                i, b = t, p
                if live(i, NG):
                    wait(act, xT_ps, i + 1)
                    wait(act, y_s, i - 1)
                    nc.scalar.copy(xT[:, b], turn_ps[:]).then_inc(xT_s, 1)
                i, b = t - 3, (p - 3) % 2
                if live(i, NG):
                    wait(act, x2T_ps, i + 1)
                    wait(act, lg_ps, i - 1)
                    nc.scalar.copy(x2T[:, b], turn2_ps[:]).then_inc(x2T_s, 1)
                    nc.scalar.copy(K.XT[:, bass.ds(i * 512, 512)], turn2_ps[:]).then_inc(XT_s, 1)
            steps(act, NG, LAG, HEAD, body)

        @block.tensor
        def _(pe):
            pe.wait_ge(K.wx_in, K.n_in[K.wx_in.name])
            pe.wait_ge(K.ctx_in, K.n_in[K.ctx_in.name])
            for n in range(2):
                nc.tensor.transpose(prep[:, 128 * n:128 * n + 128], K.wx[:, 128 * n:128 * n + 128], K.ident[:])
            nc.tensor.transpose(prep[:, 256:264], K.gate_raw[:], K.ident[0:8, 0:8]).then_inc(prep_ps, 1)
            pe.wait_ge(inv_s, 1)
            for n in range(NB):
                last = nc.tensor.matmul(mean_ps[:, n:n + 1], K.CTX[:, n, :], inv[:, 0:1], start=True, stop=True)
            last.then_inc(mean_p, 1)
            pe.wait_ge(prep_s, 2)

            def body(t, p):
                i = t
                if live(i, NG):
                    wait(pe, xs_s, i + 1)
                    wait(pe, xT_s, i)
                    for n in range(4):
                        last = nc.tensor.transpose(turn_ps[:, 128 * n:128 * n + 128], xs[:, p, n], K.ident[:])
                    last.then_inc(xT_ps, 1)
                i, b = t - 1, (p - 1) % 2
                if live(i, NG):
                    wait(pe, xT_s, i + 1)
                    wait(pe, mT_s, i + 1)
                    wait(pe, r_s, i)
                    for n in range(4):
                        c = slice(128 * n, 128 * n + 128)
                        nc.tensor.matmul(y_ps[:, c], xT[:, b, c], K.wxT[:, 0:128], start=True, stop=False)
                        nc.tensor.matmul(y_ps[:, c], mT[:, b, c], K.wxT[:, 128:256], start=False, stop=False)
                        last = nc.tensor.matmul(y_ps[:, c], K.onesb[:], K.bx[:], start=False, stop=True)
                    last.then_inc(y_s, 1)
                i, b = t - 3, (p - 3) % 2
                if live(i, NG):
                    wait(pe, x_s, i * 4 + 4)
                    wait(pe, XT_s, i)
                    for n in range(4):
                        last = nc.tensor.transpose(turn2_ps[:, 128 * n:128 * n + 128], x2s[:, b, n],
                                                   K.ident[:])
                    last.then_inc(x2T_ps, 1)
                    wait(pe, x2T_s, i + 1)
                    wait(pe, lg_s, i)
                    for n in range(4):
                        last = nc.tensor.matmul(logit_ps[:, 8 * n:8 * n + 8], x2T[:, b, 128 * n:128 * n + 128],
                                                K.gateT[:], start=True, stop=True)
                    last.then_inc(lg_ps, 1)
            steps(pe, NG, LAG, HEAD, body)


def route(nc, K):
    NG = NB // 4
    with ExitStack() as ctx:
        def sb(name, shape, dt=F32):
            return ctx.enter_context(nc.sbuf_tensor("r_" + name, shape, dt))

        sem = ctx.enter_context(semaphores(nc, "r_"))

        top = sb("top", [S, NB])
        e = sb("e", [S, NB, NE])
        total = sb("total", [S, NB])
        prob = sb("prob", [S, NB, NE])
        gt = sb("gt", [S, NB, NE, NE])
        eq = sb("eq", [S, NB, NE, NE])
        rank = sb("rank", [S, NB, NE])
        comb = sb("comb", [S, NB, NE])
        rest = sb("rest", [S, NB, NE])
        parts = sb("parts", [S, NB, 3 * NE], BF16)
        sum2 = sb("sum2", [S, NB])
        c4 = sb("c4", [S, 2, 4, 3 * NE], BF16)
        bank = [K.bank[i][:].bitcast(BF16) for i in range(2)]
        dv, ex, parts_s, c4_s, cT_ps, cT_s = sem("dve"), sem("exp"), sem("parts"), sem("c4"), sem("cT_ps"), sem("cT")
        block = ctx.enter_context(nc.Block())

        def over(x, n=NE):
            return x.unsqueeze(2).to_broadcast([S, NB, n])

        @block.vector
        def _(dve):
            done = [0]

            def then(ins):
                done[0] += 1
                ins.then_inc(dv, 1)
                dve.wait_ge(dv, done[0])

            then(nc.vector.tensor_reduce(top[:], K.logits[:], AX, ALU.max))
            nc.vector.tensor_tensor(e[:], K.logits[:], over(top[:]), ALU.subtract).then_inc(parts_s, 1)
            dve.wait_ge(ex, 1)
            then(nc.vector.tensor_reduce(total[:], prob[:], AX, ALU.add))
            then(nc.vector.reciprocal(sum2[:], total[:]))
            then(nc.vector.tensor_tensor(e[:], prob[:], over(sum2[:]), ALU.mult))
            for b in range(0, NB, 8):
                j_ = e[:, b:b + 8].unsqueeze(2).to_broadcast([S, 8, NE, NE])
                e_ = e[:, b:b + 8].unsqueeze(3).to_broadcast([S, 8, NE, NE])
                nc.vector.tensor_tensor(gt[:, b:b + 8], j_, e_, ALU.is_gt)
                then(nc.vector.tensor_tensor(eq[:, b:b + 8], j_, e_, ALU.is_equal))
            then(nc.vector.tensor_tensor(eq[:].rearrange("s b e j -> s b (e j)"),
                                         eq[:].rearrange("s b e j -> s b (e j)"),
                                         K.tie[:].unsqueeze(1).to_broadcast([S, NB, NE * NE]), ALU.mult))
            then(nc.vector.tensor_tensor(gt[:], gt[:], eq[:], ALU.add))
            then(nc.vector.tensor_reduce(rank[:], gt[:], AX, ALU.add))
            then(nc.vector.scalar_tensor_tensor(out=comb[:], in0=rank[:], scalar=1.5, in1=e[:],
                                                op0=ALU.is_lt, op1=ALU.mult))
            then(nc.vector.tensor_reduce(total[:], comb[:], AX, ALU.add))
            then(nc.vector.tensor_scalar(total[:], total[:], 1e-20, None, ALU.add))
            then(nc.vector.reciprocal(sum2[:], total[:]))
            then(nc.vector.scalar_tensor_tensor(out=comb[:], in0=comb[:], scalar=2.5, in1=over(sum2[:]),
                                                op0=ALU.mult, op1=ALU.mult))
            then(nc.vector.tensor_copy(parts[:, :, 0:NE], comb[:]))
            then(nc.vector.tensor_tensor(rest[:], comb[:], parts[:, :, 0:NE], ALU.subtract))
            then(nc.vector.tensor_copy(parts[:, :, NE:2 * NE], rest[:]))
            then(nc.vector.tensor_tensor(rest[:], rest[:], parts[:, :, NE:2 * NE], ALU.subtract))
            nc.vector.tensor_copy(parts[:, :, 2 * NE:], rest[:]).then_inc(parts_s, 1)
            dve.wait_ge(parts_s, 2)

            def body(t, p):
                i, b = t, p
                if live(i, NG):
                    wait(dve, cT_ps, i - 1)
                    nc.vector.tensor_copy(c4[:, b], parts[:, bass.ds(i * 4, 4), :]).then_inc(c4_s, 1)
            steps(dve, NG, 1, 4, body)

        @block.scalar
        def _(act):
            act.wait_ge(parts_s, 1)
            nc.scalar.activation(prob[:], e[:], ACT.Exp).then_inc(ex, 1)

            def body(t, p):
                i, b = t - 1, (p - 1) % 2
                if live(i, NG):
                    wait(act, cT_ps, i + 1)
                    nc.scalar.copy(K.combT[:, bass.ds(i * 512, 512)], bank[b][0:24, 0:512]).then_inc(cT_s, 1)
            steps(act, NG, 1, 4, body)

        @block.tensor
        def _(pe):
            def body(t, p):
                i, b = t, p
                if live(i, NG):
                    wait(pe, c4_s, i + 1)
                    wait(pe, cT_s, i - 1)
                    for n in range(4):
                        last = nc.tensor.transpose(bank[b][0:24, 128 * n:128 * n + 128], c4[:, b, n], K.identb[:])
                    last.then_inc(cT_ps, 1)
            steps(pe, NG, 1, 4, body)


def experts(nc, K):
    NG = NB // 4
    NJ = len(FCH)
    LAG, HEAD = 1, 2
    with ExitStack() as ctx:
        def sb(name, shape, dt=F32):
            return ctx.enter_context(nc.sbuf_tensor("c_" + name, shape, dt))

        sem = ctx.enter_context(semaphores(nc, "c_"))

        gate = sb("gate", [128, 2, 512])
        up = sb("up", [128, 2, 512])
        RING = 7
        hid = sb("hid", [128, RING, 512])
        r = sb("r", [S, 4, D])
        bn = sb("bn", [S, 4, 6])
        mv = sb("mv", [S, 4, 2])
        veps = sb("veps", [S, 4])
        rstd = sb("rstd", [S, 4])
        g_ps, u_ps, c_ps, y_ps = K.bank[0:2], K.bank[2:4], K.bank[4:6], K.bank[6]
        g_p, u_p, c_p = sem("gate_ps"), sem("up_ps"), sem("comb_ps")
        g_s, u_s, h_s, d_p = sem("gate"), sem("up"), sem("hid"), sem("down_ps")
        r_s, stat, agg, veps_s, rst, x_s = sem("r"), sem("stat"), sem("agg"), sem("veps"), sem("rst"), sem("x_new")
        passed = sem("passed")
        block = ctx.enter_context(nc.Block())

        @block.gpsimd
        def _(pool):
            def body(t, p):
                i = t - 1
                if live(i, NG):
                    wait(pool, agg, i * 4 + 4)
                    nc.gpsimd.tensor_tensor(veps[:], mv[:, :, 1], K.eps[:, 0:4], ALU.add).then_inc(veps_s, 1)
                    wait(pool, veps_s, i + 1)
                    nc.gpsimd.tensor_tensor(rstd[:], veps[:], K.half[:, 0:4], ALU.pow).then_inc(rst, 1)
            steps(pool, NG, LAG, HEAD, body)

        @block.vector
        def _(dve):
            def body(t, p):
                for j, (c, w) in enumerate(FCH):
                    if live(t, NG):
                        rows = slice(0, w)
                        b = j % 2
                        n = t * NJ + j
                        wait(dve, g_s, n + 1)
                        wait(dve, u_p, n + 1)
                        wait(dve, d_p, n - (RING - 1))
                        if j < NEC:
                            nc.vector.tensor_tensor(up[:, b], u_ps[b][:], gate[:, b], ALU.mult).then_inc(u_s, 1)
                            wait(dve, u_s, n + 1)
                            wait(dve, c_p, t * NEC + (j + 1))
                            nc.vector.tensor_tensor(hid[:, j % RING], up[:, b], c_ps[b][:], ALU.mult).then_inc(h_s, 1)
                        else:
                            nc.vector.tensor_tensor(hid[rows, j % RING], u_ps[b][rows, :], gate[rows, b],
                                                    ALU.mult).then_inc(u_s, 1)
                    if j == 2 and live(t - 1, NG):
                        i = t - 1
                        wait(dve, d_p, t * NJ)
                        nc.vector.tensor_tensor(r[:], y_ps[:].rearrange("s (n d) -> s n d", n=4),
                                                K.X[:, bass.ds(i * 4, 4), :], ALU.add).then_inc(r_s, 1)
                        wait(dve, r_s, i + 1)
                        for n in range(4):
                            nc.vector.bn_stats(bn[:, n], r[:, n]).then_inc(stat, 1)
                        for n in range(4):
                            wait_apart(dve, stat, i * 4 + (n + 1), passed)
                            nc.vector.bn_aggr(mv[:, n], bn[:, n]).then_inc(agg, 1)
                    if j == 3 and live(t - 1, NG):
                        i = t - 1
                        wait(dve, rst, i + 1)
                        for n in range(4):
                            nc.vector.tensor_scalar(K.X[:, i * 4 + n, :], r[:, n], mv[:, n, 0:1],
                                                    rstd[:, n:n + 1], ALU.subtract, ALU.mult).then_inc(x_s, 1)
            steps(dve, NG, LAG, HEAD, body)

        @block.scalar
        def _(act):
            def body(t, p):
                for j, (c, w) in enumerate(FCH):
                    if live(t, NG):
                        n = t * NJ + j
                        wait(act, g_p, n + 1)
                        wait(act, u_s, n - 1)
                        nc.scalar.activation(gate[0:w, j % 2], g_ps[j % 2][0:w, :], ACT.Silu).then_inc(g_s, 1)
            steps(act, NG, LAG, HEAD, body)

        @block.tensor
        def _(pe):
            pe.wait_ge(K.moe_in, K.n_in[K.moe_in.name])

            def down(t, j):
                w = FCH[j][1]
                if j < NEC:
                    wait(pe, h_s, t * NEC + (j + 1))
                else:
                    wait(pe, u_s, t * NJ + (j + 1))
                if j == 0:
                    wait(pe, r_s, t)
                for n in range(4):
                    last = nc.tensor.matmul(y_ps[:, 128 * n:128 * n + 128], hid[0:w, j % RING, 128 * n:128 * n + 128],
                                            K.wd[0:w, j, :], start=(j == 0 and n == 0), stop=(j == NJ - 1),
                                            skip_group_check=True)
                last.then_inc(d_p, 1)

            def body(t, p):
                for j, (c, w) in enumerate(FCH):
                    if live(t, NG):
                        n = t * NJ + j
                        b = j % 2
                        xT = K.XT[:, bass.ds(t * 512, 512)]
                        wait(pe, g_s, n - 1)
                        nc.tensor.matmul(g_ps[b][0:w, :], K.wg[:, c:c + w], xT, start=True, stop=True).then_inc(g_p, 1)
                        wait(pe, u_s, n - 1)
                        nc.tensor.matmul(u_ps[b][0:w, :], K.wu[:, c:c + w], xT, start=True, stop=True).then_inc(u_p, 1)
                        if j < NEC:
                            wait_apart(pe, h_s, t * NEC + max(j - 1, 0), passed)
                            nc.tensor.matmul(c_ps[b][:], K.expert_ofb[:, c:c + w], K.combT[:, bass.ds(t * 512, 512)],
                                             start=True, stop=True).then_inc(c_p, 1)
                    if j < 2 and live(t - 1, NG):
                        down(t - 1, NJ - 2 + j)
                    if j >= 2 and live(t, NG):
                        down(t, j - 2)
            steps(pe, NG, LAG, HEAD, body)


def recurrence(nc, K):
    G = 2
    NG, W = NB // G, G * S
    LAG, HEAD = 7, 10
    with ExitStack() as ctx:
        def sb(name, shape, dt=F32):
            return ctx.enter_context(nc.sbuf_tensor("d_" + name, shape, dt))

        sem = ctx.enter_context(semaphores(nc, "d_"))

        bn = [sb(f"bn{k}", [S, G, 6]) for k in range(3)]
        mv = [sb(f"mv{k}", [S, 2, G, 2]) for k in range(3)]
        veps = [sb(f"veps{k}", [S, 2, G]) for k in range(3)]
        rstd = [sb(f"rstd{k}", [S, 2, G]) for k in range(3)]
        zn = sb("zn", [S, 2, G, D])
        hT = sb("hT", [D, 2, W])
        ta = sb("ta", [D, 2, W])
        tb = sb("tb", [D, 2, W])
        tc = sb("tc", [D, 2, W])
        a = sb("a", [D, 2, W])
        u = sb("u", [D, 2, W])
        state = sb("state", [D, 2, W])
        yT = sb("yT", [D, 2, W])
        x1 = sb("x1", [S, 2, G, D])
        xsum = sb("xsum", [S, 2, G, D])
        X1 = sb("x1_tok", [S, NB, D])
        zn2 = sb("zn2", [S, 2, G, D])
        h2T = sb("h2T", [D, 2, W])
        hid = sb("hid", [128, 2, 4, W])
        r = sb("r", [S, 2, G, D])
        B = K.bank
        t1_ps, t2_ps = B[0][:, 0:W], B[7][:, 0:W]
        za, zb, zc, ty_ps = B[1][:, 0:W], B[1][:, W:2 * W], B[2][:, 0:W], B[6][:, 0:W]
        m_ps, y_ps = [B[3], B[4]], B[5]

        half_s = sem("half")
        stat, agg, veps_s, rst = ([sem(f"{n}{k}") for k in range(3)] for n in ("stat", "agg", "veps", "rst"))
        zn_s, t1_p, hT_s, z_p, tanh_s = sem("zn"), sem("t1_ps"), sem("hT"), sem("z_ps"), sem("tanh")
        au_s, sc_s, yT_s, ty_p, x1_s, xsum_s = sem("au"), sem("scan"), sem("yT"), sem("ty_ps"), sem("x1"), sem("xsum")
        zn2_s, t2_p, h2T_s, m_p, gelu_s = sem("zn2"), sem("t2_ps"), sem("h2T"), sem("mlp_ps"), sem("gelu")
        y_p, r_s, x_s = sem("y_ps"), sem("r"), sem("x_new")
        passed = sem("passed")
        block = ctx.enter_context(nc.Block())

        @block.gpsimd
        def _(pool):
            def inverse_root(i, b, k):
                wait(pool, agg[k], i * G + G)
                nc.gpsimd.tensor_tensor(veps[k][:, b], mv[k][:, b, :, 1], K.eps[:, 0:G], ALU.add).then_inc(veps_s[k], 1)
                wait(pool, veps_s[k], i + 1)
                nc.gpsimd.tensor_tensor(rstd[k][:, b], veps[k][:, b], K.half[:, 0:G], ALU.pow).then_inc(rst[k], 1)

            def body(t, p):
                i, b = t - 7, (p - 7) % 2
                if live(i, NG):
                    inverse_root(i, b, 2)
                i, b = t - 3, (p - 3) % 2
                if live(i, NG):
                    inverse_root(i, b, 1)
                i, b = t, p
                if live(i, NG):
                    inverse_root(i, b, 0)
                i, b = t - 6, p
                if live(i, NG):
                    wait(pool, r_s, i - 1)
                    wait(pool, x1_s, i * 2 + 2)
                    nc.gpsimd.tensor_tensor(xsum[:, b], X1[:, bass.ds(i * G, G), :], K.X[:, bass.ds(i * G, G), :], ALU.add).then_inc(xsum_s, 1)
            steps(pool, NG, LAG, HEAD, body)

        @block.vector
        def _(dve):
            dve.wait_ge(K.w1_in, K.n_in[K.w1_in.name])
            nc.vector.tensor_scalar(K.habc[:], K.cols1[:, 2:5], 0.5, None, ALU.mult).then_inc(half_s, 1)

            def statistics(src, i, b, k):
                for n in range(G):
                    nc.vector.bn_stats(bn[k][:, n], src(n)).then_inc(stat[k], 1)
                wait(dve, rst[k], i - 1)
                for n in range(G):
                    wait_apart(dve, stat[k], i * G + (n + 1), passed)
                    nc.vector.bn_aggr(mv[k][:, b, n], bn[k][:, n]).then_inc(agg[k], 1)

            def normalise(dst, src, b, k, done):
                for n in range(G):
                    last = nc.vector.tensor_scalar(dst(n), src(n), mv[k][:, b, n, 0:1], rstd[k][:, b, n:n + 1],
                                                   ALU.subtract, ALU.mult)
                last.then_inc(done, 1)

            def body(t, p):
                i, b = t - 7, (p - 7) % 2
                if live(i, NG):
                    wait(dve, y_p, i + 1)
                    wait(dve, xsum_s, i + 1)
                    nc.vector.tensor_tensor(r[:, b], y_ps[:, 0:W].rearrange("s (n d) -> s n d", n=G),
                                            xsum[:, b], ALU.add).then_inc(r_s, 1)
                    wait(dve, r_s, i + 1)
                    statistics(lambda n: r[:, b, n], i, b, 2)
                i, b = t - 3, (p - 3) % 2
                if live(i, NG):
                    wait(dve, ty_p, i + 1)
                    nc.vector.scalar_tensor_tensor(out=x1[:, b], in0=ty_ps.rearrange("s (n d) -> s n d", n=G),
                                                   scalar=-0.25, in1=K.X[:, bass.ds(i * G, G), :],
                                                   op0=ALU.mult, op1=ALU.add).then_inc(x1_s, 1)
                    wait(dve, x1_s, i * 2 + 1)
                    nc.vector.tensor_copy(X1[:, bass.ds(i * G, G), :], x1[:, b]).then_inc(x1_s, 1)
                    statistics(lambda n: x1[:, b, n], i, b, 1)
                i, b = t - 1, (p - 1) % 2
                if live(i, NG):
                    wait(dve, t1_p, i + 1)
                    wait(dve, z_p, (i - 1) * 3)
                    nc.vector.tensor_scalar(hT[:, b], t1_ps, K.cols1[:, 0:1], K.cols1[:, 1:2],
                                            ALU.mult, ALU.add).then_inc(hT_s, 1)
                i, b = t - 4, p
                if live(i, NG):
                    wait(dve, t2_p, i + 1)
                    wait(dve, m_p, (i - 1) * 4)
                    nc.vector.tensor_scalar(h2T[:, b], t2_ps, K.cols1[:, 5:6], K.cols1[:, 6:7],
                                            ALU.mult, ALU.add).then_inc(h2T_s, 1)
                i, b = t, p
                if live(i, NG):
                    statistics(lambda n: K.X[:, i * G + n, :], i, b, 0)
                i, b = t - 3, (p - 3) % 2
                if live(i, NG):
                    wait(dve, rst[1], i + 1)
                    wait(dve, t2_p, i - 1)
                    normalise(lambda n: zn2[:, b, n], lambda n: x1[:, b, n], b, 1, zn2_s)
                i, b = t - 7, (p - 7) % 2
                if live(i, NG):
                    wait(dve, rst[2], i + 1)
                    normalise(lambda n: K.X[:, i * G + n, :], lambda n: r[:, b, n], b, 2, x_s)
                i, b = t, p
                if live(i, NG):
                    wait(dve, rst[0], i + 1)
                    wait(dve, t1_p, i - 1)
                    normalise(lambda n: zn[:, b, n], lambda n: K.X[:, i * G + n, :], b, 0, zn_s)
                i, b = t - 2, p
                if live(i, NG):
                    wait(dve, tanh_s, i * 3 + 3)
                    wait(dve, ty_p, i - 1)
                    nc.vector.tensor_scalar(a[:, b], ta[:, b], 0.5, 0.5, ALU.mult, ALU.add).then_inc(au_s, 1)
                    nc.vector.scalar_tensor_tensor(out=u[:, b], in0=ta[:, b], scalar=1.0, in1=tb[:, b],
                                                   op0=ALU.subtract, op1=ALU.mult).then_inc(au_s, 1)
                    wait(dve, au_s, i * 3 + 1)
                    nc.vector.memset(a[:, b].rearrange("d (n s) -> d n s", n=G)[:, :, 0:1], 0.0).then_inc(au_s, 1)
                    wait(dve, au_s, i * 3 + 3)
                    nc.vector.tensor_tensor_scan(state[:, b], a[:, b], u[:, b], 0.0, ALU.mult, ALU.add).then_inc(sc_s, 1)
                    wait(dve, sc_s, i + 1)
                    nc.vector.scalar_tensor_tensor(out=yT[:, b], in0=tc[:, b], scalar=1.0, in1=state[:, b],
                                                   op0=ALU.add, op1=ALU.mult).then_inc(yT_s, 1)
            steps(dve, NG, LAG, HEAD, body)

        @block.scalar
        def _(act):
            act.wait_ge(K.w1_in, K.n_in[K.w1_in.name])
            act.wait_ge(half_s, 1)

            def body(t, p):
                i, b = t - 5, (p - 5) % 2
                if live(i, NG):
                    wait(act, y_p, i - 1)
                    for c in range(4):
                        wait(act, m_p, i * 4 + (c // 2 * 2 + 2))
                        nc.scalar.activation(hid[:, b, c], m_ps[c // 2][:, W * (c % 2):W * (c % 2) + W], ACT.Gelu,
                                             bias=K.bm1[:, c:c + 1]).then_inc(gelu_s, 1)
                i, b = t - 2, p
                if live(i, NG):
                    wait(act, yT_s, i - 1)
                    for n, (dst, z, scale, bias) in enumerate(((ta, za, 0.5, K.habc[:, 0:1]),
                                                               (tb, zb, 1.0, K.cols1[:, 3:4]),
                                                               (tc, zc, 0.5, K.habc[:, 2:3]))):
                        wait(act, z_p, i * 3 + max(n + 1, 2))
                        nc.scalar.activation(dst[:, b], z, ACT.Tanh, bias=bias, scale=scale).then_inc(tanh_s, 1)
            steps(act, NG, LAG, HEAD, body)

        @block.tensor
        def _(pe):
            pe.wait_ge(K.w1_in, K.n_in[K.w1_in.name])

            def turn(dst, src, done):
                for n in range(G):
                    last = nc.tensor.transpose(dst[:, S * n:S * n + S], src(n), K.ident[:])
                last.then_inc(done, 1)

            def body(t, p):
                i, b = t - 3, (p - 3) % 2
                if live(i, NG):
                    wait(pe, yT_s, i + 1)
                    wait(pe, x1_s, i * 2)
                    turn(ty_ps, lambda n: yT[:, b, S * n:S * n + S], ty_p)
                i, b = t - 1, (p - 1) % 2
                if live(i, NG):
                    wait(pe, zn_s, i + 1)
                    wait(pe, hT_s, i)
                    turn(t1_ps, lambda n: zn[:, b, n], t1_p)
                i, b = t - 4, p
                if live(i, NG):
                    wait(pe, zn2_s, i + 1)
                    wait(pe, h2T_s, i)
                    turn(t2_ps, lambda n: zn2[:, b, n], t2_p)
                i, b = t - 5, (p - 5) % 2
                if live(i, NG):
                    wait(pe, h2T_s, i + 1)
                    for c in range(4):
                        wait(pe, gelu_s, i * 4 + (c // 2 * 2 - 2))
                        nc.tensor.matmul(m_ps[c // 2][:, W * (c % 2):W * (c % 2) + W], K.w1[:, 128 * c:128 * c + 128],
                                         h2T[:, b], start=True, stop=True).then_inc(m_p, 1)
                i, b = t - 2, p
                if live(i, NG):
                    wait(pe, hT_s, i + 1)
                    for n, z in enumerate((za, zb, zc)):
                        wait(pe, tanh_s, i * 3 + (0 if n == 2 else -1))
                        nc.tensor.matmul(z, K.wabc[:, n, :], hT[:, b], start=True, stop=True).then_inc(z_p, 1)
                i, b = t - 6, p
                if live(i, NG):
                    wait(pe, gelu_s, i * 4 + 4)
                    wait(pe, r_s, i)
                    for n in range(G):
                        y = y_ps[:, D * n:D * n + D]
                        for c in range(4):
                            nc.tensor.matmul(y, hid[:, b, c, S * n:S * n + S], K.w2[:, c, :],
                                             start=(c == 0), stop=False)
                        last = nc.tensor.matmul(y, K.onesb[:], K.bm2[:], start=False, stop=True)
                    last.then_inc(y_p, 1)
            steps(pe, NG, LAG, HEAD, body)


def cross_attention(nc, K):
    LAG, HEAD = 7, 10
    C = INNER // 128
    NC = 6
    QK = [(1, K.wq1, 0), (1, K.wq1, 512), (1, K.wkv1, 0), (1, K.wkv1, 512), (0, K.wkv1, 0), (0, K.wkv1, 512)]
    V = [(1, INNER), (1, INNER + 512), (0, INNER), (0, INNER + 512)]
    with ExitStack() as ctx:
        def sb(name, shape, dt=F32):
            return ctx.enter_context(nc.sbuf_tensor("e_" + name, shape, dt))

        sem = ctx.enter_context(semaphores(nc, "e_"))

        bn = sb("bn", [S, 2, 6])
        mv = sb("mv", [S, 2, 2, 2])
        veps = sb("veps", [S, 2, 2])
        rstd = sb("rstd", [S, 2, 2])
        bn2 = sb("bn2", [S, 6])
        mv2 = sb("mv2", [S, 2, 2])
        veps2 = sb("veps2", [S, 2, 1])
        rstd2 = sb("rstd2", [S, 2, 1])
        zn = sb("zn", [S, 2, 2, D])
        nT = sb("nT", [D, 2, 2, S])
        nT2 = sb("nT2", [D, 2, 2, S])
        sq = sb("sq", [S, 2, 512])
        ss = sb("ss", [S, NC, 8])
        ssm = sb("ssm", [S, NC, 8])
        rs = sb("rs", [S, NC, 8])
        qk = sb("qk", [S, 2, NC, 512])
        v = sb("v", [S, 2, 2, INNER])
        qT = sb("qT", [128, 2, C, S])
        kT = sb("kT", [128, 2, C, 2, S])
        neg_max = sb("neg_max", [S, 2, NH1])
        den = sb("den", [S, 2, NH1])
        rden = sb("rden", [S, 2, NH1])
        prob = sb("prob", [S, 2, NH1, 2 * S])
        probT = sb("probT", [S, 4, 4, S])
        on = sb("on", [S, 2, INNER])
        oT = sb("oT", [128, 2, C, S])
        r = sb("r", [S, 2, D])
        mask8 = sb("mask8", [1, NB, S], mybir.dt.uint8)
        mrow = sb("mask_row", [1, NB, S], BF16)
        onesr = sb("ones_row", [1, S], BF16)
        Bk = K.bank
        n_ps, y_ps = Bk[0][:, 0:256], Bk[0][:, 256:384]
        proj, pT_b, tq_b, score, o_b = Bk[1:3], Bk[3], Bk[4], Bk[5:7], Bk[7]

        mask_in, prep, prep2 = sem("mask_in"), sem("prep"), sem("prep2")
        stat, agg, veps_s, rst, zn_s = sem("stat"), sem("agg"), sem("veps"), sem("rst"), sem("zn")
        n_p, nT_s, nT2_s = sem("n_ps"), sem("nT"), sem("nT2")
        qk_p, sq_s, ss_s, ssm_s, rs_s, qk_s = sem("qk_ps"), sem("sq"), sem("ss"), sem("ssm"), sem("rs"), sem("qk")
        v_p, v_s, tq_p, tq_d, tq_a = sem("v_ps"), sem("v"), sem("tq_ps"), sem("tq_dve"), sem("tq_act")
        s_p, mx, ex, rd_s = sem("s_ps"), sem("mx"), sem("ex"), sem("rden")
        pT_p, pT_d, pT_a, pv_p, on_s = sem("pT_ps"), sem("pT_dve"), sem("pT_act"), sem("pv_ps"), sem("on")
        oT_p, oT_a, oT_d, y_p = sem("oT_ps"), sem("oT_act"), sem("oT_dve"), sem("y_ps")
        r_s, stat2, agg2, veps2_s, rst2, x_s = (sem("r"), sem("stat2"), sem("agg2"), sem("veps2"), sem("rst2"),
                                                sem("x_new"))
        passed = sem("passed")
        block = ctx.enter_context(nc.Block())

        def most(i, k):
            return min(i, NB) * k if isinstance(i, int) else i * k

        @block.sync
        def _(sp):
            sp.dma_start(mask8[:], K.A["mask_BxS2_bf1"].rearrange("(o b) s -> o b s", o=1)).then_inc(mask_in, 16)

        @block.gpsimd
        def _(pool):
            nc.gpsimd.memset(onesr[:], 1.0).then_inc(prep2, 1)
            pool.wait_ge(prep2, 1)

            def body(t, p):
                for c in range(NC):
                    i = t - 2
                    if live(i, NB):
                        wait_apart(pool, ss_s, i * NC + (c + 1), passed)
                        nc.gpsimd.tensor_scalar(ssm[:, c], ss[:, c], DH1 * 1e-16, None, ALU.max).then_inc(ssm_s, 1)
                        wait(pool, ssm_s, i * NC + (c + 1))
                        nc.gpsimd.tensor_tensor(rs[:, c], ssm[:, c], K.half[:, 0:8], ALU.pow).then_inc(rs_s, 1)
                    if c == 1:
                        i, b = t, p
                        if live(i, NB):
                            wait(pool, agg, i * 2 + 2)
                            nc.gpsimd.tensor_tensor(veps[:, b], mv[:, b, :, 1], K.eps[:, 0:2], ALU.add
                                                    ).then_inc(veps_s, 1)
                            wait(pool, veps_s, i + 1)
                            nc.gpsimd.tensor_tensor(rstd[:, b], veps[:, b], K.half[:, 0:2], ALU.pow).then_inc(rst, 1)
                    if c == 3:
                        i, b = t - 7, (p - 7) % 2
                        if live(i, NB):
                            wait(pool, agg2, i + 1)
                            nc.gpsimd.tensor_tensor(veps2[:, b], mv2[:, b, 1:2], K.eps[:, 0:1], ALU.add
                                                    ).then_inc(veps2_s, 1)
                            wait(pool, veps2_s, i + 1)
                            nc.gpsimd.tensor_tensor(rstd2[:, b], veps2[:, b], K.half[:, 0:1], ALU.pow
                                                    ).then_inc(rst2, 1)
                i, b = t - 2, p
                if live(i, NB):
                    wait_apart(pool, v_p, (i - 1) * 4, passed)
                    nc.gpsimd.tensor_copy(nT2[:, b], nT[:, b]).then_inc(nT2_s, 1)
            steps(pool, NB, LAG, HEAD, body)

        @block.vector
        def _(dve):
            dve.wait_ge(K.wx1_in, K.n_in[K.wx1_in.name])
            nc.vector.tensor_scalar(K.qg[:], K.colsx[:, 5:6], float(DH1) ** 0.5, None, ALU.mult).then_inc(prep, 1)
            dve.wait_ge(mask_in, 16)
            nc.vector.tensor_scalar(mrow[:], mask8[:], -1.0, 1e30, ALU.add, ALU.mult).then_inc(prep, 1)

            def body(t, p):
                i2, b2, i3, b3 = t - 2, p, t - 3, (p - 3) % 2
                i4, b4, i5, b5, i6, b6 = t - 4, p, t - 5, (p - 5) % 2, t - 6, p
                for s in range(8):
                    if s == 5 and live(i5, NB):
                        norm_heads(i5, b5, 0)
                    if live(i4, NB):
                        wait(dve, s_p, i4 * 8 + (s + 1))
                        h0 = 4 * (s // 2) + s % 2
                        nc.vector.tensor_reduce(neg_max[:, b4, h0:h0 + 3:2],
                                                score[s % 2][:].rearrange("q (h k) -> q h k", h=2),
                                                AX, ALU.max, negate=True).then_inc(mx, 1)
                    if s % 2 == 0 and live(i5, NB):
                        wait(dve, pT_p, i5 * 8 + (s + 1))
                        wait(dve, pv_p, i5 * 8 + (s - 3))
                        nc.vector.tensor_copy(probT[:, s % 4], pT_b[:].rearrange("k (n q) -> k n q", n=4)
                                              ).then_inc(pT_d, 1)
                    if s < NC and live(i2, NB):
                        wait(dve, sq_s, i2 * NC + (s + 1))
                        nc.vector.tensor_reduce(ss[:, s], sq[:, s % 2].rearrange("s (h d) -> s h d", h=8),
                                                AX, ALU.add).then_inc(ss_s, 1)
                    if s == 0:
                        if live(i5, NB):
                            wait(dve, ex, i5 * 8 + 8)
                            wait(dve, on_s, (i5 - 1) * 2)
                            nc.vector.reciprocal(rden[:, b5], den[:, b5]).then_inc(rd_s, 1)
                        if live(i6, NB):
                            norm_heads(i6, b6, 1)
                    c = s - 1
                    if 0 <= c < NC and live(i2, NB):
                        wait(dve, rs_s, i2 * NC + (c + 1))
                        wait(dve, tq_p, (i2 - 1) * NC)
                        nc.vector.tensor_tensor(qk[:, b2, c].rearrange("s (h d) -> s h d", h=8),
                                                proj[c % 2][:].rearrange("s (h d) -> s h d", h=8),
                                                rs[:, c].unsqueeze(2).to_broadcast([S, 8, DH1]), ALU.mult
                                                ).then_inc(qk_s, 1)
                    if c in (0, 2, 4) and live(i3, NB):
                        wait(dve, tq_p, i3 * NC + (c + 1))
                        wait(dve, s_p, (i3 - 1) * 8)
                        dst = qT[:, b3, 0:4] if c == 0 else kT[:, b3, 0:4, 1 if c == 2 else 0]
                        gain = K.colsx[:, 4:5] if c == 0 else K.qg[:]
                        nc.vector.tensor_scalar(dst, tq_b[:].rearrange("p (c s) -> p c s", c=4), gain, None, ALU.mult
                                                ).then_inc(tq_d, 1)
                    if s == 7 and live(i6, NB):
                        wait(dve, oT_p, i6 * 2 + 2)
                        wait(dve, y_p, i6 - 1)
                        nc.vector.tensor_copy(oT[:, b6, 4:8], tq_b[:].rearrange("p (c s) -> p c s", c=4)
                                              ).then_inc(oT_d, 1)
                    i, b = t, p
                    if s == 1 and live(i, NB):
                        nc.vector.bn_stats(bn[:, 0], K.CTX[:, i, :]).then_inc(stat, 1)
                        nc.vector.bn_stats(bn[:, 1], K.X[:, i, :]).then_inc(stat, 1)
                        wait(dve, rst, i - 1)
                        for n in range(2):
                            wait_apart(dve, stat, i * 2 + (n + 1), passed)
                            nc.vector.bn_aggr(mv[:, b, n], bn[:, n]).then_inc(agg, 1)
                    if s == 4 and live(i, NB):
                        wait(dve, rst, i + 1)
                        wait(dve, n_p, i - 1)
                        for n, src in enumerate((K.CTX, K.X)):
                            last = nc.vector.tensor_scalar(zn[:, b, n], src[:, i, :], mv[:, b, n, 0:1],
                                                           rstd[:, b, n:n + 1], ALU.subtract, ALU.mult)
                        last.then_inc(zn_s, 1)
                    i, b = t - 1, (p - 1) % 2
                    if s == 2 and live(i, NB):
                        wait(dve, n_p, i + 1)
                        wait(dve, y_p, i - 5)
                        wait(dve, qk_p, (i - 1) * NC)
                        wait(dve, nT2_s, i - 1)
                        for n in range(2):
                            last = nc.vector.tensor_scalar(nT[:, b, n], n_ps[:, S * n:S * n + S],
                                                           K.colsx[:, 2 * n:2 * n + 1], K.colsx[:, 2 * n + 1:2 * n + 2],
                                                           ALU.mult, ALU.add)
                        last.then_inc(nT_s, 1)
                    i, b = t - 7, (p - 7) % 2
                    if s == 3 and live(i, NB):
                        wait(dve, y_p, i + 1)
                        nc.vector.tensor_tensor(r[:, b], y_ps, K.X[:, i, :], ALU.add).then_inc(r_s, 1)
                        wait(dve, r_s, i + 1)
                        nc.vector.bn_stats(bn2[:], r[:, b]).then_inc(stat2, 1)
                        wait(dve, stat2, i + 1)
                        wait_apart(dve, rst2, i - 1, passed)
                        nc.vector.bn_aggr(mv2[:, b], bn2[:]).then_inc(agg2, 1)
                    if s == 6 and live(i, NB):
                        wait(dve, rst2, i + 1)
                        nc.vector.tensor_scalar(K.X[:, i, :], r[:, b], mv2[:, b, 0:1], rstd2[:, b],
                                                ALU.subtract, ALU.mult).then_inc(x_s, 1)

            def norm_heads(i, b, g):
                wait(dve, pv_p, i * 8 + (4 * g + 4))
                wait(dve, rd_s, i + 1)
                if g == 0:
                    wait(dve, oT_p, (i - 1) * 2)
                nc.vector.tensor_tensor(on[:, b, 512 * g:512 * g + 512].rearrange("q (h d) -> q h d", h=8),
                                        o_b[:].rearrange("q (h d) -> q h d", h=8),
                                        rden[:, b, 8 * g:8 * g + 8].unsqueeze(2).to_broadcast([S, 8, DH1]), ALU.mult
                                        ).then_inc(on_s, 1)
            steps(dve, NB, LAG, HEAD, body)

        @block.scalar
        def _(act):
            act.wait_ge(K.wx1_in, K.n_in[K.wx1_in.name])
            act.wait_ge(prep, 2)

            def body(t, p):
                i2, i3, b3 = t - 2, t - 3, (p - 3) % 2
                i4, b4, i5, i6, b6 = t - 4, p, t - 5, t - 6, p
                for s in range(8):
                    if s < NC and live(i2, NB):
                        wait(act, qk_p, i2 * NC + (s + 1))
                        wait(act, ss_s, i2 * NC + (s - 1))
                        nc.scalar.activation(sq[:, s % 2], proj[s % 2][:], ACT.Square).then_inc(sq_s, 1)
                    if live(i4, NB):
                        wait(act, mx, i4 * 8 + (s + 1))
                        wait(act, pT_p, (i4 - 1) * 8)
                        wait(act, rd_s, i4 - 1)
                        for n in range(2):
                            h = 4 * (s // 2) + s % 2 + 2 * n
                            last = nc.scalar.activation(prob[:, b4, h], score[s % 2][:, 256 * n:256 * n + 256], ACT.Exp,
                                                        bias=neg_max[:, b4, h:h + 1], accum_out=den[:, b4, h:h + 1])
                        last.then_inc(ex, 1)
                    if s % 2 == 1 and live(i5, NB):
                        wait(act, pT_p, i5 * 8 + (s + 1))
                        wait(act, pv_p, i5 * 8 + (s - 3))
                        nc.scalar.copy(probT[:, s % 4], pT_b[:].rearrange("k (n q) -> k n q", n=4)).then_inc(pT_a, 1)
                    if s == 0 and live(i6, NB):
                        wait(act, oT_p, i6 * 2 + 1)
                        wait(act, y_p, i6 - 1)
                        nc.scalar.copy(oT[:, b6, 0:4], tq_b[:].rearrange("p (c s) -> p c s", c=4)).then_inc(oT_a, 1)
                    c = s - 1
                    if c in (1, 3, 5) and live(i3, NB):
                        wait(act, tq_p, i3 * NC + (c + 1))
                        wait(act, s_p, (i3 - 1) * 8)
                        dst = qT[:, b3, 4:8] if c == 1 else kT[:, b3, 4:8, 1 if c == 3 else 0]
                        gain = K.colsx[:, 4:5] if c == 1 else K.qg[:]
                        nc.scalar.activation(dst, tq_b[:].rearrange("p (c s) -> p c s", c=4), ACT.Copy, scale=gain
                                             ).then_inc(tq_a, 1)
                    if s in (6, 7) and live(i4, NB):
                        for n in (2 * (s - 6), 2 * (s - 6) + 1):
                            wait(act, v_p, i4 * 4 + (n + 1))
                            wait(act, pv_p, (i4 - 1) * 8)
                            src, c0 = V[n][0], V[n][1] - INNER
                            nc.scalar.copy(v[:, b4, src, c0:c0 + 512], proj[n % 2][:]).then_inc(v_s, 1)
            steps(act, NB, LAG, HEAD, body)

        @block.tensor
        def _(pe):
            pe.wait_ge(K.wx1_in, K.n_in[K.wx1_in.name])
            pe.wait_ge(prep, 2)
            pe.wait_ge(prep2, 1)

            def values(i, b, s):
                if s % 2:
                    wait(pe, pT_a, i * 4 + (s + 1) // 2)
                else:
                    wait(pe, pT_d, i * 4 + s // 2 + 1)
                if s % 4 == 0:
                    wait(pe, on_s, i * 2 + s // 4)
                if s == 0:
                    wait(pe, v_s, i * 4 + 4)
                for n in range(2):
                    h = 2 * s + n
                    o = o_b[:, 64 * (h % 8):64 * (h % 8) + 64]
                    for src in range(2):
                        last = nc.tensor.matmul(o, probT[:, s % 4, 2 * n + src], v[:, b, src, 64 * h:64 * h + 64],
                                                start=(src == 0), stop=(src == 1))
                last.then_inc(pv_p, 1)

            def body(t, p):
                i2, b2, i3, b3 = t - 2, p, t - 3, (p - 3) % 2
                i4, b4, i5, b5, i6, b6 = t - 4, p, t - 5, (p - 5) % 2, t - 6, p
                for s in range(8):
                    if s % 2 == 0 and live(i4, NB):
                        if s == 0:
                            wait(pe, tq_d, i4 * 3 + 3)
                            wait(pe, tq_a, i4 * 3 + 3)
                        wait_apart(pe, ex, i4 * 8 + s, passed)
                        for odd in range(2):
                            nc.tensor.matmul(score[odd][:].rearrange("q (h n k) -> q h n k", h=2, n=2)[:, :, 0],
                                             onesr[:], mrow[:, i4, :].unsqueeze(1).to_broadcast([1, 2, S]),
                                             start=True, stop=False, skip_group_check=True)
                        for n in range(2):
                            for odd in range(2):
                                rows = slice(64 * odd, 64 * odd + 64)
                                last = nc.tensor.matmul(score[odd][:, 256 * n:256 * n + 256], qT[rows, b4, s + n],
                                                        kT[rows, b4, s + n], start=False, stop=True,
                                                        skip_group_check=True)
                                if n:
                                    last.then_inc(s_p, 1)
                    if live(i5, NB):
                        wait(pe, ex, i5 * 8 + 8)
                        if s % 2:
                            wait(pe, pT_d, i5 * 4 + (s + 1) // 2)
                        else:
                            wait(pe, pT_a, i5 * 4 + s // 2)
                        for n in range(4):
                            last = nc.tensor.transpose(pT_b[:, 128 * n:128 * n + 128],
                                                       prob[:, b5, 2 * s + n // 2, S * (n % 2):S * (n % 2) + S], K.ident[:])
                        last.then_inc(pT_p, 1)
                        if s > 0:
                            values(i5, b5, s - 1)
                    if s < NC and live(i2, NB):
                        if s == 0:
                            wait(pe, nT_s, i2 + 1)
                        if s < 2:
                            wait(pe, v_s, most(i4, 4) + (s - 1))
                        wait(pe, qk_s, i2 * NC + (s - 1))
                        src, w, c0 = QK[s]
                        nc.tensor.matmul(proj[s % 2][:], nT[:, b2, src], w[:, c0:c0 + 512], start=True, stop=True
                                         ).then_inc(qk_p, 1)
                    f = s - 1
                    if 0 <= f < NC and live(i3, NB):
                        wait(pe, qk_s, i3 * NC + (f + 1))
                        if f == 0:
                            wait(pe, tq_a, i3 * 3)
                            wait(pe, oT_a, i6 + 1)
                            wait(pe, oT_d, i6)
                        elif f % 2:
                            wait(pe, tq_d, i3 * 3 + (f + 1) // 2)
                        else:
                            wait(pe, tq_a, i3 * 3 + f // 2)
                        for n in range(4):
                            last = nc.tensor.transpose(tq_b[:, 128 * n:128 * n + 128],
                                                       qk[:, b3, f, 128 * n:128 * n + 128], K.ident[:])
                        last.then_inc(tq_p, 1)
                    if s in (0, 7) and live(i6, NB):
                        g = s // 7
                        wait(pe, on_s, i6 * 2 + (g + 1))
                        if g == 0:
                            wait(pe, oT_d, i6)
                            wait(pe, tq_a, most(i3, 3))
                        else:
                            wait(pe, oT_a, i6 + 1)
                            wait(pe, tq_a, most(i3 + 1, 3))
                        for n in range(4):
                            c = 4 * g + n
                            last = nc.tensor.transpose(tq_b[:, 128 * n:128 * n + 128], on[:, b6, 128 * c:128 * c + 128],
                                                       K.ident[:])
                        last.then_inc(oT_p, 1)
                    if s in (6, 7) and live(i4, NB):
                        for n in (2 * (s - 6), 2 * (s - 6) + 1):
                            if n == 0:
                                wait(pe, nT2_s, i4 + 1)
                            if n < 2:
                                wait(pe, qk_s, most(i2, NC) + (5 + n) if live(i2, NB) else NB * NC)
                            wait(pe, v_s, i4 * 4 + (n - 1))
                            src, c0 = V[n]
                            nc.tensor.matmul(proj[n % 2][:], nT2[:, b4, src], K.wkv1[:, c0:c0 + 512],
                                             start=True, stop=True).then_inc(v_p, 1)
                if live(i5, NB):
                    values(i5, b5, 7)
                if live(t, NB):
                    wait(pe, zn_s, t + 1)
                    wait(pe, nT_s, t)
                    wait(pe, r_s, t - 6)
                    for n in range(2):
                        last = nc.tensor.transpose(n_ps[:, S * n:S * n + S], zn[:, p, n], K.ident[:])
                    last.then_inc(n_p, 1)
                if live(i6, NB):
                    wait(pe, oT_a, i6 + 1)
                    wait(pe, oT_d, i6 + 1)
                    wait(pe, r_s, i6)
                    for c in range(C):
                        nc.tensor.matmul(y_ps, oT[:, b6, c], K.wout[:, c, :], start=(c == 0), stop=False)
                    nc.tensor.matmul(y_ps, K.onesb[:], K.bout[:], start=False, stop=True).then_inc(y_p, 1)
            steps(pe, NB, LAG, HEAD, body)


def bit_ffn(nc, K, out):
    LAG, HEAD = 6, 8
    C = FB // 128
    with ExitStack() as ctx:
        def sb(name, shape, dt=F32):
            return ctx.enter_context(nc.sbuf_tensor("f_" + name, shape, dt))

        sem = ctx.enter_context(semaphores(nc, "f_"))

        wsum = sb("wsum", [128, 3])
        wmean = sb("wmean", [128, 3])
        winv = sb("winv", [128, 3])
        dequant = sb("dequant", [128, 3])
        wq = sb("wq", [128, 3, FB])
        wqb = sb("wqb", [128, 3, FB], BF16)
        wT = sb("wT", [128, 3, FB], BF16)
        am = sb("am", [S, 2, 1])
        amc = sb("amc", [S, 2, 1])
        inv = sb("inv", [S, 2, 1])
        inv127 = sb("inv127", [S, 2, 1])
        dg = sb("dg", [S, 2, 3])
        xm = sb("xm", [S, 2, D])
        xq = sb("xq", [S, 2, D], BF16)
        xqT = sb("xqT", [D, 2, S], BF16)
        gate = sb("gate", [S, 2, FB])
        h = sb("h", [S, 2, FB])
        am2 = sb("am2", [S, 2, 1])
        amc2 = sb("amc2", [S, 2, 1])
        inv2 = sb("inv2", [S, 2, 1])
        inv1272 = sb("inv1272", [S, 2, 1])
        dh = sb("dh", [S, 2, 1])
        hm = sb("hm", [S, 2, FB])
        hq = sb("hq", [S, 2, FB], BF16)
        hqT = sb("hqT", [128, 2, FB], BF16)
        r = sb("r", [S, 2, D])
        bn = sb("bn", [S, 6])
        mv = sb("mv", [S, 2, 2])
        veps = sb("veps", [S, 2, 1])
        rstd = sb("rstd", [S, 2, 1])
        xo = sb("xo", [S, 2, D])
        Bk = K.bank
        xT_b, g_b, u_b, hT_b, y_b, w_b = Bk[0][:].bitcast(BF16), Bk[1], Bk[2], Bk[3][:].bitcast(BF16), Bk[4], Bk[5]

        wr, wsum_s, wtot_p, wp, wT_p, wT_s = sem("wr"), sem("wsum"), sem("wtot"), sem("wp"), sem("wT_ps"), sem("wT")
        am_s, amc_s, inv_s, i127_s, dg_s = sem("am"), sem("amc"), sem("inv"), sem("i127"), sem("dg")
        xm_s, xq_s, xT_p, xT_s, gu_p, g_s, h_s = (sem("xm"), sem("xq"), sem("xT_ps"), sem("xT"), sem("gu_ps"),
                                                  sem("gate"), sem("h"))
        am2_s, amc2_s, inv2_s, i1272_s, dh_s = sem("am2"), sem("amc2"), sem("inv2"), sem("i1272"), sem("dh")
        hm_s, hq_s, hT_p, hT_s, y_p, r_s = sem("hm"), sem("hq"), sem("hT_ps"), sem("hT"), sem("y_ps"), sem("r")
        stat, agg, veps_s, rst, x_s, out_s = (sem("stat"), sem("agg"), sem("veps"), sem("rst"), sem("x_new"),
                                              sem("stored"))
        passed = sem("passed")
        block = ctx.enter_context(nc.Block())

        @block.gpsimd
        def _(pool):
            def body(t, p):
                i, b = t - 5, (p - 5) % 2
                if live(i, NB):
                    wait(pool, agg, i + 1)
                    nc.gpsimd.tensor_tensor(veps[:, b], mv[:, b, 1:2], K.eps[:, 0:1], ALU.add).then_inc(veps_s, 1)
                    wait(pool, veps_s, i + 1)
                    nc.gpsimd.tensor_tensor(rstd[:, b], veps[:, b], K.half[:, 0:1], ALU.pow).then_inc(rst, 1)
            steps(pool, NB, LAG, HEAD, body)

        @block.sync
        def _(sp):
            def body(t, p):
                i, b = t - 6, p
                if live(i, NB):
                    wait_apart(sp, x_s, i + 1, passed)
                    wait(sp, out_s, i * 16)
                    sp.dma_start(out[i], xo[:, b]).then_inc(out_s, 16)
            steps(sp, NB, LAG, HEAD, body)
            sp.wait_ge(out_s, NB * 16)

        @block.vector
        def _(dve):
            dve.wait_ge(K.wb_in, K.n_in[K.wb_in.name])
            done = [0]

            def then(ins):
                done[0] += 1
                ins.then_inc(wp, 1)
                dve.wait_ge(wp, done[0])

            nc.vector.tensor_reduce(wsum[:], K.wbraw[:], AX, ALU.add, apply_absolute_value=True).then_inc(wsum_s, 1)
            dve.wait_ge(wtot_p, 1)
            then(nc.vector.tensor_scalar(wmean[:], w_b[:, 0:3], 1.0 / (D * FB), 1e-5, ALU.mult, ALU.max))
            then(nc.vector.reciprocal(winv[:], wmean[:]))
            then(nc.vector.tensor_scalar(dequant[:], wmean[:], 1.0 / 127.0, None, ALU.mult))
            for n in range(3):
                then(nc.vector.tensor_scalar(wq[:, n], K.wbraw[:, n], winv[:, n:n + 1], MAGIC, ALU.mult, ALU.add))
                then(nc.vector.tensor_scalar(wq[:, n], wq[:, n], -MAGIC, 1.0, ALU.add, ALU.min))
                nc.vector.tensor_scalar(wqb[:, n], wq[:, n], -1.0, None, ALU.max).then_inc(wr, 1)
                dve.wait_ge(wT_p, n + 1)
                nc.vector.tensor_copy(wT[:, n], hT_b[:, 0:FB]).then_inc(wT_s, 1)

            def body(t, p):
                i5, b5 = t - 5, (p - 5) % 2
                if live(i5, NB):
                    wait(dve, y_p, i5 + 1)
                    nc.vector.scalar_tensor_tensor(out=r[:, b5], in0=y_b[:, 0:D], scalar=dh[:, b5], in1=K.X[:, i5, :],
                                                   op0=ALU.mult, op1=ALU.add).then_inc(r_s, 1)
                i, b = t, p
                if live(i, NB):
                    wait(dve, am_s, i)
                    nc.vector.tensor_reduce(am[:, b], K.X[:, i, :], AX, ALU.max, apply_absolute_value=True
                                            ).then_inc(am_s, 1)
                if live(i5, NB):
                    wait(dve, r_s, i5 + 1)
                    nc.vector.bn_stats(bn[:], r[:, b5]).then_inc(stat, 1)
                if live(i, NB):
                    wait(dve, am_s, i + 1)
                    nc.vector.tensor_scalar(amc[:, b], am[:, b], 1e-5, None, ALU.max).then_inc(amc_s, 1)
                if live(i5, NB):
                    wait(dve, stat, i5 + 1)
                    wait_apart(dve, rst, i5 - 1, passed)
                    nc.vector.bn_aggr(mv[:, b5], bn[:]).then_inc(agg, 1)
                if live(i, NB):
                    wait(dve, amc_s, i + 1)
                    nc.vector.reciprocal(inv[:, b], amc[:, b]).then_inc(inv_s, 1)
                i3, b3 = t - 3, (p - 3) % 2
                if live(i3, NB):
                    wait(dve, h_s, i3 + 1)
                    nc.vector.tensor_reduce(am2[:, b3], h[:, b3], AX, ALU.max, apply_absolute_value=True
                                            ).then_inc(am2_s, 1)
                if live(i, NB):
                    wait(dve, inv_s, i + 1)
                    nc.vector.tensor_scalar(inv127[:, b], inv[:, b], 127.0, None, ALU.mult).then_inc(i127_s, 1)
                if live(i3, NB):
                    wait(dve, am2_s, i3 + 1)
                    nc.vector.tensor_scalar(amc2[:, b3], am2[:, b3], 1e-5, None, ALU.max).then_inc(amc2_s, 1)
                if live(i, NB):
                    wait(dve, i127_s, i + 1)
                    nc.vector.tensor_scalar(xm[:, b], K.X[:, i, :], inv127[:, b], MAGIC, ALU.mult, ALU.add
                                            ).then_inc(xm_s, 1)
                if live(i3, NB):
                    wait(dve, amc2_s, i3 + 1)
                    nc.vector.reciprocal(inv2[:, b3], amc2[:, b3]).then_inc(inv2_s, 1)
                i2, b2 = t - 2, p
                if live(i2, NB):
                    wait(dve, g_s, i2 + 1)
                    wait(dve, gu_p, i2 * 2 + 2)
                    wait(dve, hm_s, i2 - 1)
                    nc.vector.scalar_tensor_tensor(out=h[:, b2], in0=u_b[:], scalar=dg[:, b2, 1:2], in1=gate[:, b2],
                                                   op0=ALU.mult, op1=ALU.mult).then_inc(h_s, 1)
                if live(i, NB):
                    wait(dve, g_s, i - 1)
                    wait(dve, h_s, i - 1)
                    nc.vector.tensor_scalar(dg[:, b], dequant[:], amc[:, b], None, ALU.mult).then_inc(dg_s, 1)
                if live(i3, NB):
                    wait(dve, inv2_s, i3 + 1)
                    wait(dve, hm_s, i3 - 1)
                    nc.vector.tensor_scalar(inv1272[:, b3], inv2[:, b3], 127.0, None, ALU.mult).then_inc(i1272_s, 1)
                if live(i, NB):
                    wait(dve, xm_s, i + 1)
                    wait(dve, xT_p, i - 1)
                    nc.vector.tensor_scalar(xq[:, b], xm[:, b], -MAGIC, None, ALU.add).then_inc(xq_s, 1)
                if live(i3, NB):
                    nc.vector.tensor_scalar(dh[:, b3], amc2[:, b3], dequant[:, 2:3], None, ALU.mult).then_inc(dh_s, 1)
                    wait(dve, hm_s, i3 + 1)
                    wait(dve, hT_p, i3 - 1)
                    nc.vector.tensor_scalar(hq[:, b3], hm[:, b3], -MAGIC, None, ALU.add).then_inc(hq_s, 1)
                if live(i5, NB):
                    wait(dve, rst, i5 + 1)
                    wait(dve, out_s, (i5 - 1) * 16)
                    nc.vector.tensor_scalar(xo[:, b5], r[:, b5], mv[:, b5, 0:1], rstd[:, b5],
                                            ALU.subtract, ALU.mult).then_inc(x_s, 1)
            steps(dve, NB, LAG, HEAD, body)

        @block.scalar
        def _(act):
            def body(t, p):
                i, b = t - 1, (p - 1) % 2
                if live(i, NB):
                    wait(act, xT_p, i + 1)
                    wait(act, gu_p, (i - 1) * 2)
                    nc.scalar.copy(xqT[:, b], xT_b[:, 0:S]).then_inc(xT_s, 1)
                i, b = t - 2, p
                if live(i, NB):
                    wait(act, gu_p, i * 2 + 1)
                    wait(act, dg_s, i + 1)
                    wait(act, h_s, i - 1)
                    nc.scalar.activation(gate[:, b], g_b[:], ACT.Silu, scale=dg[:, b, 0:1]).then_inc(g_s, 1)
                i, b = t - 3, (p - 3) % 2
                if live(i, NB):
                    wait(act, i1272_s, i + 1)
                    wait(act, hq_s, i - 1)
                    nc.scalar.activation(hm[:, b], h[:, b], ACT.Identity, bias=K.magic[:], scale=inv1272[:, b]
                                         ).then_inc(hm_s, 1)
                i, b = t - 4, p
                if live(i, NB):
                    wait(act, hT_p, i + 1)
                    wait(act, y_p, i - 1)
                    nc.scalar.copy(hqT[:, b], hT_b[:, 0:FB]).then_inc(hT_s, 1)
            steps(act, NB, LAG, HEAD, body)

        @block.tensor
        def _(pe):
            pe.wait_ge(wsum_s, 1)
            nc.tensor.matmul(w_b[:, 0:3], K.ones[:], wsum[:], start=True, stop=True).then_inc(wtot_p, 1)
            for n in range(3):
                pe.wait_ge(wr, n + 1)
                wait(pe, wT_s, n)
                for c in range(C):
                    last = nc.tensor.transpose(hT_b[:, 128 * c:128 * c + 128], wqb[:, n, 128 * c:128 * c + 128],
                                               K.identb[:])
                last.then_inc(wT_p, 1)
            pe.wait_ge(wT_s, 3)

            def body(t, p):
                i, b = t - 4, p
                if live(i, NB):
                    wait(pe, hq_s, i + 1)
                    wait(pe, hT_s, i)
                    for c in range(C):
                        last = nc.tensor.transpose(hT_b[:, 128 * c:128 * c + 128], hq[:, b, 128 * c:128 * c + 128],
                                                   K.identb[:])
                    last.then_inc(hT_p, 1)
                i, b = t - 2, p
                if live(i, NB):
                    wait(pe, xT_s, i + 1)
                    wait(pe, g_s, i)
                    nc.tensor.matmul(g_b[:], xqT[:, b], wT[:, 0], start=True, stop=True).then_inc(gu_p, 1)
                    wait(pe, h_s, i)
                    nc.tensor.matmul(u_b[:], xqT[:, b], wT[:, 1], start=True, stop=True).then_inc(gu_p, 1)
                i, b = t - 1, (p - 1) % 2
                if live(i, NB):
                    wait(pe, xq_s, i + 1)
                    wait(pe, xT_s, i)
                    nc.tensor.transpose(xT_b[:, 0:S], xq[:, b], K.identb[:]).then_inc(xT_p, 1)
                i, b = t - 4, p
                if live(i, NB):
                    wait(pe, hT_s, i + 1)
                    wait(pe, r_s, i)
                    for c in range(C):
                        last = nc.tensor.matmul(y_b[:, 0:D], hqT[:, b, 128 * c:128 * c + 128],
                                                wT[:, 2, 128 * c:128 * c + 128], start=(c == 0), stop=(c == C - 1))
                    last.then_inc(y_p, 1)
            steps(pe, NB, LAG, HEAD, body)


STAGES = ("self_attention", "context_mix", "experts", "recurrence", "cross_attention", "bit_ffn")


def decoder(nc, A, out, last="bit_ffn"):
    K = Shared()
    K.A = A
    with ExitStack() as ctx:
        K.bank = [ctx.enter_context(nc.psum_tensor(f"bank{i}", [128, 512], F32)) for i in range(8)]
        K.magic = ctx.enter_context(nc.sbuf_tensor("magic", [128, 1], F32))
        with ExitStack() as early:
            load_stage(nc, K, ctx, early)
            self_attention(nc, K)
            if last == "self_attention":
                return store(nc, K, out)
            with ExitStack() as moe:
                K.XT = moe.enter_context(nc.sbuf_tensor("xT_all", [D, NB * S], F32))
                K.combT = moe.enter_context(nc.sbuf_tensor("combT", [3 * NE, NB * S], BF16))
                K.logits = moe.enter_context(nc.sbuf_tensor("logits", [S, NB, NE], F32))
                context_mix(nc, K)
                if last == "context_mix":
                    return store(nc, K, out)
                route(nc, K)
                experts(nc, K)
            if last == "experts":
                return store(nc, K, out)
            recurrence(nc, K)
            if last == "recurrence":
                return store(nc, K, out)
        cross_attention(nc, K)
        if last == "cross_attention":
            return store(nc, K, out)
        bit_ffn(nc, K, out)


def store(nc, K, out):
    with nc.semaphore("stored") as s, nc.Block() as block:
        @block.sync
        def _(sp):
            sp.dma_start(out.rearrange("b s d -> s b d"), K.X[:]).then_inc(s, 16)
            sp.wait_ge(s, 16)
            for q in (K.x_in, K.ctx_in, K.consts_in, K.w0_in, K.wx_in, K.moe_in, K.w1_in, K.wx1_in, K.wb_in):
                sp.wait_ge(q, K.n_in[q.name])


def constants():
    p = np.arange(128)
    head_mask = ((p[:, None] % 64) // DH0 == np.arange(8)[None, :]).astype(np.float32)
    ones_mask = np.broadcast_to(np.arange(32)[None, :] // DH0 == np.arange(4)[:, None], (128, 4, 32)).astype(np.float32)
    e = np.arange(NE)
    tie = (e[None, :] < e[:, None]).astype(np.float32).reshape(-1)
    expert_of = (np.arange(NE * FE)[None, :] // FE == np.arange(3 * NE)[:, None] % NE).astype(np.float32)
    return {"c_ident": np.eye(128, dtype=np.float32), "c_head_mask": head_mask, "c_ones_mask": ones_mask,
            "c_tie": tie, "c_expert_of": expert_of}


def kernel(**inputs):
    import numpy as _np
    import concourse.bacc as _bacc
    from concourse import mybir as _mybir
    from concourse.bass_utils import run_bass_kernel_spmd as _run

    nc = _bacc.Bacc("TRN2", target_bir_lowering=False, num_devices=1)
    arrays, aps = {}, {}
    for name, value in {**inputs, **constants()}.items():
        a = _np.ascontiguousarray(value)
        if a.dtype == _np.bool_:
            a = a.view(_np.uint8)
        arrays[f"in_{name}"] = a
        aps[name] = nc.dram_tensor(f"in_{name}", a.shape, _mybir.dt.from_np(a.dtype), kind="ExternalInput").ap()
    out = nc.dram_tensor("out_dram", (NB, S, D), F32, kind="ExternalOutput").ap()
    decoder(nc, aps, out)
    r = _run(nc, [arrays], core_ids=[0])
    return r.results[0]["out_dram"]
```

```python
from contextlib import ExitStack, contextmanager

import numpy as np

import concourse.bass as bass
from concourse import mybir

F32 = mybir.dt.float32
BF16 = mybir.dt.bfloat16
F32R = mybir.dt.float32r
ALU = mybir.AluOpType
ACT = mybir.ActivationFunctionType
AX = mybir.AxisListType.X

NB, S, D = 32, 128, 128
NH0, DH0 = 16, 8
NE, FE, FS = 8, 176, 352
FF = NE * FE + FS
FCH = [(c, min(128, FF - c)) for c in range(0, FF, 128)]
FFP = 128 * len(FCH)
NEC = NE * FE // 128
HM = 4 * D
NH1, DH1 = 16, 64
INNER = NH1 * DH1
FB = 512
EPS = 1e-5
MAGIC = 1.5 * 2.0 ** 23


class Shared:
    pass


@contextmanager
def semaphores(nc, prefix):
    taken = []

    def sem(name):
        taken.append(nc.alloc_semaphore(name=prefix + name))
        return taken[-1]

    yield sem
    nc.clear_and_free_semaphores(taken)
    nc.all_engine_barrier()


def wait(eng, sem, count):
    if isinstance(count, int) and count <= 0:
        return
    eng.wait_ge(sem, count)


def wait_apart(eng, sem, count, passed):
    wait(eng, sem, count)
    if not isinstance(count, int):
        eng.sem_inc(passed, 1)


def live(i, n):
    return not isinstance(i, int) or 0 <= i < n


def steps(eng, n, lag, head, body, unroll=2):
    assert (n - head) % unroll == 0
    for t in range(head):
        body(t, t % unroll)
    with eng.Fori(0, (n - head) // unroll) as r:
        for u in range(unroll):
            body(r * unroll + (head + u), (head + u) % unroll)
    for t in range(n, n + lag):
        body(t, t % unroll)


def load_one(K, sp, s, dst, src):
    K.n_in[s.name] = K.n_in.get(s.name, 0) + 16
    sp.dma_start(dst, src).then_inc(s, 16)


def load_later(K, sp):
    A = K.A

    def load(s, dst, src):
        load_one(K, sp, s, dst, src)

    cs = A["ctx_1024"].rearrange("b s d -> s b d")
    load(K.route_in, K.tie[:], A["c_tie"].partition_broadcast(128))
    load(K.route_in, K.expert_of[:], A["c_expert_of"])
    for b in range(0, NB, 8):
        load(K.ctx_in, K.CTX[:, b:b + 8, :], cs[:, b:b + 8, :])
    load(K.wx_in, K.wx[:], A["L0_xattn_W"])
    load(K.wx_in, K.bx[:], A["L0_xattn_b"].partition_broadcast(128))
    load(K.wx_in, K.gate_raw[:], A["L0_ffn_gate_w"])
    for dst, w, shared in ((K.wg, "w_gate", "sw_gate"), (K.wu, "w_up", "sw_up")):
        load(K.moe_in, dst[:, 0:NE * FE].rearrange("d (e f) -> d e f", e=NE),
             A["L0_ffn_" + w].rearrange("e d f -> d e f"))
        load(K.moe_in, dst[:, NE * FE:FF], A["L0_ffn_" + shared])
    down = A["L0_ffn_w_down"].rearrange("e f d -> (e f) d")
    load(K.moe_in, K.wd[:, 0:NEC, :], down.rearrange("(c p) d -> p c d", p=128))
    for n, (c, w) in enumerate(FCH):
        if n >= NEC:
            load(K.moe_in, K.wd[0:w, n, :], A["L0_ffn_sw_down"][c - NE * FE:c - NE * FE + w, :])
    for n, w in enumerate(("Wa", "Wb", "Wc")):
        load(K.w1_in, K.wabc[:, n, :], A["L1_attn_" + w])
    for n, w in enumerate(("g1", "b1", "ba", "bb", "bc", "g2", "b2")):
        load(K.w1_in, K.cols1[:, n:n + 1], A["L1_attn_" + w].rearrange("(p o) -> p o", o=1))
    load(K.w1_in, K.w1[:], A["L1_attn_W1"])
    for n in range(HM // 128):
        load(K.w1_in, K.bm1[:, n:n + 1], A["L1_attn_bm1"][128 * n:128 * n + 128].rearrange("(p o) -> p o", o=1))
    load(K.w1_in, K.w2[:], A["L1_attn_W2"].rearrange("(c p) d -> p c d", p=128))
    load(K.w1_in, K.bm2[:], A["L1_attn_bm2"].partition_broadcast(128))
    for n, w in enumerate(("ln_x_g", "ln_x_b", "ln_l_g", "ln_l_b")):
        load(K.wx1_in, K.colsx[:, n:n + 1], A["L1_xattn_" + w].rearrange("(p o) -> p o", o=1))
    for n, w in enumerate(("qn_g", "kn_g")):
        for half in range(2):
            load(K.wx1_in, K.colsx[64 * half:64 * half + 64, 4 + n:5 + n],
                 A["L1_xattn_" + w].rearrange("(p o) -> p o", o=1))
    load(K.wx1_in, K.wq1[:], A["L1_xattn_Wq"])
    load(K.wx1_in, K.wkv1[:], A["L1_xattn_Wkv"])
    load(K.wx1_in, K.wout[:], A["L1_xattn_Wout"].rearrange("(c p) d -> p c d", p=128))
    load(K.wx1_in, K.bout[:], A["L1_xattn_bout"].partition_broadcast(128))
    for n, w in enumerate(("w_gate", "w_up")):
        load(K.wb_in, K.wbraw[:, n, :].rearrange("p (c i) -> p c i", c=4),
             A["L1_ffn_" + w].rearrange("(c p) i -> p c i", p=128))
    load(K.wb_in, K.wbraw[:, 2, :], A["L1_ffn_w_down"])


def load_stage(nc, K, ctx, early):
    def sb(name, shape, dt=F32):
        return ctx.enter_context(nc.sbuf_tensor(name, shape, dt))

    def sb_early(name, shape, dt=F32):
        return early.enter_context(nc.sbuf_tensor(name, shape, dt))

    def sem(name):
        return ctx.enter_context(nc.semaphore(name))

    K.X = sb("x_tok", [S, NB, D])
    K.CTX = sb("ctx_tok", [S, NB, D])
    K.ident = sb("ident", [128, 128])
    K.identb = sb("identb", [128, 128], BF16)
    K.ones = sb("ones", [128, 128])
    K.half = sb("minus_half", [128, 64])
    K.eps = sb("eps", [128, 64])
    K.colsx = sb("colsx", [128, 6])
    K.qg = sb("qg_scaled", [128, 1])
    K.wq1 = sb("wq1", [D, INNER])
    K.wkv1 = sb("wkv1", [D, 2 * INNER])
    K.wout = sb("wout", [128, INNER // 128, D])
    K.bout = sb("bout", [128, D])
    K.wbraw = sb("wb_raw", [128, 3, FB])
    K.head_mask = sb_early("head_mask", [128, 8])
    K.ones_mask = sb_early("ones_mask", [128, 4, 32])
    K.tie = sb_early("tie", [128, 64])
    K.expert_of = sb_early("expert_of", [24, NE * FE])
    K.expert_ofb = sb_early("expert_ofb", [24, NE * FE], BF16)
    K.w_qkv = sb_early("w_qkv", [D, 3 * D])
    K.w_proj = sb_early("w_proj", [D, D])
    K.cols0 = sb_early("cols0", [128, 4])
    K.bv = sb_early("bv_rows", [128, D])
    K.bproj = sb_early("bproj_rows", [128, D])
    K.wx = sb_early("wx_raw", [D, 2 * D])
    K.wxT = sb_early("wxT", [128, 2 * D])
    K.bx = sb_early("bx", [128, D])
    K.gate_raw = sb_early("gate_raw", [NE, D])
    K.gateT = sb_early("gateT", [D, NE])
    K.wg = sb_early("wg", [D, FF])
    K.wu = sb_early("wu", [D, FF])
    K.wd = sb_early("wd", [128, len(FCH), D])
    K.wabc = sb_early("wabc", [D, 3, D])
    K.cols1 = sb_early("cols1", [128, 7])
    K.habc = sb_early("half_ba_bc", [128, 3])
    K.w1 = sb_early("w1", [D, HM])
    K.bm1 = sb_early("bm1", [128, HM // 128])
    K.w2 = sb_early("w2", [128, HM // 128, D])
    K.bm2 = sb_early("bm2", [128, D])
    K.x0_in, K.x_in, K.ctx_in, K.route_in = sem("x0_in"), sem("x_in"), sem("ctx_in"), sem("route_in")
    K.consts_in, K.w0_in, K.wx_in = sem("consts_in"), sem("w0_in"), sem("wx_in")
    K.moe_in, K.w1_in, K.wx1_in, K.wb_in = sem("moe_in"), sem("w1_in"), sem("wx1_in"), sem("wb_in")
    K.n_in = {}
    K.FIRST = 4
    K.small_ready = sem("small_ready")
    A = K.A

    with nc.Block() as block:
        @block.sync
        def _(sp):
            def load(s, dst, src):
                load_one(K, sp, s, dst, src)

            xs = A["x"].rearrange("b s d -> s b d")
            load(K.x0_in, K.X[:, 0:K.FIRST, :], xs[:, 0:K.FIRST, :])
            load(K.consts_in, K.ident[:], A["c_ident"])
            load(K.consts_in, K.head_mask[:], A["c_head_mask"])
            load(K.consts_in, K.ones_mask[:], A["c_ones_mask"])
            load(K.w0_in, K.w_qkv[:], A["L0_attn_W_qkv"])
            load(K.w0_in, K.cols0[:, 0:1], A["L0_attn_ln_w"].rearrange("(p o) -> p o", o=1))
            load(K.w0_in, K.cols0[:, 1:2], A["L0_attn_ln_b"].rearrange("(p o) -> p o", o=1))
            for n in range(2):
                load(K.w0_in, K.cols0[:, 2 + n:3 + n], A["L0_attn_b_qkv"][D * n:D * n + D].rearrange("(p o) -> p o", o=1))
            load(K.w0_in, K.bv[:], A["L0_attn_b_qkv"][2 * D:3 * D].partition_broadcast(128))
            load(K.w0_in, K.w_proj[:], A["L0_attn_W_proj"])
            load(K.w0_in, K.bproj[:], A["L0_attn_b_proj"].partition_broadcast(128))
            for b in range(K.FIRST, NB, 7):
                load(K.x_in, K.X[:, b:b + 7, :], xs[:, b:b + 7, :])

        @block.gpsimd
        def _(pool):
            nc.gpsimd.memset(K.ones[:], 1.0)
            nc.gpsimd.memset(K.half[:], -0.5)
            nc.gpsimd.memset(K.eps[:], EPS)
            nc.gpsimd.memset(K.magic[:], MAGIC)

        @block.vector
        def _(dve):
            dve.wait_ge(K.consts_in, 16 * 3)
            nc.vector.tensor_copy(K.identb[:], K.ident[:])


def self_attention(nc, K):
    LAG, HEAD = 6, 8
    with ExitStack() as ctx:
        def sb(name, shape, dt=F32):
            return ctx.enter_context(nc.sbuf_tensor("a_" + name, shape, dt))

        sem = ctx.enter_context(semaphores(nc, "a_"))

        bn = sb("bn", [S, 6])
        mv = sb("mv", [S, 2, 2])
        rstd = sb("rstd", [S, 2, 1])
        veps = sb("veps", [S, 2, 1])
        bn2 = sb("bn2", [S, 6])
        mv2 = sb("mv2", [S, 2, 2])
        rstd2 = sb("rstd2", [S, 2, 1])
        veps2 = sb("veps2", [S, 2, 1])
        zn = sb("zn", [S, 2, D])
        znT = sb("znT", [D, 2, S])
        q = sb("q", [D, 2, S])
        kmask = sb("kmask", [D, 2, 8, S])
        vmask = sb("vmask", [S, 4, NH0, 32])
        neg_max = sb("neg_max", [S, 2, NH0])
        prob = sb("prob", [S, 2, NH0, S])
        probT = sb("probT", [S, NH0, S])
        recip = sb("recip", [D, S])
        att = sb("att", [D, 2, S])
        resid = sb("resid", [S, 2, D])
        r = sb("r", [S, 2, D])
        score, ring, tq, out = K.bank[0:4], K.bank[4:6], K.bank[6], K.bank[7]

        stat, agg, rst, veps_s, zn_s = sem("stat"), sem("agg"), sem("rst"), sem("veps"), sem("zn")
        znT_ps, znT_s, qkv_ps = sem("znT_ps"), sem("znT"), sem("qkv_ps")
        q_s, k_s, v_s, vzero = sem("q"), sem("k"), sem("v"), sem("vzero")
        s_ps, mx, ex = sem("s_ps"), sem("mx"), sem("ex")
        pT_ps, pT_s = sem("pT_ps"), [sem(f"pT{j}") for j in range(4)]
        pv_ps, rc, att_s, y_ps = sem("pv_ps"), sem("rc"), sem("att"), sem("y_ps")
        res0, res_s, r_s = sem("res0"), sem("res"), sem("r")
        stat2, agg2, veps2_s, rst2, x_s = sem("stat2"), sem("agg2"), sem("veps2"), sem("rst2"), sem("x_new")

        passed = sem("passed")
        block = ctx.enter_context(nc.Block())

        @block.sync
        def _(sp):
            load_later(K, sp)

        @block.gpsimd
        def _(pool):
            nc.gpsimd.memset(vmask[:], 0.0).then_inc(vzero, 1)
            pool.wait_ge(K.w0_in, K.n_in[K.w0_in.name])
            pool.wait_ge(K.x0_in, K.n_in[K.x0_in.name])

            def body(t, p):
                i, b = t, p % 2
                if live(i, NB):
                    wait(pool, agg, i + 1)
                    nc.gpsimd.tensor_tensor(veps[:, b], mv[:, b, 1:2], K.eps[:, 0:1], ALU.add).then_inc(veps_s, 1)
                    wait(pool, veps_s, i + 1)
                    nc.gpsimd.tensor_tensor(rstd[:, b], veps[:, b], K.half[:, 0:1], ALU.pow).then_inc(rst, 1)
                i, b = t - 5, (p - 5) % 2
                if isinstance(i, int) and i == 0:
                    pool.wait_ge(K.x_in, K.n_in[K.x_in.name])
                if live(i, NB):
                    wait(pool, r_s, i - 1)
                    nc.gpsimd.tensor_tensor(resid[:, b], K.X[:, i, :], K.X[:, i, :], ALU.add).then_inc(res0, 1)
                    wait(pool, res0, i + 1)
                    nc.gpsimd.tensor_tensor(resid[:, b], resid[:, b], K.bproj[:], ALU.add).then_inc(res_s, 1)
                i, b = t - 6, (p - 6) % 2
                if live(i, NB):
                    wait(pool, agg2, i + 1)
                    nc.gpsimd.tensor_tensor(veps2[:, b], mv2[:, b, 1:2], K.eps[:, 0:1], ALU.add).then_inc(veps2_s, 1)
                    wait(pool, veps2_s, i + 1)
                    nc.gpsimd.tensor_tensor(rstd2[:, b], veps2[:, b], K.half[:, 0:1], ALU.pow).then_inc(rst2, 1)
            steps(pool, NB, LAG, HEAD, body, 4)

        @block.vector
        def _(dve):
            dve.wait_ge(K.consts_in, K.n_in[K.consts_in.name])
            dve.wait_ge(K.w0_in, K.n_in[K.w0_in.name])
            dve.wait_ge(K.x0_in, K.n_in[K.x0_in.name])
            dve.wait_ge(vzero, 1)

            def row_max(i, b, j):
                wait(dve, s_ps, i * 4 + (j + 1))
                nc.vector.tensor_reduce(neg_max[:, b, 4 * j:4 * j + 4],
                                        score[j][:].rearrange("q (h k) -> q h k", h=4),
                                        AX, ALU.max, negate=True).then_inc(mx, 1)

            def turn(i, j):
                wait(dve, pT_ps, i * 4 + (j + 1))
                wait(dve, pv_ps, i)
                nc.vector.tensor_copy(probT[:, 4 * j:4 * j + 4, :],
                                      ring[j % 2][:].rearrange("k (h q) -> k h q", h=4)).then_inc(pT_s[j], 1)

            def body(t, p):
                if isinstance(t, int) and t == K.FIRST:
                    dve.wait_ge(K.x_in, K.n_in[K.x_in.name])
                i, b = t - 6, (p - 6) % 2
                if live(i, NB):
                    wait(dve, y_ps, i + 1)
                    wait(dve, res_s, i + 1)
                    nc.vector.tensor_tensor(r[:, b], out[:, 256:384], resid[:, b], ALU.add).then_inc(r_s, 1)
                    wait(dve, r_s, i + 1)
                    nc.vector.bn_stats(bn2[:], r[:, b]).then_inc(stat2, 1)
                    wait(dve, stat2, i + 1)
                    wait_apart(dve, rst2, i - 1, passed)
                    nc.vector.bn_aggr(mv2[:, b], bn2[:]).then_inc(agg2, 1)
                i, b = t, p % 2
                if live(i, NB):
                    nc.vector.bn_stats(bn[:], K.X[:, i, :]).then_inc(stat, 1)
                    wait(dve, stat, i + 1)
                    wait_apart(dve, rst, i - 1, passed)
                    nc.vector.bn_aggr(mv[:, b], bn[:]).then_inc(agg, 1)
                i3, b3 = t - 3, (p - 3) % 2
                i4 = t - 4
                if live(i3, NB):
                    row_max(i3, b3, 0)
                    row_max(i3, b3, 1)
                i, b = t - 1, (p - 1) % 2
                if live(i, NB):
                    wait(dve, znT_ps, i + 1)
                    wait(dve, qkv_ps, i)
                    nc.vector.tensor_scalar(znT[:, b], tq[:, 0:128], K.cols0[:, 0:1], K.cols0[:, 1:2],
                                            ALU.mult, ALU.add).then_inc(znT_s, 1)
                i, b = t - 2, (p - 2) % 2
                if live(i, NB):
                    wait(dve, qkv_ps, i + 1)
                    wait(dve, s_ps, (i - 1) * 4)
                    nc.vector.scalar_tensor_tensor(
                        out=kmask[:, b], in0=tq[:, 256:384].unsqueeze(1).to_broadcast([D, 8, S]),
                        scalar=K.cols0[:, 3:4], in1=K.head_mask[:].unsqueeze(2).to_broadcast([D, 8, S]),
                        op0=ALU.add, op1=ALU.mult).then_inc(k_s, 1)
                    nc.vector.tensor_scalar(q[:, b], tq[:, 128:256], K.cols0[:, 2:3], float(DH0) ** -0.5,
                                            ALU.add, ALU.mult).then_inc(q_s, 1)
                    wait(dve, pv_ps, i - 3)
                    nc.vector.tensor_tensor(
                        head_columns(vmask, (p - 2) % 4),
                        tq[:, 384:512].rearrange("k (j g c) -> k j g c", j=4, g=4),
                        K.bv[:].rearrange("k (j g c) -> k j g c", j=4, g=4), ALU.add).then_inc(v_s, 1)
                i, b = t - 5, (p - 5) % 2
                if live(i, NB):
                    wait(dve, pv_ps, i + 1)
                    nc.vector.reciprocal(recip[:], out[:, 128:256]).then_inc(rc, 1)
                    wait(dve, rc, i + 1)
                    wait(dve, y_ps, i - 1)
                    nc.vector.tensor_tensor(att[:, b], out[:, 0:128], recip[:], ALU.mult).then_inc(att_s, 1)
                if live(i4, NB):
                    turn(i4, 0)
                i, b = t, p % 2
                if live(i, NB):
                    wait(dve, rst, i + 1)
                    wait(dve, znT_ps, i - 1)
                    nc.vector.tensor_scalar(zn[:, b], K.X[:, i, :], mv[:, b, 0:1], rstd[:, b],
                                            ALU.subtract, ALU.mult).then_inc(zn_s, 1)
                if live(i3, NB):
                    row_max(i3, b3, 2)
                i, b = t - 6, (p - 6) % 2
                if live(i, NB):
                    wait(dve, rst2, i + 1)
                    nc.vector.tensor_scalar(K.X[:, i, :], r[:, b], mv2[:, b, 0:1], rstd2[:, b],
                                            ALU.subtract, ALU.mult).then_inc(x_s, 1)
                if live(i3, NB):
                    row_max(i3, b3, 3)
            steps(dve, NB, LAG, HEAD, body, 4)

        @block.scalar
        def _(act):
            def exps(i, b, j):
                wait(act, mx, i * 4 + (j + 1))
                wait(act, pT_ps, (i - 1) * 4)
                for h in range(4 * j, 4 * j + 4):
                    last = nc.scalar.activation(prob[:, b, h, :], score[j][:, 128 * (h % 4):128 * (h % 4) + 128],
                                                ACT.Exp, bias=neg_max[:, b, h:h + 1])
                last.then_inc(ex, 1)

            def turn(i, j):
                wait(act, pT_ps, i * 4 + (j + 1))
                wait(act, pv_ps, i)
                nc.scalar.copy(probT[:, 4 * j:4 * j + 4, :],
                               ring[j % 2][:].rearrange("k (h q) -> k h q", h=4)).then_inc(pT_s[j], 1)

            def body(t, p):
                i3, b3, i4 = t - 3, (p - 3) % 2, t - 4
                if live(i3, NB):
                    exps(i3, b3, 0)
                    exps(i3, b3, 1)
                if live(i4, NB):
                    turn(i4, 1)
                if live(i3, NB):
                    exps(i3, b3, 2)
                if live(i4, NB):
                    turn(i4, 2)
                    turn(i4, 3)
                if live(i3, NB):
                    exps(i3, b3, 3)
            steps(act, NB, LAG, HEAD, body, 4)

        @block.tensor
        def _(pe):
            pe.wait_ge(K.consts_in, K.n_in[K.consts_in.name])
            pe.wait_ge(K.w0_in, K.n_in[K.w0_in.name])

            def scores(i, b, j):
                rows = slice(64 * (j // 2), 64 * (j // 2) + 64)
                wait(pe, q_s, i + 1)
                wait(pe, k_s, i + 1)
                wait(pe, ex, (i - 1) * 4 + (j + 1))
                nc.tensor.matmul(score[j][:], q[rows, b, :], kmask[rows, b, 4 * (j % 2):4 * (j % 2) + 4, :],
                                 start=True, stop=True).then_inc(s_ps, 1)

            def turn(i, b, j):
                wait(pe, ex, i * 4 + (j + 1))
                wait(pe, pT_s[(j + 2) % 4], i + (j >= 2))
                for h in range(4 * j, 4 * j + 4):
                    last = nc.tensor.transpose(ring[j % 2][:, 128 * (h % 4):128 * (h % 4) + 128],
                                               prob[:, b, h, :], K.ident[:])
                last.then_inc(pT_ps, 1)

            def body(t, p):
                i3, b3, i4, b4 = t - 3, (p - 3) % 2, t - 4, (p - 4) % 2
                i5 = t - 5
                if live(i3, NB):
                    scores(i3, b3, 0)
                    scores(i3, b3, 1)
                i, b = t - 1, (p - 1) % 2
                if live(i, NB):
                    wait(pe, zn_s, i + 1)
                    wait(pe, znT_s, i)
                    wait(pe, v_s, i - 1)
                    nc.tensor.transpose(tq[:, 0:128], zn[:, b], K.ident[:]).then_inc(znT_ps, 1)
                i, b = t - 2, (p - 2) % 2
                if live(i, NB):
                    wait(pe, znT_s, i + 1)
                    wait(pe, v_s, i)
                    nc.tensor.matmul(tq[:, 128:256], K.w_qkv[:, 0:128], znT[:, b], start=True, stop=True)
                    nc.tensor.matmul(tq[:, 256:384], K.w_qkv[:, 128:256], znT[:, b], start=True, stop=True)
                    nc.tensor.matmul(tq[:, 384:512], znT[:, b], K.w_qkv[:, 256:384],
                                     start=True, stop=True).then_inc(qkv_ps, 1)
                if live(i5, NB):
                    wait(pe, v_s, i5 + 1)
                    for j in range(4):
                        wait(pe, pT_s[j], i5 + 1)
                    wait(pe, att_s, i5)
                    wait(pe, r_s, i5)
                    for cols, weights in ((slice(0, 128), 0), (slice(128, 256), 1)):
                        for g in range(4):
                            for j in range(4):
                                h = 4 * j + g
                                lhsT = K.ones_mask[:, g, :] if weights else vmask[:, (p - 5) % 4, h, :]
                                last = nc.tensor.matmul(out[32 * j:32 * j + 32, cols], lhsT, probT[:, h, :],
                                                        start=(g == 0), stop=(g == 3))
                    last.then_inc(pv_ps, 1)
                if live(i4, NB):
                    turn(i4, b4, 0)
                if live(i3, NB):
                    scores(i3, b3, 2)
                if live(i4, NB):
                    turn(i4, b4, 1)
                if live(i3, NB):
                    scores(i3, b3, 3)
                if live(i4, NB):
                    turn(i4, b4, 2)
                    turn(i4, b4, 3)
                i, b = t - 5, (p - 5) % 2
                if live(i, NB):
                    wait(pe, att_s, i + 1)
                    wait(pe, r_s, i)
                    nc.tensor.matmul(out[:, 256:384], att[:, b], K.w_proj[:], start=True, stop=True).then_inc(y_ps, 1)
            steps(pe, NB, LAG, HEAD, body, 4)


def head_columns(vmask, b):
    v = vmask[:, b, :, :].rearrange("k (j g) (e c) -> k j g e c", j=4, e=4)
    return diagonal(v)


def diagonal(v):
    (ps, pn), (js, jn), (gs, gn), (es, en), (cs, cn) = [tuple(x) for x in v.ap]
    return bass.AP(tensor=v.tensor, offset=v.offset, ap=[[ps, pn], [js, jn], [gs + es, gn], [cs, cn]])


def context_mix(nc, K):
    NG = NB // 4
    LAG, HEAD = 3, 4
    with ExitStack() as ctx:
        def sb(name, shape, dt=F32):
            return ctx.enter_context(nc.sbuf_tensor("b_" + name, shape, dt))

        sem = ctx.enter_context(semaphores(nc, "b_"))

        mean_row = sb("mean_col", [D, NB])
        xT = sb("xT", [D, 2, 512])
        mT = sb("mT", [D, 2, 512])
        x2T = sb("x2T", [D, 2, 512])
        xs = sb("xs", [S, 2, 4, D])
        x2s = sb("x2s", [S, 2, 4, D])
        r = sb("r", [S, 2, 4, D])
        bn = sb("bn", [S, 4, 6])
        mv = sb("mv", [S, 2, 4, 2])
        veps = sb("veps", [S, 2, 4])
        rstd = sb("rstd", [S, 2, 4])
        turn_ps, y_ps, turn2_ps, logit_ps, prep = K.bank[0], K.bank[1], K.bank[2], K.bank[3], K.bank[4]
        mean_ps = K.bank[5]

        prep_ps, prep_s, mean_p, mean_s, inv_s = sem("prep_ps"), sem("prep"), sem("mean_ps"), sem("mean"), sem("inv")
        xs_s, X_s = sem("xs"), sem("X")
        xT_ps, xT_s, mT_s, y_s, r_s = sem("xT_ps"), sem("xT"), sem("mT"), sem("y_ps"), sem("r")
        stat, agg, veps_s, rst, x_s = sem("stat"), sem("agg"), sem("veps"), sem("rst"), sem("x_new")
        x2T_ps, x2T_s, XT_s, lg_ps, lg_s = sem("x2T_ps"), sem("x2T"), sem("XT"), sem("lg_ps"), sem("lg")
        inv = sb("inv", [S, 2])
        passed = sem("passed")
        part_s, XL_s, xb_s = sem("part"), sem("XL"), sem("x_bias")
        xb = sb("x_bias", [S, 2, 4, D])
        block = ctx.enter_context(nc.Block())

        @block.gpsimd
        def _(pool):
            nc.gpsimd.memset(inv[:], 1.0 / S).then_inc(inv_s, 1)
            pool.wait_ge(K.wx_in, K.n_in[K.wx_in.name])
            for parts in (K.wgp, K.wup):
                for part in parts:
                    nc.gpsimd.memset(part[:, FF:FFP].bitcast(F32), 0.0)

            def body(t, p):
                i, b = t - 1, (p - 1) % 2
                if live(i, NG):
                    wait(pool, r_s, i - 1)
                    nc.gpsimd.tensor_tensor(xb[:, b], K.X[:, bass.ds(i * 4, 4), :],
                                            K.bx[:].unsqueeze(1).to_broadcast([S, 4, D]), ALU.add).then_inc(xb_s, 1)
                i, b = t - 2, p
                if live(i, NG):
                    wait(pool, agg, i * 4 + 4)
                    nc.gpsimd.tensor_tensor(veps[:, b], mv[:, b, :, 1], K.eps[:, 0:4], ALU.add).then_inc(veps_s, 1)
                    wait(pool, veps_s, i + 1)
                    nc.gpsimd.tensor_tensor(rstd[:, b], veps[:, b], K.half[:, 0:4], ALU.pow).then_inc(rst, 1)
            steps(pool, NG, LAG, HEAD, body)

        @block.vector
        def _(dve):
            dve.wait_ge(K.route_in, K.n_in[K.route_in.name])
            nc.vector.tensor_copy(K.expert_ofb[:], K.expert_of[:])
            dve.wait_ge(K.moe_in, K.n_in[K.moe_in.name])
            for n, (w, parts) in enumerate(((K.wg, K.wgp), (K.wu, K.wup))):
                dve.wait_ge(part_s, n + 1)
                nc.vector.tensor_tensor(parts[1][:, 0:FF], w[:], parts[0][:, 0:FF].bitcast(F32), ALU.subtract)
            dve.wait_ge(prep_ps, 1)
            nc.vector.tensor_copy(K.wxT[:], prep[:, 0:256]).then_inc(prep_s, 1)
            nc.vector.tensor_copy(K.gateT[:], prep[:, 256:264]).then_inc(prep_s, 1)
            dve.wait_ge(mean_p, 1)
            nc.vector.tensor_copy(mean_row[:], mean_ps[:, 0:NB]).then_inc(mean_s, 1)
            dve.wait_ge(mean_s, 1)

            def body(t, p):
                i, b = t, p
                if live(i, NG):
                    wait(dve, xT_ps, i - 1)
                    nc.vector.tensor_copy(xs[:, b], K.X[:, bass.ds(i * 4, 4), :]).then_inc(xs_s, 1)
                i, b = t - 2, p
                if live(i, NG):
                    wait(dve, y_s, i + 1)
                    wait(dve, xb_s, i + 1)
                    nc.vector.tensor_tensor(r[:, b], y_ps[:].rearrange("s (n d) -> s n d", n=4),
                                            xb[:, b], ALU.add).then_inc(r_s, 1)
                    wait(dve, r_s, i + 1)
                    for n in range(4):
                        nc.vector.bn_stats(bn[:, n], r[:, b, n]).then_inc(stat, 1)
                    for n in range(4):
                        wait_apart(dve, stat, i * 4 + (n + 1), passed)
                        nc.vector.bn_aggr(mv[:, b, n], bn[:, n]).then_inc(agg, 1)
                i, b = t, p
                if live(i, NG):
                    wait(dve, y_s, i - 1)
                    nc.vector.tensor_copy(mT[:, b].rearrange("d (n s) -> d n s", n=4),
                                          mean_row[:, bass.ds(i * 4, 4)].unsqueeze(2).to_broadcast([D, 4, S])
                                          ).then_inc(mT_s, 1)
                i, b = t - 2, p
                if live(i, NG):
                    wait(dve, rst, i + 1)
                    wait(dve, x2T_ps, i - 1)
                    for n in range(4):
                        nc.vector.tensor_scalar(x2s[:, b, n], r[:, b, n], mv[:, b, n, 0:1],
                                                rstd[:, b, n:n + 1], ALU.subtract, ALU.mult).then_inc(x_s, 1)
                if live(i, NG):
                    wait_apart(dve, x_s, i * 4 + 4, passed)
                    nc.vector.tensor_copy(K.X[:, bass.ds(i * 4, 4), :], x2s[:, b]).then_inc(X_s, 1)
                i = t - 3
                if live(i, NG):
                    c = bass.ds(i * 512, 512)
                    wait(dve, XT_s, i + 1)
                    nc.vector.tensor_tensor(K.XT[1][:, c], turn2_ps[:], K.XT[0][:, c].bitcast(F32), ALU.subtract
                                            ).then_inc(XL_s, 1)
                if live(i, NG):
                    wait(dve, lg_ps, i + 1)
                    nc.vector.tensor_copy(K.logits[:, bass.ds(i * 4, 4), :],
                                          logit_ps[:, 0:32].rearrange("s (n e) -> s n e", n=4)).then_inc(lg_s, 1)
            steps(dve, NG, LAG, HEAD, body)

        @block.scalar
        def _(act):
            act.wait_ge(K.moe_in, K.n_in[K.moe_in.name])
            for w, parts in ((K.wg, K.wgp), (K.wu, K.wup)):
                nc.scalar.copy(parts[0][:, 0:FF], w[:]).then_inc(part_s, 1)

            def body(t, p):
                i, b = t - 3, (p - 3) % 2
                if live(i, NG):
                    wait(act, x2T_ps, i + 1)
                    wait(act, lg_ps, i)
                    nc.scalar.copy(x2T[:, b], turn2_ps[:]).then_inc(x2T_s, 1)
                    nc.scalar.copy(K.XT[0][:, bass.ds(i * 512, 512)], turn2_ps[:]).then_inc(XT_s, 1)
                i, b = t, p
                if live(i, NG):
                    wait(act, xT_ps, i + 1)
                    wait(act, y_s, i - 1)
                    nc.scalar.copy(xT[:, b], turn_ps[:]).then_inc(xT_s, 1)
            steps(act, NG, LAG, HEAD, body)

        @block.tensor
        def _(pe):
            pe.wait_ge(K.wx_in, K.n_in[K.wx_in.name])
            pe.wait_ge(K.ctx_in, K.n_in[K.ctx_in.name])
            for n in range(2):
                nc.tensor.transpose(prep[:, 128 * n:128 * n + 128], K.wx[:, 128 * n:128 * n + 128], K.ident[:])
            nc.tensor.transpose(prep[:, 256:264], K.gate_raw[:], K.ident[0:8, 0:8]).then_inc(prep_ps, 1)
            pe.wait_ge(inv_s, 1)
            for n in range(NB):
                last = nc.tensor.matmul(mean_ps[:, n:n + 1], K.CTX[:, n, :], inv[:, 0:1], start=True, stop=True)
            last.then_inc(mean_p, 1)
            pe.wait_ge(prep_s, 2)

            def body(t, p):
                i, b = t - 3, (p - 3) % 2
                if live(i, NG):
                    wait(pe, x_s, i * 4 + 4)
                    wait(pe, XL_s, i)
                    for n in range(4):
                        last = nc.tensor.transpose(turn2_ps[:, 128 * n:128 * n + 128], x2s[:, b, n],
                                                   K.ident[:])
                    last.then_inc(x2T_ps, 1)
                i, b = t - 1, (p - 1) % 2
                if live(i, NG):
                    wait(pe, xT_s, i + 1)
                    wait(pe, mT_s, i + 1)
                    wait(pe, r_s, i)
                    for n in range(4):
                        c = slice(128 * n, 128 * n + 128)
                        nc.tensor.matmul(y_ps[:, c], xT[:, b, c], K.wxT[:, 0:128], start=True, stop=False)
                        last = nc.tensor.matmul(y_ps[:, c], mT[:, b, c], K.wxT[:, 128:256], start=False, stop=True)
                    last.then_inc(y_s, 1)
                i = t
                if live(i, NG):
                    wait(pe, xs_s, i + 1)
                    wait(pe, xT_s, i)
                    for n in range(4):
                        last = nc.tensor.transpose(turn_ps[:, 128 * n:128 * n + 128], xs[:, p, n], K.ident[:])
                    last.then_inc(xT_ps, 1)
                i, b = t - 3, (p - 3) % 2
                if live(i, NG):
                    wait(pe, x2T_s, i + 1)
                    wait(pe, lg_s, i)
                    for n in range(4):
                        last = nc.tensor.matmul(logit_ps[:, 8 * n:8 * n + 8], x2T[:, b, 128 * n:128 * n + 128],
                                                K.gateT[:], start=True, stop=True)
                    last.then_inc(lg_ps, 1)
            steps(pe, NG, LAG, HEAD, body)


def route(nc, K):
    NG = NB // 4
    with ExitStack() as ctx:
        def sb(name, shape, dt=F32):
            return ctx.enter_context(nc.sbuf_tensor("r_" + name, shape, dt))

        sem = ctx.enter_context(semaphores(nc, "r_"))

        top = sb("top", [S, NB])
        e = sb("e", [S, NB, NE])
        total = sb("total", [S, NB])
        prob = sb("prob", [S, NB, NE])
        gt = sb("gt", [S, NB, NE, NE])
        eq = sb("eq", [S, NB, NE, NE])
        rank = sb("rank", [S, NB, NE])
        comb = sb("comb", [S, NB, NE])
        rest = sb("rest", [S, NB, NE])
        parts = sb("parts", [S, NB, 3 * NE], BF16)
        sum2 = sb("sum2", [S, NB])
        c4 = sb("c4", [S, 2, 4, 3 * NE], BF16)
        bank = [K.bank[i][:].bitcast(BF16) for i in range(2)]
        dv, ex, parts_s, c4_s, cT_ps, cT_s = sem("dve"), sem("exp"), sem("parts"), sem("c4"), sem("cT_ps"), sem("cT")
        block = ctx.enter_context(nc.Block())

        def over(x, n=NE):
            return x.unsqueeze(2).to_broadcast([S, NB, n])

        @block.vector
        def _(dve):
            done = [0]

            def then(ins):
                done[0] += 1
                ins.then_inc(dv, 1)
                dve.wait_ge(dv, done[0])

            then(nc.vector.tensor_reduce(top[:], K.logits[:], AX, ALU.max))
            nc.vector.tensor_tensor(e[:], K.logits[:], over(top[:]), ALU.subtract).then_inc(parts_s, 1)
            dve.wait_ge(ex, 1)
            then(nc.vector.tensor_reduce(total[:], prob[:], AX, ALU.add))
            then(nc.vector.reciprocal(sum2[:], total[:]))
            then(nc.vector.tensor_tensor(e[:], prob[:], over(sum2[:]), ALU.mult))
            for b in range(0, NB, 8):
                j_ = e[:, b:b + 8].unsqueeze(2).to_broadcast([S, 8, NE, NE])
                e_ = e[:, b:b + 8].unsqueeze(3).to_broadcast([S, 8, NE, NE])
                nc.vector.tensor_tensor(gt[:, b:b + 8], j_, e_, ALU.is_gt)
                then(nc.vector.tensor_tensor(eq[:, b:b + 8], j_, e_, ALU.is_equal))
            then(nc.vector.tensor_tensor(eq[:].rearrange("s b e j -> s b (e j)"),
                                         eq[:].rearrange("s b e j -> s b (e j)"),
                                         K.tie[:].unsqueeze(1).to_broadcast([S, NB, NE * NE]), ALU.mult))
            then(nc.vector.tensor_tensor(gt[:], gt[:], eq[:], ALU.add))
            then(nc.vector.tensor_reduce(rank[:], gt[:], AX, ALU.add))
            then(nc.vector.scalar_tensor_tensor(out=comb[:], in0=rank[:], scalar=1.5, in1=e[:],
                                                op0=ALU.is_lt, op1=ALU.mult))
            then(nc.vector.tensor_reduce(total[:], comb[:], AX, ALU.add))
            then(nc.vector.tensor_scalar(total[:], total[:], 1e-20, None, ALU.add))
            then(nc.vector.reciprocal(sum2[:], total[:]))
            then(nc.vector.scalar_tensor_tensor(out=comb[:], in0=comb[:], scalar=2.5, in1=over(sum2[:]),
                                                op0=ALU.mult, op1=ALU.mult))
            then(nc.vector.tensor_copy(parts[:, :, 0:NE], comb[:]))
            then(nc.vector.tensor_tensor(rest[:], comb[:], parts[:, :, 0:NE], ALU.subtract))
            then(nc.vector.tensor_copy(parts[:, :, NE:2 * NE], rest[:]))
            then(nc.vector.tensor_tensor(rest[:], rest[:], parts[:, :, NE:2 * NE], ALU.subtract))
            nc.vector.tensor_copy(parts[:, :, 2 * NE:], rest[:]).then_inc(parts_s, 1)
            dve.wait_ge(parts_s, 2)

            def body(t, p):
                i, b = t, p
                if live(i, NG):
                    wait(dve, cT_ps, i - 1)
                    nc.vector.tensor_copy(c4[:, b], parts[:, bass.ds(i * 4, 4), :]).then_inc(c4_s, 1)
            steps(dve, NG, 1, 4, body)

        @block.scalar
        def _(act):
            act.wait_ge(parts_s, 1)
            nc.scalar.activation(prob[:], e[:], ACT.Exp).then_inc(ex, 1)

            def body(t, p):
                i, b = t - 1, (p - 1) % 2
                if live(i, NG):
                    wait(act, cT_ps, i + 1)
                    nc.scalar.copy(K.combT[:, bass.ds(i * 512, 512)], bank[b][0:24, 0:512]).then_inc(cT_s, 1)
            steps(act, NG, 1, 4, body)

        @block.tensor
        def _(pe):
            def body(t, p):
                i, b = t, p
                if live(i, NG):
                    wait(pe, c4_s, i + 1)
                    wait(pe, cT_s, i - 1)
                    for n in range(4):
                        last = nc.tensor.transpose(bank[b][0:24, 128 * n:128 * n + 128], c4[:, b, n], K.identb[:])
                    last.then_inc(cT_ps, 1)
            steps(pe, NG, 1, 4, body)


def experts(nc, K):
    NG = NB // 4
    NJ = len(FCH)
    LAG, HEAD = 1, 2
    with ExitStack() as ctx:
        def sb(name, shape, dt=F32):
            return ctx.enter_context(nc.sbuf_tensor("c_" + name, shape, dt))

        sem = ctx.enter_context(semaphores(nc, "c_"))

        gate = sb("gate", [128, 2, 512])
        up = sb("up", [128, 2, 512])
        RING = 7
        hid = sb("hid", [128, RING, 512])
        r = sb("r", [S, 4, D])
        bn = sb("bn", [S, 4, 6])
        mv = sb("mv", [S, 4, 2])
        veps = sb("veps", [S, 4])
        rstd = sb("rstd", [S, 4])
        g_ps, u_ps, c_ps, y_ps = K.bank[0:2], K.bank[2:4], K.bank[4:6], K.bank[6]
        g_p, u_p, c_p = sem("gate_ps"), sem("up_ps"), sem("comb_ps")
        g_s, u_s, h_s, d_p = sem("gate"), sem("up"), sem("hid"), sem("down_ps")
        r_s, stat, agg, veps_s, rst, x_s = sem("r"), sem("stat"), sem("agg"), sem("veps"), sem("rst"), sem("x_new")
        passed = sem("passed")
        block = ctx.enter_context(nc.Block())

        @block.gpsimd
        def _(pool):
            def body(t, p):
                i = t - 1
                if live(i, NG):
                    wait(pool, agg, i * 4 + 4)
                    nc.gpsimd.tensor_tensor(veps[:], mv[:, :, 1], K.eps[:, 0:4], ALU.add).then_inc(veps_s, 1)
                    wait(pool, veps_s, i + 1)
                    nc.gpsimd.tensor_tensor(rstd[:], veps[:], K.half[:, 0:4], ALU.pow).then_inc(rst, 1)
            steps(pool, NG, LAG, HEAD, body)

        @block.vector
        def _(dve):
            def body(t, p):
                for j, (c, w) in enumerate(FCH):
                    if live(t, NG):
                        rows = slice(0, w)
                        b = j % 2
                        n = t * NJ + j
                        wait(dve, g_s, n + 1)
                        wait(dve, u_p, n + 1)
                        wait(dve, d_p, n - (RING - 1))
                        if j < NEC:
                            nc.vector.tensor_tensor(up[:, b], u_ps[b][:], gate[:, b], ALU.mult).then_inc(u_s, 1)
                            wait(dve, u_s, n + 1)
                            wait(dve, c_p, t * NEC + (j + 1))
                            nc.vector.tensor_tensor(hid[:, j % RING], up[:, b], c_ps[b][:], ALU.mult).then_inc(h_s, 1)
                        else:
                            nc.vector.tensor_tensor(hid[rows, j % RING], u_ps[b][rows, :], gate[rows, b],
                                                    ALU.mult).then_inc(u_s, 1)
                    if j == 2 and live(t - 1, NG):
                        i = t - 1
                        wait(dve, d_p, t * NJ)
                        nc.vector.tensor_tensor(r[:], y_ps[:].rearrange("s (n d) -> s n d", n=4),
                                                K.X[:, bass.ds(i * 4, 4), :], ALU.add).then_inc(r_s, 1)
                        wait(dve, r_s, i + 1)
                        for n in range(4):
                            nc.vector.bn_stats(bn[:, n], r[:, n]).then_inc(stat, 1)
                        for n in range(4):
                            wait_apart(dve, stat, i * 4 + (n + 1), passed)
                            nc.vector.bn_aggr(mv[:, n], bn[:, n]).then_inc(agg, 1)
                    if j == 3 and live(t - 1, NG):
                        i = t - 1
                        wait(dve, rst, i + 1)
                        for n in range(4):
                            nc.vector.tensor_scalar(K.X[:, i * 4 + n, :], r[:, n], mv[:, n, 0:1],
                                                    rstd[:, n:n + 1], ALU.subtract, ALU.mult).then_inc(x_s, 1)
            steps(dve, NG, LAG, HEAD, body)

        @block.scalar
        def _(act):
            def body(t, p):
                for j, (c, w) in enumerate(FCH):
                    if live(t, NG):
                        n = t * NJ + j
                        wait(act, g_p, n + 1)
                        wait(act, u_s, n - 1)
                        nc.scalar.activation(gate[0:w, j % 2], g_ps[j % 2][0:w, :], ACT.Silu).then_inc(g_s, 1)
            steps(act, NG, LAG, HEAD, body)

        @block.tensor
        def _(pe):
            pe.wait_ge(K.moe_in, K.n_in[K.moe_in.name])

            def product(dst, w, c, x):
                for k, (m, n) in enumerate(((0, 0), (0, 1), (1, 0))):
                    last = nc.tensor.matmul(dst[:], w[m][:, c:c + 128], x[n], start=(k == 0), stop=(k == 2))
                return last

            def down(t, j):
                w = FCH[j][1]
                if j < NEC:
                    wait(pe, h_s, t * NEC + (j + 1))
                else:
                    wait(pe, u_s, t * NJ + (j + 1))
                if j == 0:
                    wait(pe, r_s, t)
                for n in range(4):
                    last = nc.tensor.matmul(y_ps[:, 128 * n:128 * n + 128], hid[0:w, j % RING, 128 * n:128 * n + 128],
                                            K.wd[0:w, j, :], start=(j == 0 and n == 0), stop=(j == NJ - 1),
                                            skip_group_check=True)
                last.then_inc(d_p, 1)

            def body(t, p):
                for j, (c, w) in enumerate(FCH):
                    if live(t, NG):
                        n = t * NJ + j
                        b = j % 2
                        xT = [K.XT[m][:, bass.ds(t * 512, 512)] for m in range(2)]
                        wait(pe, g_s, n - 1)
                        product(g_ps[b], K.wgp, c, xT).then_inc(g_p, 1)
                        wait(pe, u_s, n - 1)
                        product(u_ps[b], K.wup, c, xT).then_inc(u_p, 1)
                        if j < NEC:
                            wait_apart(pe, h_s, t * NEC + max(j - 1, 0), passed)
                            nc.tensor.matmul(c_ps[b][:], K.expert_ofb[:, c:c + w], K.combT[:, bass.ds(t * 512, 512)],
                                             start=True, stop=True).then_inc(c_p, 1)
                    if j < 2 and live(t - 1, NG):
                        down(t - 1, NJ - 2 + j)
                    if j >= 2 and live(t, NG):
                        down(t, j - 2)
            steps(pe, NG, LAG, HEAD, body)


def recurrence(nc, K):
    G = 2
    NG, W = NB // G, G * S
    LAG, HEAD = 7, 10
    with ExitStack() as ctx:
        def sb(name, shape, dt=F32):
            return ctx.enter_context(nc.sbuf_tensor("d_" + name, shape, dt))

        sem = ctx.enter_context(semaphores(nc, "d_"))

        bn = [sb(f"bn{k}", [S, G, 6]) for k in range(3)]
        mv = [sb(f"mv{k}", [S, 2, G, 2]) for k in range(3)]
        veps = [sb(f"veps{k}", [S, 2, G]) for k in range(3)]
        rstd = [sb(f"rstd{k}", [S, 2, G]) for k in range(3)]
        zn = sb("zn", [S, 2, G, D])
        hT = sb("hT", [D, 2, W])
        ta = sb("ta", [D, 2, W])
        tb = sb("tb", [D, 2, W])
        tc = sb("tc", [D, 2, W])
        a = sb("a", [D, 2, W])
        u = sb("u", [D, 2, W])
        state = sb("state", [D, 2, W])
        yT = sb("yT", [D, 2, W])
        x1 = sb("x1", [S, 2, G, D])
        xsum = sb("xsum", [S, 2, G, D])
        X1 = sb("x1_tok", [S, NB, D])
        zn2 = sb("zn2", [S, 2, G, D])
        h2T = sb("h2T", [D, 2, W])
        hid = sb("hid", [128, 2, 4, W])
        r = sb("r", [S, 2, G, D])
        B = K.bank
        t1_ps, t2_ps = B[0][:, 0:W], B[7][:, 0:W]
        za, zb, zc, ty_ps = B[1][:, 0:W], B[1][:, W:2 * W], B[2][:, 0:W], B[6][:, 0:W]
        m_ps, y_ps = [B[3], B[4]], B[5]

        half_s = sem("half")
        stat, agg, veps_s, rst = ([sem(f"{n}{k}") for k in range(3)] for n in ("stat", "agg", "veps", "rst"))
        zn_s, t1_p, hT_s, z_p, tanh_s = sem("zn"), sem("t1_ps"), sem("hT"), sem("z_ps"), sem("tanh")
        au_s, sc_s, yT_s, ty_p, x1_s, xsum_s = sem("au"), sem("scan"), sem("yT"), sem("ty_ps"), sem("x1"), sem("xsum")
        zn2_s, t2_p, h2T_s, m_p, gelu_s = sem("zn2"), sem("t2_ps"), sem("h2T"), sem("mlp_ps"), sem("gelu")
        y_p, r_s, x_s = sem("y_ps"), sem("r"), sem("x_new")
        passed = sem("passed")
        block = ctx.enter_context(nc.Block())

        @block.gpsimd
        def _(pool):
            pool.wait_ge(K.w1_in, K.n_in[K.w1_in.name])

            def inverse_root(i, b, k):
                wait(pool, agg[k], i * G + G)
                nc.gpsimd.tensor_tensor(veps[k][:, b], mv[k][:, b, :, 1], K.eps[:, 0:G], ALU.add).then_inc(veps_s[k], 1)
                wait(pool, veps_s[k], i + 1)
                nc.gpsimd.tensor_tensor(rstd[k][:, b], veps[k][:, b], K.half[:, 0:G], ALU.pow).then_inc(rst[k], 1)

            def body(t, p):
                i, b = t - 7, (p - 7) % 2
                if live(i, NG):
                    inverse_root(i, b, 2)
                i, b = t - 3, (p - 3) % 2
                if live(i, NG):
                    inverse_root(i, b, 1)
                i, b = t, p
                if live(i, NG):
                    inverse_root(i, b, 0)
                i, b = t - 6, p
                if live(i, NG):
                    wait(pool, r_s, i - 1)
                    wait(pool, x1_s, i * 2 + 2)
                    nc.gpsimd.tensor_tensor(xsum[:, b], X1[:, bass.ds(i * G, G), :], K.X[:, bass.ds(i * G, G), :],
                                            ALU.add).then_inc(xsum_s, 1)
                    wait(pool, xsum_s, i * 2 + 1)
                    nc.gpsimd.tensor_tensor(xsum[:, b], xsum[:, b], K.bm2[:].unsqueeze(1).to_broadcast([S, G, D]),
                                            ALU.add).then_inc(xsum_s, 1)
            steps(pool, NG, LAG, HEAD, body)

        @block.vector
        def _(dve):
            dve.wait_ge(K.w1_in, K.n_in[K.w1_in.name])
            nc.vector.tensor_scalar(K.habc[:], K.cols1[:, 2:5], 0.5, None, ALU.mult).then_inc(half_s, 1)

            def statistics(src, i, b, k):
                for n in range(G):
                    nc.vector.bn_stats(bn[k][:, n], src(n)).then_inc(stat[k], 1)
                wait(dve, rst[k], i - 1)
                for n in range(G):
                    wait_apart(dve, stat[k], i * G + (n + 1), passed)
                    nc.vector.bn_aggr(mv[k][:, b, n], bn[k][:, n]).then_inc(agg[k], 1)

            def normalise(dst, src, b, k, done):
                for n in range(G):
                    last = nc.vector.tensor_scalar(dst(n), src(n), mv[k][:, b, n, 0:1], rstd[k][:, b, n:n + 1],
                                                   ALU.subtract, ALU.mult)
                last.then_inc(done, 1)

            def body(t, p):
                i, b = t - 7, (p - 7) % 2
                if live(i, NG):
                    wait(dve, y_p, i + 1)
                    wait(dve, xsum_s, i * 2 + 2)
                    nc.vector.tensor_tensor(r[:, b], y_ps[:, 0:W].rearrange("s (n d) -> s n d", n=G),
                                            xsum[:, b], ALU.add).then_inc(r_s, 1)
                    wait(dve, r_s, i + 1)
                    statistics(lambda n: r[:, b, n], i, b, 2)
                i, b = t - 3, (p - 3) % 2
                if live(i, NG):
                    wait(dve, ty_p, i + 1)
                    nc.vector.scalar_tensor_tensor(out=x1[:, b], in0=ty_ps.rearrange("s (n d) -> s n d", n=G),
                                                   scalar=-0.25, in1=K.X[:, bass.ds(i * G, G), :],
                                                   op0=ALU.mult, op1=ALU.add).then_inc(x1_s, 1)
                    wait(dve, x1_s, i * 2 + 1)
                    nc.vector.tensor_copy(X1[:, bass.ds(i * G, G), :], x1[:, b]).then_inc(x1_s, 1)
                    statistics(lambda n: x1[:, b, n], i, b, 1)
                i, b = t - 1, (p - 1) % 2
                if live(i, NG):
                    wait(dve, t1_p, i + 1)
                    wait(dve, z_p, (i - 1) * 3)
                    nc.vector.tensor_scalar(hT[:, b], t1_ps, K.cols1[:, 0:1], K.cols1[:, 1:2],
                                            ALU.mult, ALU.add).then_inc(hT_s, 1)
                i, b = t - 4, p
                if live(i, NG):
                    wait(dve, t2_p, i + 1)
                    wait(dve, m_p, (i - 1) * 4)
                    nc.vector.tensor_scalar(h2T[:, b], t2_ps, K.cols1[:, 5:6], K.cols1[:, 6:7],
                                            ALU.mult, ALU.add).then_inc(h2T_s, 1)
                i, b = t, p
                if live(i, NG):
                    statistics(lambda n: K.X[:, i * G + n, :], i, b, 0)
                i, b = t - 3, (p - 3) % 2
                if live(i, NG):
                    wait(dve, rst[1], i + 1)
                    wait(dve, t2_p, i - 1)
                    normalise(lambda n: zn2[:, b, n], lambda n: x1[:, b, n], b, 1, zn2_s)
                i, b = t - 7, (p - 7) % 2
                if live(i, NG):
                    wait(dve, rst[2], i + 1)
                    normalise(lambda n: K.X[:, i * G + n, :], lambda n: r[:, b, n], b, 2, x_s)
                i, b = t, p
                if live(i, NG):
                    wait(dve, rst[0], i + 1)
                    wait(dve, t1_p, i - 1)
                    normalise(lambda n: zn[:, b, n], lambda n: K.X[:, i * G + n, :], b, 0, zn_s)
                i, b = t - 2, p
                if live(i, NG):
                    wait(dve, tanh_s, i * 3 + 3)
                    wait(dve, ty_p, i - 1)
                    nc.vector.tensor_scalar(a[:, b], ta[:, b], 0.5, 0.5, ALU.mult, ALU.add).then_inc(au_s, 1)
                    nc.vector.scalar_tensor_tensor(out=u[:, b], in0=ta[:, b], scalar=1.0, in1=tb[:, b],
                                                   op0=ALU.subtract, op1=ALU.mult).then_inc(au_s, 1)
                    wait(dve, au_s, i * 3 + 1)
                    nc.vector.memset(a[:, b].rearrange("d (n s) -> d n s", n=G)[:, :, 0:1], 0.0).then_inc(au_s, 1)
                    wait(dve, au_s, i * 3 + 3)
                    nc.vector.tensor_tensor_scan(state[:, b], a[:, b], u[:, b], 0.0, ALU.mult, ALU.add).then_inc(sc_s, 1)
                    wait(dve, sc_s, i + 1)
                    nc.vector.scalar_tensor_tensor(out=yT[:, b], in0=tc[:, b], scalar=1.0, in1=state[:, b],
                                                   op0=ALU.add, op1=ALU.mult).then_inc(yT_s, 1)
            steps(dve, NG, LAG, HEAD, body)

        @block.scalar
        def _(act):
            act.wait_ge(K.w1_in, K.n_in[K.w1_in.name])
            act.wait_ge(half_s, 1)

            def body(t, p):
                i, b = t - 5, (p - 5) % 2
                if live(i, NG):
                    wait(act, y_p, i - 1)
                    for c in range(4):
                        wait(act, m_p, i * 4 + (c // 2 * 2 + 2))
                        nc.scalar.activation(hid[:, b, c], m_ps[c // 2][:, W * (c % 2):W * (c % 2) + W], ACT.Gelu,
                                             bias=K.bm1[:, c:c + 1]).then_inc(gelu_s, 1)
                i, b = t - 2, p
                if live(i, NG):
                    wait(act, yT_s, i - 1)
                    for n, (dst, z, scale, bias) in enumerate(((ta, za, 0.5, K.habc[:, 0:1]),
                                                               (tb, zb, 1.0, K.cols1[:, 3:4]),
                                                               (tc, zc, 0.5, K.habc[:, 2:3]))):
                        wait(act, z_p, i * 3 + max(n + 1, 2))
                        nc.scalar.activation(dst[:, b], z, ACT.Tanh, bias=bias, scale=scale).then_inc(tanh_s, 1)
            steps(act, NG, LAG, HEAD, body)

        @block.tensor
        def _(pe):
            pe.wait_ge(K.w1_in, K.n_in[K.w1_in.name])

            def turn(dst, src, done):
                for n in range(G):
                    last = nc.tensor.transpose(dst[:, S * n:S * n + S], src(n), K.ident[:])
                last.then_inc(done, 1)

            def body(t, p):
                i, b = t - 3, (p - 3) % 2
                if live(i, NG):
                    wait(pe, yT_s, i + 1)
                    wait(pe, x1_s, i * 2)
                    turn(ty_ps, lambda n: yT[:, b, S * n:S * n + S], ty_p)
                i, b = t - 1, (p - 1) % 2
                if live(i, NG):
                    wait(pe, zn_s, i + 1)
                    wait(pe, hT_s, i)
                    turn(t1_ps, lambda n: zn[:, b, n], t1_p)
                i, b = t - 4, p
                if live(i, NG):
                    wait(pe, zn2_s, i + 1)
                    wait(pe, h2T_s, i)
                    turn(t2_ps, lambda n: zn2[:, b, n], t2_p)
                i, b = t - 5, (p - 5) % 2
                if live(i, NG):
                    wait(pe, h2T_s, i + 1)
                    for c in range(4):
                        wait(pe, gelu_s, i * 4 + (c // 2 * 2 - 2))
                        nc.tensor.matmul(m_ps[c // 2][:, W * (c % 2):W * (c % 2) + W], K.w1[:, 128 * c:128 * c + 128],
                                         h2T[:, b], start=True, stop=True).then_inc(m_p, 1)
                i, b = t - 2, p
                if live(i, NG):
                    wait(pe, hT_s, i + 1)
                    for n, z in enumerate((za, zb, zc)):
                        wait(pe, tanh_s, i * 3 + (0 if n == 2 else -1))
                        nc.tensor.matmul(z, K.wabc[:, n, :], hT[:, b], start=True, stop=True).then_inc(z_p, 1)
                i, b = t - 6, p
                if live(i, NG):
                    wait(pe, gelu_s, i * 4 + 4)
                    wait(pe, r_s, i)
                    for n in range(G):
                        y = y_ps[:, D * n:D * n + D]
                        for c in range(4):
                            last = nc.tensor.matmul(y, hid[:, b, c, S * n:S * n + S], K.w2[:, c, :],
                                                    start=(c == 0), stop=(c == 3))
                    last.then_inc(y_p, 1)
            steps(pe, NG, LAG, HEAD, body)


def cross_attention(nc, K):
    LAG, HEAD = 7, 10
    C = INNER // 128
    NC = 6
    QK = [(1, K.wq1, 0), (1, K.wq1, 512), (1, K.wkv1, 0), (1, K.wkv1, 512), (0, K.wkv1, 0), (0, K.wkv1, 512)]
    V = [(1, INNER), (1, INNER + 512), (0, INNER), (0, INNER + 512)]
    QK_AT = {0: 0, 1: 1, 3: 2, 4: 3, 6: 4, 7: 5}
    V_AT = {2: (0, 1), 5: (2, 3)}

    ON_DVE, ON_POOL = (0, 2, 4), (1, 3, 5)

    TQ_DVE, TQ_ACT = (0, 3, 4), (1, 2, 5)

    def chunk_at(s, after, t):
        return QK_AT.get((s - after) % 8), t - 2 - (1 if s < after else 0)
    with ExitStack() as ctx:
        def sb(name, shape, dt=F32):
            return ctx.enter_context(nc.sbuf_tensor("e_" + name, shape, dt))

        sem = ctx.enter_context(semaphores(nc, "e_"))

        bn = sb("bn", [S, 2, 6])
        mv = sb("mv", [S, 2, 2, 2])
        veps = sb("veps", [S, 2, 2])
        rstd = sb("rstd", [S, 2, 2])
        bn2 = sb("bn2", [S, 6])
        mv2 = sb("mv2", [S, 2, 2])
        veps2 = sb("veps2", [S, 2, 1])
        rstd2 = sb("rstd2", [S, 2, 1])
        zn = sb("zn", [S, 2, 2, D])
        nT = sb("nT", [D, 2, 2, S])
        nT2 = sb("nT2", [D, 2, 2, S])
        sq = sb("sq", [S, 2, 512])
        ss = sb("ss", [S, NC, 8])
        ssm = sb("ssm", [S, NC, 8])
        rs = sb("rs", [S, NC, 8])
        qk = sb("qk", [S, 2, NC, 512])
        v = sb("v", [S, 2, 2, INNER])
        qT = sb("qT", [128, 2, C, S])
        kT = sb("kT", [128, 2, C, 2, S])
        neg_max = sb("neg_max", [S, 2, NH1])
        den = sb("den", [S, 2, NH1])
        rden = sb("rden", [S, 2, NH1])
        prob = sb("prob", [S, 2, NH1, 2 * S])
        probT = sb("probT", [S, 4, 4, S])
        oT = sb("oT", [128, 2, C, S])
        r = sb("r", [S, 2, D])
        mask8 = sb("mask8", [1, NB, S], mybir.dt.uint8)
        mrow = sb("mask_row", [1, NB, S], BF16)
        onesr = sb("ones_row", [1, S], BF16)
        Bk = K.bank
        n_ps, y_ps = Bk[0][:, 0:256], Bk[0][:, 256:384]
        proj, pT_b, tq_b, score, o_b = Bk[1:3], Bk[3], Bk[4], Bk[5:7], Bk[7]

        mask_in, prep, prep2 = sem("mask_in"), sem("prep"), sem("prep2")
        stat, agg, veps_s, rst, zn_s = sem("stat"), sem("agg"), sem("veps"), sem("rst"), sem("zn")
        n_p, nT_s, nT2_s = sem("n_ps"), sem("nT"), sem("nT2")
        qk_p, sq_s, ss_s, ssm_s, rs_s, qk_s = sem("qk_ps"), sem("sq"), sem("ss"), sem("ssm"), sem("rs"), sem("qk")
        raw_s, qkg_s = sem("raw"), sem("qk_pool")
        v_p, v_c, tq_p, tq_d, tq_a = sem("v_ps"), (sem("v_dve"), sem("v_act")), sem("tq_ps"), sem("tq_dve"), sem("tq_act")
        s_p, mx, ex, rd_s = sem("s_ps"), sem("mx"), sem("ex"), sem("rden")
        pn_s, pT_p, pT_d, pT_a, pv_p = sem("prob"), sem("pT_ps"), sem("pT_dve"), sem("pT_act"), sem("pv_ps")
        oT_s, y_p = sem("oT"), sem("y_ps")
        r_s, stat2, agg2, veps2_s, rst2, x_s = (sem("r"), sem("stat2"), sem("agg2"), sem("veps2"), sem("rst2"),
                                                sem("x_new"))
        passed = sem("passed")
        xb_s = sem("x_bias")
        xb = sb("x_bias", [S, 2, D])
        block = ctx.enter_context(nc.Block())

        def most(i, k):
            return min(i, NB) * k if isinstance(i, int) else i * k

        @block.sync
        def _(sp):
            sp.dma_start(mask8[:], K.A["mask_BxS2_bf1"].rearrange("(o b) s -> o b s", o=1)).then_inc(mask_in, 16)

        @block.gpsimd
        def _(pool):
            nc.gpsimd.memset(onesr[:], 1.0).then_inc(prep2, 1)
            pool.wait_ge(K.wx1_in, K.n_in[K.wx1_in.name])
            pool.wait_ge(prep2, 1)

            def body(t, p):
                for c, i in ((5, t - 3), (0, t - 2), (1, t - 2), (2, t - 2), (3, t - 2), (4, t - 2)):
                    if live(i, NB):
                        wait_apart(pool, ss_s, i * NC + (c + 1), passed)
                        nc.gpsimd.tensor_scalar(ssm[:, c], ss[:, c], DH1 * 1e-16, None, ALU.max).then_inc(ssm_s, 1)
                        wait(pool, ssm_s, i * NC + (c + 1))
                        nc.gpsimd.tensor_tensor(rs[:, c], ssm[:, c], K.half[:, 0:8], ALU.pow).then_inc(rs_s, 1)
                        if c in ON_POOL:
                            b = (p - 3) % 2 if c == 5 else p
                            wait(pool, rs_s, i * NC + (c + 1))
                            wait(pool, raw_s, i * NC + (c + 1))
                            nc.gpsimd.tensor_tensor(qk[:, b, c].rearrange("s (h d) -> s h d", h=8),
                                                    qk[:, b, c].rearrange("s (h d) -> s h d", h=8),
                                                    rs[:, c].unsqueeze(2).to_broadcast([S, 8, DH1]), ALU.mult
                                                    ).then_inc(qkg_s, 1)
                    if c == 0:
                        i, b = t, p
                        if live(i, NB):
                            wait(pool, agg, i * 2 + 2)
                            nc.gpsimd.tensor_tensor(veps[:, b], mv[:, b, :, 1], K.eps[:, 0:2], ALU.add
                                                    ).then_inc(veps_s, 1)
                            wait(pool, veps_s, i + 1)
                            nc.gpsimd.tensor_tensor(rstd[:, b], veps[:, b], K.half[:, 0:2], ALU.pow).then_inc(rst, 1)
                    if c == 1:
                        i, b = t - 7, (p - 7) % 2
                        if live(i, NB):
                            wait(pool, agg2, i + 1)
                            nc.gpsimd.tensor_tensor(veps2[:, b], mv2[:, b, 1:2], K.eps[:, 0:1], ALU.add
                                                    ).then_inc(veps2_s, 1)
                            wait(pool, veps2_s, i + 1)
                            nc.gpsimd.tensor_tensor(rstd2[:, b], veps2[:, b], K.half[:, 0:1], ALU.pow
                                                    ).then_inc(rst2, 1)
                i, b = t - 6, p
                if live(i, NB):
                    wait(pool, r_s, i - 1)
                    nc.gpsimd.tensor_tensor(xb[:, b], K.X[:, i, :], K.bout[:], ALU.add).then_inc(xb_s, 1)
                i, b = t - 2, p
                if live(i, NB):
                    wait_apart(pool, v_p, (i - 1) * 4, passed)
                    nc.gpsimd.tensor_copy(nT2[:, b], nT[:, b]).then_inc(nT2_s, 1)
            steps(pool, NB, LAG, HEAD, body)

        @block.vector
        def _(dve):
            dve.wait_ge(K.wx1_in, K.n_in[K.wx1_in.name])
            nc.vector.tensor_scalar(K.qg[:], K.colsx[:, 5:6], float(DH1) ** 0.5, None, ALU.mult).then_inc(prep, 1)
            dve.wait_ge(mask_in, 16)
            nc.vector.tensor_scalar(mrow[:], mask8[:], -1.0, 1e30, ALU.add, ALU.mult).then_inc(prep, 1)

            def body(t, p):
                i4, b4, i5 = t - 4, p, t - 5
                for s in range(8):
                    if s % 2 and live(i4, NB):
                        h0 = 2 * (s - 1)
                        wait(dve, ex, i4 * 8 + (s + 1))
                        nc.vector.reciprocal(rden[:, b4, h0:h0 + 4], den[:, b4, h0:h0 + 4]).then_inc(rd_s, 1)
                        wait_apart(dve, rd_s, i4 * 4 + (s + 1) // 2, passed)
                        for h in range(h0, h0 + 4):
                            last = nc.vector.tensor_scalar(prob[:, b4, h], prob[:, b4, h], rden[:, b4, h:h + 1], None,
                                                           ALU.mult)
                        last.then_inc(pn_s, 1)
                    c, i = chunk_at(s, 1, t)
                    if c is not None and live(i, NB):
                        wait(dve, sq_s, i * NC + (c + 1))
                        nc.vector.tensor_reduce(ss[:, c], sq[:, c % 2].rearrange("s (h d) -> s h d", h=8),
                                                AX, ALU.add).then_inc(ss_s, 1)
                    if s % 2 == 0 and live(i5, NB):
                        wait(dve, pT_p, i5 * 8 + (s + 1))
                        wait(dve, pv_p, i5 * 8 + (s - 3))
                        nc.vector.tensor_copy(probT[:, s % 4], pT_b[:].rearrange("k (n q) -> k n q", n=4)
                                              ).then_inc(pT_d, 1)
                    if s % 2 == 0 and live(i4, NB):
                        for odd in range(2):
                            wait(dve, s_p, i4 * 8 + (s + odd + 1))
                            h0 = 2 * s + odd
                            nc.vector.tensor_reduce(neg_max[:, b4, h0:h0 + 3:2],
                                                    score[odd][:].rearrange("q (h k) -> q h k", h=2),
                                                    AX, ALU.max, negate=True).then_inc(mx, 1)
                    if live(i4, NB):
                        for n in V_AT.get(s, ())[:1]:
                            wait(dve, v_p, i4 * 4 + (n + 1))
                            wait(dve, pv_p, (i4 - 1) * 8)
                            src, c0 = V[n][0], V[n][1] - INNER
                            nc.vector.tensor_copy(v[:, b4, src, c0:c0 + 512], proj[n % 2][:]).then_inc(v_c[0], 1)
                    c, i = chunk_at(s, 2, t)
                    b = p if s >= 2 else (p - 3) % 2
                    if c in ON_DVE and live(i, NB):
                        wait(dve, rs_s, i * NC + (c + 1))
                        wait(dve, raw_s, i * NC + (c + 1))
                        nc.vector.tensor_tensor(qk[:, b, c].rearrange("s (h d) -> s h d", h=8),
                                                qk[:, b, c].rearrange("s (h d) -> s h d", h=8),
                                                rs[:, c].unsqueeze(2).to_broadcast([S, 8, DH1]), ALU.mult
                                                ).then_inc(qk_s, 1)
                    c, i3, b3 = QK_AT.get(s), t - 3, (p - 3) % 2
                    if c in TQ_DVE and live(i3, NB):
                        wait(dve, tq_p, i3 * NC + (c + 1))
                        wait(dve, s_p, (i3 - 1) * 8)
                        half = slice(4 * (c % 2), 4 * (c % 2) + 4)
                        dst = qT[:, b3, half] if c < 2 else kT[:, b3, half, 1 if c < 4 else 0]
                        nc.vector.tensor_scalar(dst, tq_b[:].rearrange("p (c s) -> p c s", c=4),
                                                K.colsx[:, 4:5] if c < 2 else K.qg[:], None, ALU.mult
                                                ).then_inc(tq_d, 1)
                    i, b = t, p
                    if s == 1 and live(i, NB):
                        nc.vector.bn_stats(bn[:, 0], K.CTX[:, i, :]).then_inc(stat, 1)
                        nc.vector.bn_stats(bn[:, 1], K.X[:, i, :]).then_inc(stat, 1)
                        wait(dve, rst, i - 1)
                        for n in range(2):
                            wait_apart(dve, stat, i * 2 + (n + 1), passed)
                            nc.vector.bn_aggr(mv[:, b, n], bn[:, n]).then_inc(agg, 1)
                    if s == 4 and live(i, NB):
                        wait(dve, rst, i + 1)
                        wait(dve, n_p, i - 1)
                        for n, src in enumerate((K.CTX, K.X)):
                            last = nc.vector.tensor_scalar(zn[:, b, n], src[:, i, :], mv[:, b, n, 0:1],
                                                           rstd[:, b, n:n + 1], ALU.subtract, ALU.mult)
                        last.then_inc(zn_s, 1)
                    i, b = t - 1, (p - 1) % 2
                    if s == 2 and live(i, NB):
                        wait(dve, n_p, i + 1)
                        wait(dve, y_p, i - 5)
                        wait(dve, qk_p, (i - 1) * NC)
                        wait(dve, nT2_s, i - 1)
                        for n in range(2):
                            last = nc.vector.tensor_scalar(nT[:, b, n], n_ps[:, S * n:S * n + S],
                                                           K.colsx[:, 2 * n:2 * n + 1], K.colsx[:, 2 * n + 1:2 * n + 2],
                                                           ALU.mult, ALU.add)
                        last.then_inc(nT_s, 1)
                    i, b = t - 7, (p - 7) % 2
                    if s == 3 and live(i, NB):
                        wait(dve, y_p, i + 1)
                        wait(dve, xb_s, i + 1)
                        nc.vector.tensor_tensor(r[:, b], y_ps, xb[:, b], ALU.add).then_inc(r_s, 1)
                        wait(dve, r_s, i + 1)
                        nc.vector.bn_stats(bn2[:], r[:, b]).then_inc(stat2, 1)
                        wait(dve, stat2, i + 1)
                        wait_apart(dve, rst2, i - 1, passed)
                        nc.vector.bn_aggr(mv2[:, b], bn2[:]).then_inc(agg2, 1)
                    if s == 6 and live(i, NB):
                        wait(dve, rst2, i + 1)
                        nc.vector.tensor_scalar(K.X[:, i, :], r[:, b], mv2[:, b, 0:1], rstd2[:, b],
                                                ALU.subtract, ALU.mult).then_inc(x_s, 1)
            steps(dve, NB, LAG, HEAD, body)

        @block.scalar
        def _(act):
            act.wait_ge(K.wx1_in, K.n_in[K.wx1_in.name])
            act.wait_ge(prep, 2)

            def squares(i, b, c):
                wait(act, raw_s, i * NC + (c + 1))
                wait(act, ss_s, i * NC + (c - 1))
                nc.scalar.activation(sq[:, c % 2], qk[:, b, c], ACT.Square).then_inc(sq_s, 1)

            def body(t, p):
                i2, b2, i3, b3 = t - 2, p, t - 3, (p - 3) % 2
                i4, b4, i5, i6, b6 = t - 4, p, t - 5, t - 6, p
                for s in range(8):
                    for g, (i, b) in ((0, (i5, (p - 5) % 2)), (1, (i6, b6))):
                        if s == (5, 0)[g] and live(i, NB):
                            wait(act, pv_p, i * 8 + (4 * g + 4))
                            wait(act, y_p, i - 1)
                            nc.scalar.copy(oT[:, b, 4 * g:4 * g + 4], o_b[:].rearrange("p (c s) -> p c s", c=4)
                                           ).then_inc(oT_s, 1)
                    if s % 2 == 0 and live(i4, NB):
                        wait(act, pT_p, (i4 - 1) * 8)
                        wait(act, rd_s, (i4 - 1) * 4)
                        for odd in range(2):
                            wait(act, mx, i4 * 8 + (s + odd + 1))
                            for n in range(2):
                                h = 2 * s + odd + 2 * n
                                last = nc.scalar.activation(prob[:, b4, h], score[odd][:, 256 * n:256 * n + 256],
                                                            ACT.Exp, bias=neg_max[:, b4, h:h + 1],
                                                            accum_out=den[:, b4, h:h + 1])
                            last.then_inc(ex, 1)
                    if s % 2 == 1 and live(i5, NB):
                        wait(act, pT_p, i5 * 8 + (s + 1))
                        wait(act, pv_p, i5 * 8 + (s - 3))
                        nc.scalar.copy(probT[:, s % 4], pT_b[:].rearrange("k (n q) -> k n q", n=4)).then_inc(pT_a, 1)
                    c = QK_AT.get(s - 1)
                    if s % 2 and c is not None and live(i2, NB):
                        squares(i2, b2, c)
                    c = QK_AT.get(s)
                    if c is not None and live(i2, NB):
                        wait(act, qk_p, i2 * NC + (c + 1))
                        wait(act, tq_p, (i2 - 1) * NC)
                        nc.scalar.copy(qk[:, b2, c], proj[c % 2][:]).then_inc(raw_s, 1)
                        if s % 2:
                            squares(i2, b2, c)
                    if c in TQ_ACT and live(i3, NB):
                        wait(act, tq_p, i3 * NC + (c + 1))
                        wait(act, s_p, (i3 - 1) * 8)
                        half = slice(4 * (c % 2), 4 * (c % 2) + 4)
                        dst = qT[:, b3, half] if c < 2 else kT[:, b3, half, 1 if c < 4 else 0]
                        nc.scalar.activation(dst, tq_b[:].rearrange("p (c s) -> p c s", c=4), ACT.Copy,
                                             scale=K.colsx[:, 4:5] if c < 2 else K.qg[:]).then_inc(tq_a, 1)
                    if live(i4, NB):
                        for n in V_AT.get(s, ())[1:]:
                            wait(act, v_p, i4 * 4 + (n + 1))
                            wait(act, pv_p, (i4 - 1) * 8)
                            src, c0 = V[n][0], V[n][1] - INNER
                            nc.scalar.copy(v[:, b4, src, c0:c0 + 512], proj[n % 2][:]).then_inc(v_c[1], 1)
            steps(act, NB, LAG, HEAD, body)

        @block.tensor
        def _(pe):
            pe.wait_ge(K.wx1_in, K.n_in[K.wx1_in.name])
            pe.wait_ge(prep, 2)
            pe.wait_ge(prep2, 1)

            def values(i, b, s):
                if s % 2:
                    wait(pe, pT_a, i * 4 + (s + 1) // 2)
                else:
                    wait(pe, pT_d, i * 4 + s // 2 + 1)
                if s % 4 == 0:
                    wait(pe, oT_s, i * 2 + s // 4)
                if s == 0:
                    wait(pe, v_c[0], i * 2 + 2)
                    wait(pe, v_c[1], i * 2 + 2)
                for src in range(2):
                    for n in range(2):
                        h = 2 * s + n
                        last = nc.tensor.matmul(o_b[64 * n:64 * n + 64, 128 * (s % 4):128 * (s % 4) + 128],
                                                v[:, b, src, 64 * h:64 * h + 64], probT[:, s % 4, 2 * n + src],
                                                start=(src == 0), stop=(src == 1), skip_group_check=True)
                last.then_inc(pv_p, 1)

            def body(t, p):
                i2, b2, i3, b3 = t - 2, p, t - 3, (p - 3) % 2
                i4, b4, i5, b5, i6, b6 = t - 4, p, t - 5, (p - 5) % 2, t - 6, p
                for s in range(8):
                    if live(i5, NB):
                        wait(pe, pn_s, i5 * 4 + (s // 2 + 1))
                        if s % 2:
                            wait(pe, pT_d, i5 * 4 + (s + 1) // 2)
                        else:
                            wait(pe, pT_a, i5 * 4 + s // 2)
                        for n in range(4):
                            last = nc.tensor.transpose(pT_b[:, 128 * n:128 * n + 128],
                                                       prob[:, b5, 2 * s + n // 2, S * (n % 2):S * (n % 2) + S], K.ident[:])
                        last.then_inc(pT_p, 1)
                    if s % 2 == 0 and live(i4, NB):
                        if s == 0:
                            wait(pe, tq_d, i4 * len(TQ_DVE) + len(TQ_DVE))
                            wait(pe, tq_a, i4 * len(TQ_ACT) + len(TQ_ACT))
                        wait_apart(pe, ex, i4 * 8 + s, passed)
                        for odd in range(2):
                            nc.tensor.matmul(score[odd][:].rearrange("q (h n k) -> q h n k", h=2, n=2)[:, :, 0],
                                             onesr[:], mrow[:, i4, :].unsqueeze(1).to_broadcast([1, 2, S]),
                                             start=True, stop=False, skip_group_check=True)
                        for n in range(2):
                            for odd in range(2):
                                rows = slice(64 * odd, 64 * odd + 64)
                                last = nc.tensor.matmul(score[odd][:, 256 * n:256 * n + 256], qT[rows, b4, s + n],
                                                        kT[rows, b4, s + n], start=False, stop=True,
                                                        skip_group_check=True)
                                if n:
                                    last.then_inc(s_p, 1)
                    c = QK_AT.get(s)
                    if c is not None and live(i2, NB):
                        if c == 0:
                            wait(pe, nT_s, i2 + 1)
                        if c < 2 or not live(i4, NB):
                            wait(pe, raw_s, i2 * NC + (c - 1))
                        else:
                            wait(pe, v_c[c % 2], i4 * 2 + c // 2)
                        src, w, c0 = QK[c]
                        nc.tensor.matmul(proj[c % 2][:], nT[:, b2, src], w[:, c0:c0 + 512], start=True, stop=True
                                         ).then_inc(qk_p, 1)
                    if c is not None and live(i3, NB):
                        if c in ON_DVE:
                            wait(pe, qk_s, i3 * len(ON_DVE) + (ON_DVE.index(c) + 1))
                        else:
                            wait(pe, qkg_s, i3 * len(ON_POOL) + (ON_POOL.index(c) + 1))
                        before = (c - 1) % NC
                        for done, chunks in ((tq_d, TQ_DVE), (tq_a, TQ_ACT)):
                            if before in chunks:
                                wait(pe, done, (i3 - (c == 0)) * len(chunks) + (chunks.index(before) + 1))
                        for n in range(4):
                            last = nc.tensor.transpose(tq_b[:, 128 * n:128 * n + 128],
                                                       qk[:, b3, c, 128 * n:128 * n + 128], K.ident[:])
                        last.then_inc(tq_p, 1)
                    if live(i4, NB):
                        for n in V_AT.get(s, ()):
                            if n == 0:
                                wait(pe, nT2_s, i4 + 1)
                            wait(pe, raw_s, i2 * NC + (n + 1) if live(i2, NB) else NB * NC)
                            if not live(i2, NB):
                                wait(pe, v_c[n % 2], i4 * 2 + n // 2)
                            src, c0 = V[n]
                            nc.tensor.matmul(proj[n % 2][:], nT2[:, b4, src], K.wkv1[:, c0:c0 + 512],
                                             start=True, stop=True).then_inc(v_p, 1)
                    if s > 0 and live(i5, NB):
                        values(i5, b5, s - 1)
                if live(i5, NB):
                    values(i5, b5, 7)
                if live(t, NB):
                    wait(pe, zn_s, t + 1)
                    wait(pe, nT_s, t)
                    wait(pe, r_s, t - 6)
                    for n in range(2):
                        last = nc.tensor.transpose(n_ps[:, S * n:S * n + S], zn[:, p, n], K.ident[:])
                    last.then_inc(n_p, 1)
                if live(i6, NB):
                    wait(pe, oT_s, i6 * 2 + 2)
                    wait(pe, r_s, i6)
                    for c in range(C):
                        last = nc.tensor.matmul(y_ps, oT[:, b6, c], K.wout[:, c, :], start=(c == 0), stop=(c == C - 1))
                    last.then_inc(y_p, 1)
            steps(pe, NB, LAG, HEAD, body)


def bit_ffn(nc, K, out):
    LAG, HEAD = 6, 8
    C = FB // 128
    with ExitStack() as ctx:
        def sb(name, shape, dt=F32):
            return ctx.enter_context(nc.sbuf_tensor("f_" + name, shape, dt))

        sem = ctx.enter_context(semaphores(nc, "f_"))

        wsum = sb("wsum", [128, 3])
        wmean = sb("wmean", [128, 3])
        winv = sb("winv", [128, 3])
        dequant = sb("dequant", [128, 3])
        wq = sb("wq", [128, 3, FB])
        wqb = sb("wqb", [128, 3, FB], BF16)
        wT = sb("wT", [128, 3, FB], BF16)
        am = sb("am", [S, 2, 1])
        amc = sb("amc", [S, 2, 1])
        inv = sb("inv", [S, 2, 1])
        inv127 = sb("inv127", [S, 2, 1])
        dg = sb("dg", [S, 2, 3])
        xm = sb("xm", [S, 2, D])
        xq = sb("xq", [S, 2, D], BF16)
        xqT = sb("xqT", [D, 2, S], BF16)
        gate = sb("gate", [S, 2, FB])
        h = sb("h", [S, 2, FB])
        am2 = sb("am2", [S, 2, 1])
        amc2 = sb("amc2", [S, 2, 1])
        inv2 = sb("inv2", [S, 2, 1])
        inv1272 = sb("inv1272", [S, 2, 1])
        dh = sb("dh", [S, 2, 1])
        hm = sb("hm", [S, 2, FB])
        hq = sb("hq", [S, 2, FB], BF16)
        hqT = sb("hqT", [128, 2, FB], BF16)
        r = sb("r", [S, 2, D])
        bn = sb("bn", [S, 6])
        mv = sb("mv", [S, 2, 2])
        veps = sb("veps", [S, 2, 1])
        rstd = sb("rstd", [S, 2, 1])
        xo = sb("xo", [S, 2, D])
        Bk = K.bank
        xT_b, g_b, u_b, hT_b, y_b, w_b = Bk[0][:].bitcast(BF16), Bk[1], Bk[2], Bk[3][:].bitcast(BF16), Bk[4], Bk[5]

        wr, wsum_s, wtot_p, wp, wT_p, wT_s = sem("wr"), sem("wsum"), sem("wtot"), sem("wp"), sem("wT_ps"), sem("wT")
        am_s, amc_s, inv_s, i127_s, dg_s = sem("am"), sem("amc"), sem("inv"), sem("i127"), sem("dg")
        xm_s, xq_s, xT_p, xT_s, gu_p, g_s, h_s = (sem("xm"), sem("xq"), sem("xT_ps"), sem("xT"), sem("gu_ps"),
                                                  sem("gate"), sem("h"))
        am2_s, amc2_s, inv2_s, i1272_s, dh_s = sem("am2"), sem("amc2"), sem("inv2"), sem("i1272"), sem("dh")
        hm_s, hq_s, hT_p, hT_s, y_p, r_s = sem("hm"), sem("hq"), sem("hT_ps"), sem("hT"), sem("y_ps"), sem("r")
        stat, agg, veps_s, rst, x_s, out_s = (sem("stat"), sem("agg"), sem("veps"), sem("rst"), sem("x_new"),
                                              sem("stored"))
        passed = sem("passed")
        block = ctx.enter_context(nc.Block())

        @block.gpsimd
        def _(pool):
            def body(t, p):
                i, b = t - 5, (p - 5) % 2
                if live(i, NB):
                    wait(pool, agg, i + 1)
                    nc.gpsimd.tensor_tensor(veps[:, b], mv[:, b, 1:2], K.eps[:, 0:1], ALU.add).then_inc(veps_s, 1)
                    wait(pool, veps_s, i + 1)
                    nc.gpsimd.tensor_tensor(rstd[:, b], veps[:, b], K.half[:, 0:1], ALU.pow).then_inc(rst, 1)
                    wait(pool, rst, i + 1)
                    wait_apart(pool, out_s, (i - 1) * 16, passed)
                    nc.gpsimd.tensor_scalar(xo[:, b], r[:, b], mv[:, b, 0:1], rstd[:, b],
                                            ALU.subtract, ALU.mult).then_inc(x_s, 1)
            steps(pool, NB, LAG, HEAD, body)

        @block.sync
        def _(sp):
            def body(t, p):
                i, b = t - 6, p
                if live(i, NB):
                    wait_apart(sp, x_s, i + 1, passed)
                    wait(sp, out_s, i * 16)
                    sp.dma_start(out[i], xo[:, b]).then_inc(out_s, 16)
            steps(sp, NB, LAG, HEAD, body)
            sp.wait_ge(out_s, NB * 16)

        @block.vector
        def _(dve):
            dve.wait_ge(K.wb_in, K.n_in[K.wb_in.name])
            done = [0]

            def then(ins):
                done[0] += 1
                ins.then_inc(wp, 1)
                dve.wait_ge(wp, done[0])

            nc.vector.tensor_reduce(wsum[:], K.wbraw[:], AX, ALU.add, apply_absolute_value=True).then_inc(wsum_s, 1)
            dve.wait_ge(wtot_p, 1)
            then(nc.vector.tensor_scalar(wmean[:], w_b[:, 0:3], 1.0 / (D * FB), 1e-5, ALU.mult, ALU.max))
            then(nc.vector.reciprocal(winv[:], wmean[:]))
            then(nc.vector.tensor_scalar(dequant[:], wmean[:], 1.0 / 127.0, None, ALU.mult))
            for n in range(3):
                then(nc.vector.tensor_scalar(wq[:, n], K.wbraw[:, n], winv[:, n:n + 1], MAGIC, ALU.mult, ALU.add))
                then(nc.vector.tensor_scalar(wq[:, n], wq[:, n], -MAGIC, 1.0, ALU.add, ALU.min))
                nc.vector.tensor_scalar(wqb[:, n], wq[:, n], -1.0, None, ALU.max).then_inc(wr, 1)
                dve.wait_ge(wT_p, n + 1)
                nc.vector.tensor_copy(wT[:, n], hT_b[:, 0:FB]).then_inc(wT_s, 1)

            def body(t, p):
                i5, b5 = t - 5, (p - 5) % 2
                if live(i5, NB):
                    wait(dve, y_p, i5 + 1)
                    wait(dve, x_s, i5 - 1)
                    nc.vector.scalar_tensor_tensor(out=r[:, b5], in0=y_b[:, 0:D], scalar=dh[:, b5], in1=K.X[:, i5, :],
                                                   op0=ALU.mult, op1=ALU.add).then_inc(r_s, 1)
                i, b = t, p
                if live(i, NB):
                    wait(dve, am_s, i)
                    nc.vector.tensor_reduce(am[:, b], K.X[:, i, :], AX, ALU.max, apply_absolute_value=True
                                            ).then_inc(am_s, 1)
                if live(i5, NB):
                    wait(dve, r_s, i5 + 1)
                    nc.vector.bn_stats(bn[:], r[:, b5]).then_inc(stat, 1)
                if live(i, NB):
                    wait(dve, am_s, i + 1)
                    nc.vector.tensor_scalar(amc[:, b], am[:, b], 1e-5, None, ALU.max).then_inc(amc_s, 1)
                if live(i5, NB):
                    wait(dve, stat, i5 + 1)
                    wait_apart(dve, rst, i5 - 1, passed)
                    nc.vector.bn_aggr(mv[:, b5], bn[:]).then_inc(agg, 1)
                if live(i, NB):
                    wait(dve, amc_s, i + 1)
                    nc.vector.reciprocal(inv[:, b], amc[:, b]).then_inc(inv_s, 1)
                i3, b3 = t - 3, (p - 3) % 2
                if live(i3, NB):
                    wait(dve, h_s, i3 + 1)
                    nc.vector.tensor_reduce(am2[:, b3], h[:, b3], AX, ALU.max, apply_absolute_value=True
                                            ).then_inc(am2_s, 1)
                if live(i, NB):
                    wait(dve, inv_s, i + 1)
                    nc.vector.tensor_scalar(inv127[:, b], inv[:, b], 127.0, None, ALU.mult).then_inc(i127_s, 1)
                if live(i3, NB):
                    wait(dve, am2_s, i3 + 1)
                    nc.vector.tensor_scalar(amc2[:, b3], am2[:, b3], 1e-5, None, ALU.max).then_inc(amc2_s, 1)
                if live(i, NB):
                    wait(dve, i127_s, i + 1)
                    nc.vector.tensor_scalar(xm[:, b], K.X[:, i, :], inv127[:, b], MAGIC, ALU.mult, ALU.add
                                            ).then_inc(xm_s, 1)
                if live(i3, NB):
                    wait(dve, amc2_s, i3 + 1)
                    nc.vector.reciprocal(inv2[:, b3], amc2[:, b3]).then_inc(inv2_s, 1)
                if live(i3, NB):
                    wait(dve, inv2_s, i3 + 1)
                    wait(dve, hm_s, i3 - 1)
                    nc.vector.tensor_scalar(inv1272[:, b3], inv2[:, b3], 127.0, None, ALU.mult).then_inc(i1272_s, 1)
                if live(i, NB):
                    wait(dve, xm_s, i + 1)
                    wait(dve, xT_p, i - 1)
                    nc.vector.tensor_scalar(xq[:, b], xm[:, b], -MAGIC, None, ALU.add).then_inc(xq_s, 1)
                if live(i3, NB):
                    nc.vector.tensor_scalar(dh[:, b3], amc2[:, b3], dequant[:, 2:3], None, ALU.mult).then_inc(dh_s, 1)
                i2, b2 = t - 2, p
                if live(i2, NB):
                    wait(dve, g_s, i2 + 1)
                    wait(dve, gu_p, i2 * 2 + 2)
                    wait(dve, hm_s, i2 - 1)
                    nc.vector.scalar_tensor_tensor(out=h[:, b2], in0=u_b[:], scalar=dg[:, b2, 1:2], in1=gate[:, b2],
                                                   op0=ALU.mult, op1=ALU.mult).then_inc(h_s, 1)
                if live(i, NB):
                    wait(dve, g_s, i - 1)
                    wait(dve, h_s, i - 1)
                    nc.vector.tensor_scalar(dg[:, b], dequant[:], amc[:, b], None, ALU.mult).then_inc(dg_s, 1)
                if live(i3, NB):
                    wait(dve, hm_s, i3 + 1)
                    wait(dve, hT_p, i3 - 1)
                    nc.vector.tensor_scalar(hq[:, b3], hm[:, b3], -MAGIC, None, ALU.add).then_inc(hq_s, 1)
            steps(dve, NB, LAG, HEAD, body)

        @block.scalar
        def _(act):
            def body(t, p):
                i, b = t - 4, p
                if live(i, NB):
                    wait(act, hT_p, i + 1)
                    wait(act, y_p, i - 1)
                    nc.scalar.copy(hqT[:, b], hT_b[:, 0:FB]).then_inc(hT_s, 1)
                i, b = t - 1, (p - 1) % 2
                if live(i, NB):
                    wait(act, xT_p, i + 1)
                    wait(act, gu_p, (i - 1) * 2)
                    nc.scalar.copy(xqT[:, b], xT_b[:, 0:S]).then_inc(xT_s, 1)
                i, b = t - 2, p
                if live(i, NB):
                    wait(act, gu_p, i * 2 + 1)
                    wait(act, dg_s, i + 1)
                    wait(act, h_s, i - 1)
                    nc.scalar.activation(gate[:, b], g_b[:], ACT.Silu, scale=dg[:, b, 0:1]).then_inc(g_s, 1)
                i, b = t - 3, (p - 3) % 2
                if live(i, NB):
                    wait(act, i1272_s, i + 1)
                    wait(act, hq_s, i - 1)
                    nc.scalar.activation(hm[:, b], h[:, b], ACT.Identity, bias=K.magic[:], scale=inv1272[:, b]
                                         ).then_inc(hm_s, 1)
            steps(act, NB, LAG, HEAD, body)

        @block.tensor
        def _(pe):
            pe.wait_ge(wsum_s, 1)
            nc.tensor.matmul(w_b[:, 0:3], K.ones[:], wsum[:], start=True, stop=True).then_inc(wtot_p, 1)
            for n in range(3):
                pe.wait_ge(wr, n + 1)
                wait(pe, wT_s, n)
                for c in range(C):
                    last = nc.tensor.transpose(hT_b[:, 128 * c:128 * c + 128], wqb[:, n, 128 * c:128 * c + 128],
                                               K.identb[:])
                last.then_inc(wT_p, 1)
            pe.wait_ge(wT_s, 3)

            def body(t, p):
                i, b = t - 4, p
                if live(i, NB):
                    wait(pe, hq_s, i + 1)
                    wait(pe, hT_s, i)
                    for c in range(C):
                        last = nc.tensor.transpose(hT_b[:, 128 * c:128 * c + 128], hq[:, b, 128 * c:128 * c + 128],
                                                   K.identb[:])
                    last.then_inc(hT_p, 1)
                i, b = t - 2, p
                if live(i, NB):
                    wait(pe, xT_s, i + 1)
                    wait(pe, g_s, i)
                    nc.tensor.matmul(g_b[:], xqT[:, b], wT[:, 0], start=True, stop=True).then_inc(gu_p, 1)
                    wait(pe, h_s, i)
                    nc.tensor.matmul(u_b[:], xqT[:, b], wT[:, 1], start=True, stop=True).then_inc(gu_p, 1)
                i, b = t - 1, (p - 1) % 2
                if live(i, NB):
                    wait(pe, xq_s, i + 1)
                    wait(pe, xT_s, i)
                    nc.tensor.transpose(xT_b[:, 0:S], xq[:, b], K.identb[:]).then_inc(xT_p, 1)
                i, b = t - 4, p
                if live(i, NB):
                    wait(pe, hT_s, i + 1)
                    wait(pe, r_s, i)
                    for c in range(C):
                        last = nc.tensor.matmul(y_b[:, 0:D], hqT[:, b, 128 * c:128 * c + 128],
                                                wT[:, 2, 128 * c:128 * c + 128], start=(c == 0), stop=(c == C - 1))
                    last.then_inc(y_p, 1)
            steps(pe, NB, LAG, HEAD, body)


STAGES = ("self_attention", "context_mix", "experts", "recurrence", "cross_attention", "bit_ffn")


def decoder(nc, A, out, last="bit_ffn"):
    K = Shared()
    K.A = A
    with ExitStack() as ctx:
        K.bank = [ctx.enter_context(nc.psum_tensor(f"bank{i}", [128, 512], F32)) for i in range(8)]
        K.magic = ctx.enter_context(nc.sbuf_tensor("magic", [128, 1], F32))
        with ExitStack() as early:
            load_stage(nc, K, ctx, early)
            self_attention(nc, K)
            if last == "self_attention":
                return store(nc, K, out)
            with ExitStack() as moe:
                K.XT = [moe.enter_context(nc.sbuf_tensor(f"xT_all{n}", [D, NB * S], F32R)) for n in range(2)]
                K.wgp = [moe.enter_context(nc.sbuf_tensor(f"wg_part{n}", [D, FFP], F32R)) for n in range(2)]
                K.wup = [moe.enter_context(nc.sbuf_tensor(f"wu_part{n}", [D, FFP], F32R)) for n in range(2)]
                K.combT = moe.enter_context(nc.sbuf_tensor("combT", [3 * NE, NB * S], BF16))
                K.logits = moe.enter_context(nc.sbuf_tensor("logits", [S, NB, NE], F32))
                context_mix(nc, K)
                if last == "context_mix":
                    return store(nc, K, out)
                route(nc, K)
                experts(nc, K)
            if last == "experts":
                return store(nc, K, out)
            recurrence(nc, K)
            if last == "recurrence":
                return store(nc, K, out)
        cross_attention(nc, K)
        if last == "cross_attention":
            return store(nc, K, out)
        bit_ffn(nc, K, out)


def store(nc, K, out):
    with nc.semaphore("stored") as s, nc.Block() as block:
        @block.sync
        def _(sp):
            sp.dma_start(out.rearrange("b s d -> s b d"), K.X[:]).then_inc(s, 16)
            sp.wait_ge(s, 16)
            for q in (K.x0_in, K.x_in, K.route_in, K.ctx_in, K.consts_in, K.w0_in, K.wx_in, K.moe_in, K.w1_in, K.wx1_in, K.wb_in):
                sp.wait_ge(q, K.n_in[q.name])


def constants():
    p = np.arange(128)
    head_mask = ((p[:, None] % 64) // DH0 == np.arange(8)[None, :]).astype(np.float32)
    ones_mask = np.broadcast_to(np.arange(32)[None, :] // DH0 == np.arange(4)[:, None], (128, 4, 32)).astype(np.float32)
    e = np.arange(NE)
    tie = (e[None, :] < e[:, None]).astype(np.float32).reshape(-1)
    expert_of = (np.arange(NE * FE)[None, :] // FE == np.arange(3 * NE)[:, None] % NE).astype(np.float32)
    return {"c_ident": np.eye(128, dtype=np.float32), "c_head_mask": head_mask, "c_ones_mask": ones_mask,
            "c_tie": tie, "c_expert_of": expert_of}


def kernel(**inputs):
    import numpy as _np
    import concourse.bacc as _bacc
    from concourse import mybir as _mybir
    from concourse.bass_utils import run_bass_kernel_spmd as _run

    nc = _bacc.Bacc("TRN2", target_bir_lowering=False, num_devices=1)
    arrays, aps = {}, {}
    for name, value in {**inputs, **constants()}.items():
        a = _np.ascontiguousarray(value)
        if a.dtype == _np.bool_:
            a = a.view(_np.uint8)
        arrays[f"in_{name}"] = a
        aps[name] = nc.dram_tensor(f"in_{name}", a.shape, _mybir.dt.from_np(a.dtype), kind="ExternalInput").ap()
    out = nc.dram_tensor("out_dram", (NB, S, D), F32, kind="ExternalOutput").ap()
    decoder(nc, aps, out)
    r = _run(nc, [arrays], core_ids=[0])
    return r.results[0]["out_dram"]
```
